# Optimizing a Trainium2 kernel written in Bass

```python
import numpy as np
import jax
import jax.numpy as jnp

def _softmax(x, axis=-1):
    return jax.nn.softmax(x, axis=axis)

def _gelu(x):
    return jax.nn.gelu(x, approximate=True)

def _silu(x):
    return jax.nn.silu(x)

def _sigmoid(x):
    return jax.nn.sigmoid(x)

def _layernorm(x, axis=-1, eps=1e-05):
    m = jnp.mean(x, axis=axis, keepdims=True)
    v = jnp.var(x, axis=axis, keepdims=True)
    return (x - m) / jnp.sqrt(v + eps)

def _scatter_add(tgt, idx, src, axis=0):
    return tgt.at[idx].add(src)

def _segment_sum(src, seg, n):
    return jax.ops.segment_sum(src, seg, n)
kernel_name = 'mk_lm_tower_d4_tok_ids512_r4_29d956'

def setup_inputs(seed: int=0):
    np.random.seed(seed)
    _w = jnp.asarray

    def _rec_inputs():
        import jax
        import jax.numpy as jnp
        _rk = jax.random.key(seed)
        x = jax.random.randint(jax.random.fold_in(_rk, 1), (8, 512), 0, 64, jnp.int32)
        return x
    x = _rec_inputs()

    def _L0_tok_setup():
        import jax, jax.numpy as jnp
        import numpy as np
        NGRAM_SIZES = (2, 3, 4)
        HASH_VOCAB = 25000
        EMBED_DIM = 128
        BATCH, SEQ = (8, 1024)

        def _ngram_hash_ids(byte_sequence, n):
            L = byte_sequence.shape[1] - n + 1
            h = jnp.zeros((byte_sequence.shape[0], L), dtype=jnp.int64)
            for j in range(n):
                h = (h * 64 + byte_sequence[:, j:j + L]) % HASH_VOCAB
            return h

        def _ngram_embed(byte_sequence, table, n):
            B, S = byte_sequence.shape
            ids = _ngram_hash_ids(byte_sequence, n)
            emb = table[ids]
            out = jnp.zeros((B, S, table.shape[1]), dtype=table.dtype)
            c = n // 2
            return out.at[:, c:c + emb.shape[1]].set(emb)
        key = jax.random.key(seed)
        ks = jax.random.split(key, 6)
        return {'byte_sequence': jax.random.randint(ks[0], (BATCH, SEQ), 0, 64, dtype=jnp.int64), 'emb_2': jax.random.normal(ks[1], (HASH_VOCAB, EMBED_DIM), dtype=jnp.float32), 'emb_3': jax.random.normal(ks[2], (HASH_VOCAB, EMBED_DIM), dtype=jnp.float32), 'emb_4': jax.random.normal(ks[3], (HASH_VOCAB, EMBED_DIM), dtype=jnp.float32), 'proj_w': jax.random.normal(ks[4], (EMBED_DIM, len(NGRAM_SIZES) * EMBED_DIM), dtype=jnp.float32) * 0.02, 'proj_b': jax.random.normal(ks[5], (EMBED_DIM,), dtype=jnp.float32) * 0.02}
    _L0_tok_all = _L0_tok_setup()
    _L0_tok_in = {k: v for k, v in _L0_tok_all.items() if k in ('emb_2', 'emb_3', 'emb_4', 'proj_w', 'proj_b')}
    del _L0_tok_all

    def _L0_attn_setup():
        import jax, jax.numpy as jnp
        import numpy as np
        B, S, DIM, HID, K = (4, 2048, 128, 256, 4)
        MEM_LR, MEM_MOM = (0.01, 0.9)
        EPS = 1e-12

        def _proj2(x, w1, w2):
            return jax.nn.silu(x @ w1.T) @ w2.T

        def _causal_dwconv(x, w, b):
            xp = jnp.pad(x, ((0, 0), (K - 1, 0), (0, 0)))
            kern = jnp.transpose(w, (2, 1, 0))
            out = jax.lax.conv_general_dilated(xp, kern, (1,), 'VALID', dimension_numbers=('NWC', 'WIO', 'NWC'), feature_group_count=x.shape[-1])
            return out + b

        def _l2norm(x):
            n = jnp.linalg.norm(x, axis=-1, keepdims=True)
            return x / jnp.maximum(n, EPS)

        def _mem_fwd(h, ws):
            for i, w in enumerate(ws):
                h = h @ w.T
                if i < len(ws) - 1:
                    h = jax.nn.silu(h)
            return h

        def _reference_tuple_inner(x, w_k1, w_k2, w_v1, w_v2, w_q1, w_q2, conv_k_w, conv_k_b, conv_v_w, conv_v_b, conv_q_w, conv_q_b, gate_d_w, gate_d_b, gate_lr_w, gate_lr_b, gate_m_w, gate_m_b, w_out, mem_w1, mem_w2, mom1, mom2):
            keys = _proj2(x, w_k1, w_k2)
            values = _proj2(x, w_v1, w_v2)
            queries = _proj2(x, w_q1, w_q2)
            keys = _causal_dwconv(keys, conv_k_w, conv_k_b)
            values = _causal_dwconv(values, conv_v_w, conv_v_b)
            queries = _causal_dwconv(queries, conv_q_w, conv_q_b)
            keys = _l2norm(jax.nn.silu(keys))
            values = jax.nn.silu(values)
            queries = _l2norm(jax.nn.silu(queries))
            retrieved = _mem_fwd(queries, (mem_w1, mem_w2))
            x_mean = jnp.mean(x, axis=1, keepdims=True)
            alpha = jnp.mean(jax.nn.sigmoid(x_mean @ gate_d_w.T + gate_d_b))
            theta = jnp.mean(jax.nn.sigmoid(x_mean @ gate_lr_w.T + gate_lr_b)) * MEM_LR
            eta = jnp.mean(jax.nn.sigmoid(x_mean @ gate_m_w.T + gate_m_b)) * MEM_MOM

            def loss_fn(ws):
                pred = _mem_fwd(keys, ws)
                return jnp.mean((pred - values) ** 2)
            g1, g2 = jax.grad(loss_fn)((mem_w1, mem_w2))
            s1 = eta * mom1 - theta * g1
            s2 = eta * mom2 - theta * g2
            nw1 = (1.0 - alpha) * mem_w1 + s1
            nw2 = (1.0 - alpha) * mem_w2 + s2
            output = retrieved @ w_out.T
            return (output, nw1, nw2, s1, s2)
        if __name__ == '__main__':
            out = reference(**setup_inputs())
            print([o.shape for o in out])
        key = jax.random.key(seed)
        ks = jax.random.split(key, 16)
        n = lambda k, shp: jax.random.normal(k, shp, jnp.float32) * 0.02
        inp = {'x': jax.random.normal(ks[0], (B, S, DIM), jnp.float32), 'w_k1': n(ks[1], (DIM, DIM)), 'w_k2': n(ks[2], (DIM, DIM)), 'w_v1': n(ks[3], (DIM, DIM)), 'w_v2': n(ks[4], (DIM, DIM)), 'w_q1': n(ks[5], (DIM, DIM)), 'w_q2': n(ks[6], (DIM, DIM)), 'conv_k_w': n(ks[7], (DIM, 1, K)), 'conv_k_b': jnp.zeros((DIM,), jnp.float32), 'conv_v_w': n(ks[8], (DIM, 1, K)), 'conv_v_b': jnp.zeros((DIM,), jnp.float32), 'conv_q_w': n(ks[9], (DIM, 1, K)), 'conv_q_b': jnp.zeros((DIM,), jnp.float32), 'gate_d_w': n(ks[10], (DIM, DIM)), 'gate_d_b': jnp.zeros((DIM,), jnp.float32), 'gate_lr_w': n(ks[11], (DIM, DIM)), 'gate_lr_b': jnp.zeros((DIM,), jnp.float32), 'gate_m_w': n(ks[12], (DIM, DIM)), 'gate_m_b': jnp.zeros((DIM,), jnp.float32), 'w_out': n(ks[13], (DIM, DIM)), 'mem_w1': n(ks[14], (HID, DIM)), 'mem_w2': n(ks[15], (DIM, HID)), 'mom1': jnp.zeros((HID, DIM), jnp.float32), 'mom2': jnp.zeros((DIM, HID), jnp.float32)}
        return inp
    _L0_attn_all = _L0_attn_setup()
    _L0_attn_in = {k: v for k, v in _L0_attn_all.items() if k in ('w_k1', 'w_k2', 'w_v1', 'w_v2', 'w_q1', 'w_q2', 'conv_k_w', 'conv_k_b', 'conv_v_w', 'conv_v_b', 'conv_q_w', 'conv_q_b', 'gate_d_w', 'gate_d_b', 'gate_lr_w', 'gate_lr_b', 'gate_m_w', 'gate_m_b', 'w_out', 'mem_w1', 'mem_w2', 'mom1', 'mom2')}
    del _L0_attn_all

    def _L0_ffn_setup():
        import jax, jax.numpy as jnp
        import numpy as np
        B, S, D, O = (1, 512, 128, 128)
        H, QD, K, PK = (8, 64, 16, 64)
        N = PK * PK
        HALF = QD // 2

        def _l2norm(x):
            n = jnp.sqrt(jnp.sum(x * x, axis=-1, keepdims=True))
            return x / jnp.maximum(n, 1e-12)
        key = jax.random.key(seed)
        ks = jax.random.split(key, 9)
        return {'hidden_states': jax.random.normal(ks[0], (B, S, D), jnp.float32), 'Wq': jax.random.normal(ks[1], (H * QD, D), jnp.float32) * 0.02, 'bq': jnp.zeros((H * QD,), jnp.float32), 'ln_g': jnp.ones((QD,), jnp.float32), 'ln_b': jnp.zeros((QD,), jnp.float32), 'keys0': jax.random.normal(ks[2], (PK, HALF), jnp.float32) * 0.02, 'keys1': jax.random.normal(ks[3], (PK, HALF), jnp.float32) * 0.02, 'expert_down': jax.random.normal(ks[4], (N, D), jnp.float32) * 0.02, 'expert_up': jax.random.normal(ks[5], (N, O), jnp.float32) * 0.02}
    _L0_ffn_all = _L0_ffn_setup()
    _L0_ffn_in = {k: v for k, v in _L0_ffn_all.items() if k in ('Wq', 'bq', 'ln_g', 'ln_b', 'keys0', 'keys1', 'expert_down', 'expert_up')}
    del _L0_ffn_all

    def _L1_attn_setup():
        import jax, jax.numpy as jnp
        import numpy as np
        B, S, INP = (4, 512, 128)
        HIDDEN, NHEADS = (128, 8)
        DH = HIDDEN // NHEADS
        BASE = 10000.0

        def rope(x):
            b, s, h, d = x.shape
            d2 = d // 2
            theta = 1.0 / BASE ** (jnp.arange(0, d, 2, dtype=jnp.float32) / d)
            idx_theta = jnp.arange(s, dtype=jnp.float32)[:, None] * theta[None, :]
            idx_theta2 = jnp.concatenate([idx_theta, idx_theta], axis=1)
            neg_half = jnp.concatenate([-x[..., d2:], x[..., :d2]], axis=-1)
            cos = jnp.cos(idx_theta2)[None, :, None, :]
            sin = jnp.sin(idx_theta2)[None, :, None, :]
            return x * cos + neg_half * sin
        key = jax.random.key(seed)
        ks = jax.random.split(key, 9)
        sd = 1.0 / np.sqrt(INP)
        x = jax.random.normal(ks[0], (B, S, INP), dtype=jnp.float32)
        Wq = jax.random.uniform(ks[1], (INP, HIDDEN), jnp.float32, -sd, sd)
        bq = jax.random.uniform(ks[2], (HIDDEN,), jnp.float32, -sd, sd)
        Wk = jax.random.uniform(ks[3], (INP, HIDDEN), jnp.float32, -sd, sd)
        bk = jax.random.uniform(ks[4], (HIDDEN,), jnp.float32, -sd, sd)
        Wv = jax.random.uniform(ks[5], (INP, HIDDEN), jnp.float32, -sd, sd)
        bv = jax.random.uniform(ks[6], (HIDDEN,), jnp.float32, -sd, sd)
        Wo = jax.random.uniform(ks[7], (HIDDEN, INP), jnp.float32, -sd, sd)
        bo = jax.random.uniform(ks[8], (INP,), jnp.float32, -sd, sd)
        return {'x': x, 'Wq': Wq, 'bq': bq, 'Wk': Wk, 'bk': bk, 'Wv': Wv, 'bv': bv, 'Wo': Wo, 'bo': bo}
    _L1_attn_all = _L1_attn_setup()
    _L1_attn_in = {k: v for k, v in _L1_attn_all.items() if k in ('Wq', 'bq', 'Wk', 'bk', 'Wv', 'bv', 'Wo', 'bo')}
    del _L1_attn_all

    def _L1_ffn_setup():
        import jax, jax.numpy as jnp
        import numpy as np
        B, T, DIM = (2, 64, 128)
        E, H, K = (64, 256, 42)
        key = jax.random.key(seed)
        ks = jax.random.split(key, 7)
        s1 = 1.0 / np.sqrt(DIM).astype(np.float32)
        s2 = 1.0 / np.sqrt(H).astype(np.float32)
        return {'x': jax.random.normal(ks[0], (B, T, DIM), jnp.float32), 'w1': jax.random.uniform(ks[1], (E, DIM, H), jnp.float32, -s1, s1), 'b1': jax.random.uniform(ks[2], (E, H), jnp.float32, -s1, s1), 'w2': jax.random.uniform(ks[3], (E, H, DIM), jnp.float32, -s2, s2), 'b2': jax.random.uniform(ks[4], (E, DIM), jnp.float32, -s2, s2), 'router_w': jax.random.uniform(ks[5], (DIM, E), jnp.float32, -s1, s1), 'router_b': jax.random.uniform(ks[6], (E,), jnp.float32, -s1, s1)}
    _L1_ffn_all = _L1_ffn_setup()
    _L1_ffn_in = {k: v for k, v in _L1_ffn_all.items() if k in ('w1', 'b1', 'w2', 'b2', 'router_w', 'router_b')}
    del _L1_ffn_all

    def _L2_attn_setup():
        import jax, jax.numpy as jnp
        import numpy as np
        B, L, C = (2, 256, 128)
        H, P = (8, 4)
        D = C // H
        LN_EPS = 1e-05

        def _layernorm(x, g, b):
            mu = jnp.mean(x, axis=-1, keepdims=True)
            var = jnp.mean((x - mu) ** 2, axis=-1, keepdims=True)
            return (x - mu) * jax.lax.rsqrt(var + LN_EPS) * g + b
        key = jax.random.key(seed)
        ks = jax.random.split(key, 12)
        s = 0.02
        inp = {'features': jax.random.normal(ks[0], (B, L, C), jnp.float32), 'coords': jax.random.normal(ks[1], (B, L, 3), jnp.float32), 'ln_g': jnp.ones((C,), jnp.float32), 'ln_b': jnp.zeros((C,), jnp.float32), 'wq': jax.random.normal(ks[2], (C, C), jnp.float32) * s, 'bq': jnp.zeros((C,), jnp.float32), 'wk': jax.random.normal(ks[3], (C, C), jnp.float32) * s, 'bk': jnp.zeros((C,), jnp.float32), 'wv': jax.random.normal(ks[4], (C, C), jnp.float32) * s, 'bv': jnp.zeros((C,), jnp.float32), 'wqp': jax.random.normal(ks[5], (C, H * P * 3), jnp.float32) * s, 'bqp': jnp.zeros((H * P * 3,), jnp.float32), 'wkp': jax.random.normal(ks[6], (C, H * P * 3), jnp.float32) * s, 'bkp': jnp.zeros((H * P * 3,), jnp.float32), 'wvp': jax.random.normal(ks[7], (C, H * P * 3), jnp.float32) * s, 'bvp': jnp.zeros((H * P * 3,), jnp.float32), 'wo': jax.random.normal(ks[8], (C, C), jnp.float32) * s, 'bo': jnp.zeros((C,), jnp.float32), 'pscale': jnp.full((H,), 1.0 / np.sqrt(P), jnp.float32)}
        return inp
    _L2_attn_all = _L2_attn_setup()
    _L2_attn_in = {k: v for k, v in _L2_attn_all.items() if k in ('coords', 'ln_g', 'ln_b', 'wq', 'bq', 'wk', 'bk', 'wv', 'bv', 'wqp', 'bqp', 'wkp', 'bkp', 'wvp', 'bvp', 'wo', 'bo', 'pscale')}
    del _L2_attn_all

    def _L2_ffn_setup():
        import jax, jax.numpy as jnp
        import numpy as np
        E = 8
        K = 1
        D = 128
        I = 512
        B, T = (2, 512)
        key = jax.random.key(seed)
        ks = jax.random.split(key, 7)
        s = 0.02
        x = jax.random.normal(ks[0], (B, T, D), jnp.float32)
        gate_w = jax.random.normal(ks[1], (E, D), jnp.float32) * s
        w1 = jax.random.normal(ks[2], (E, I, D), jnp.float32) * s
        w2 = jax.random.normal(ks[3], (E, D, I), jnp.float32) * s
        w3 = jax.random.normal(ks[4], (E, I, D), jnp.float32) * s
        sw1 = jax.random.normal(ks[5], (I, D), jnp.float32) * s
        sw2 = jax.random.normal(ks[6], (D, I), jnp.float32) * s
        return {'x': x, 'gate_w': gate_w, 'w1': w1, 'w2': w2, 'w3': w3, 'sw1': sw1, 'sw2': sw2}
    _L2_ffn_all = _L2_ffn_setup()
    _L2_ffn_in = {k: v for k, v in _L2_ffn_all.items() if k in ('gate_w', 'w1', 'w2', 'w3', 'sw1', 'sw2')}
    del _L2_ffn_all

    def _L3_attn_setup():
        import jax, jax.numpy as jnp
        import numpy as np
        EMB = 128
        HEADS = 8
        HEAD_DIM = EMB // HEADS
        LN_EPS = 1e-05

        def _layernorm(v, gamma, beta):
            mu = jnp.mean(v, axis=-1, keepdims=True)
            var = jnp.var(v, axis=-1, keepdims=True)
            return (v - mu) * jax.lax.rsqrt(var + LN_EPS) * gamma + beta
        key = jax.random.key(seed)
        ks = jax.random.split(key, 7)
        b, t, e = (2, 768, EMB)
        x = jax.random.normal(ks[0], (b, t, e), dtype=jnp.float32)
        scale = 0.02
        Wq = jax.random.normal(ks[1], (e, e), dtype=jnp.float32) * scale
        Wk = jax.random.normal(ks[2], (e, e), dtype=jnp.float32) * scale
        Wv = jax.random.normal(ks[3], (e, e), dtype=jnp.float32) * scale
        Wo = jax.random.normal(ks[4], (e, e), dtype=jnp.float32) * scale
        bo = jnp.zeros((e,), dtype=jnp.float32)
        q_gamma = jnp.ones((HEAD_DIM,), dtype=jnp.float32)
        q_beta = jnp.zeros((HEAD_DIM,), dtype=jnp.float32)
        k_gamma = jnp.ones((HEAD_DIM,), dtype=jnp.float32)
        k_beta = jnp.zeros((HEAD_DIM,), dtype=jnp.float32)
        return {'x': x, 'Wq': Wq, 'Wk': Wk, 'Wv': Wv, 'Wo': Wo, 'bo': bo, 'q_gamma': q_gamma, 'q_beta': q_beta, 'k_gamma': k_gamma, 'k_beta': k_beta}
    _L3_attn_all = _L3_attn_setup()
    _L3_attn_in = {k: v for k, v in _L3_attn_all.items() if k in ('Wq', 'Wk', 'Wv', 'Wo', 'bo', 'q_gamma', 'q_beta', 'k_gamma', 'k_beta')}
    del _L3_attn_all

    def _L3_ffn_setup():
        import jax, jax.numpy as jnp
        import numpy as np
        NUM_EXPERTS = 8
        TOP_K = 2
        D_MODEL = 128
        D_FF = 512
        key = jax.random.key(seed)
        ks = jax.random.split(key, 6)
        sd = 1.0 / np.sqrt(D_MODEL)
        sf = 1.0 / np.sqrt(D_FF)
        x = jax.random.normal(ks[0], (8, 512, D_MODEL), dtype=jnp.float32)
        gate_w = jax.random.uniform(ks[1], (NUM_EXPERTS, D_MODEL), jnp.float32, -sd, sd)
        w1 = jax.random.uniform(ks[2], (NUM_EXPERTS, D_MODEL, D_FF), jnp.float32, -sd, sd)
        b1 = jax.random.uniform(ks[3], (NUM_EXPERTS, D_FF), jnp.float32, -sd, sd)
        w2 = jax.random.uniform(ks[4], (NUM_EXPERTS, D_FF, D_MODEL), jnp.float32, -sf, sf)
        b2 = jax.random.uniform(ks[5], (NUM_EXPERTS, D_MODEL), jnp.float32, -sf, sf)
        return {'x': x, 'gate_w': gate_w, 'w1': w1, 'b1': b1, 'w2': w2, 'b2': b2}
    _L3_ffn_all = _L3_ffn_setup()
    _L3_ffn_in = {k: v for k, v in _L3_ffn_all.items() if k in ('gate_w', 'w1', 'b1', 'w2', 'b2')}
    del _L3_ffn_all
    return {'x': x, 'L0_tok_emb_2': _L0_tok_in['emb_2'], 'L0_tok_emb_3': _L0_tok_in['emb_3'], 'L0_tok_emb_4': _L0_tok_in['emb_4'], 'L0_tok_proj_w': _L0_tok_in['proj_w'], 'L0_tok_proj_b': _L0_tok_in['proj_b'], 'L0_attn_w_k1': _L0_attn_in['w_k1'], 'L0_attn_w_k2': _L0_attn_in['w_k2'], 'L0_attn_w_v1': _L0_attn_in['w_v1'], 'L0_attn_w_v2': _L0_attn_in['w_v2'], 'L0_attn_w_q1': _L0_attn_in['w_q1'], 'L0_attn_w_q2': _L0_attn_in['w_q2'], 'L0_attn_conv_k_w': _L0_attn_in['conv_k_w'], 'L0_attn_conv_k_b': _L0_attn_in['conv_k_b'], 'L0_attn_conv_v_w': _L0_attn_in['conv_v_w'], 'L0_attn_conv_v_b': _L0_attn_in['conv_v_b'], 'L0_attn_conv_q_w': _L0_attn_in['conv_q_w'], 'L0_attn_conv_q_b': _L0_attn_in['conv_q_b'], 'L0_attn_gate_d_w': _L0_attn_in['gate_d_w'], 'L0_attn_gate_d_b': _L0_attn_in['gate_d_b'], 'L0_attn_gate_lr_w': _L0_attn_in['gate_lr_w'], 'L0_attn_gate_lr_b': _L0_attn_in['gate_lr_b'], 'L0_attn_gate_m_w': _L0_attn_in['gate_m_w'], 'L0_attn_gate_m_b': _L0_attn_in['gate_m_b'], 'L0_attn_w_out': _L0_attn_in['w_out'], 'L0_attn_mem_w1': _L0_attn_in['mem_w1'], 'L0_attn_mem_w2': _L0_attn_in['mem_w2'], 'L0_attn_mom1': _L0_attn_in['mom1'], 'L0_attn_mom2': _L0_attn_in['mom2'], 'L0_ffn_Wq': _L0_ffn_in['Wq'], 'L0_ffn_bq': _L0_ffn_in['bq'], 'L0_ffn_ln_g': _L0_ffn_in['ln_g'], 'L0_ffn_ln_b': _L0_ffn_in['ln_b'], 'L0_ffn_keys0': _L0_ffn_in['keys0'], 'L0_ffn_keys1': _L0_ffn_in['keys1'], 'L0_ffn_expert_down': _L0_ffn_in['expert_down'], 'L0_ffn_expert_up': _L0_ffn_in['expert_up'], 'L1_attn_Wq': _L1_attn_in['Wq'], 'L1_attn_bq': _L1_attn_in['bq'], 'L1_attn_Wk': _L1_attn_in['Wk'], 'L1_attn_bk': _L1_attn_in['bk'], 'L1_attn_Wv': _L1_attn_in['Wv'], 'L1_attn_bv': _L1_attn_in['bv'], 'L1_attn_Wo': _L1_attn_in['Wo'], 'L1_attn_bo': _L1_attn_in['bo'], 'L1_ffn_w1': _L1_ffn_in['w1'], 'L1_ffn_b1': _L1_ffn_in['b1'], 'L1_ffn_w2': _L1_ffn_in['w2'], 'L1_ffn_b2': _L1_ffn_in['b2'], 'L1_ffn_router_w': _L1_ffn_in['router_w'], 'L1_ffn_router_b': _L1_ffn_in['router_b'], 'L2_attn_coords': _L2_attn_in['coords'], 'L2_attn_ln_g': _L2_attn_in['ln_g'], 'L2_attn_ln_b': _L2_attn_in['ln_b'], 'L2_attn_wq': _L2_attn_in['wq'], 'L2_attn_bq': _L2_attn_in['bq'], 'L2_attn_wk': _L2_attn_in['wk'], 'L2_attn_bk': _L2_attn_in['bk'], 'L2_attn_wv': _L2_attn_in['wv'], 'L2_attn_bv': _L2_attn_in['bv'], 'L2_attn_wqp': _L2_attn_in['wqp'], 'L2_attn_bqp': _L2_attn_in['bqp'], 'L2_attn_wkp': _L2_attn_in['wkp'], 'L2_attn_bkp': _L2_attn_in['bkp'], 'L2_attn_wvp': _L2_attn_in['wvp'], 'L2_attn_bvp': _L2_attn_in['bvp'], 'L2_attn_wo': _L2_attn_in['wo'], 'L2_attn_bo': _L2_attn_in['bo'], 'L2_attn_pscale': _L2_attn_in['pscale'], 'L2_ffn_gate_w': _L2_ffn_in['gate_w'], 'L2_ffn_w1': _L2_ffn_in['w1'], 'L2_ffn_w2': _L2_ffn_in['w2'], 'L2_ffn_w3': _L2_ffn_in['w3'], 'L2_ffn_sw1': _L2_ffn_in['sw1'], 'L2_ffn_sw2': _L2_ffn_in['sw2'], 'L3_attn_Wq': _L3_attn_in['Wq'], 'L3_attn_Wk': _L3_attn_in['Wk'], 'L3_attn_Wv': _L3_attn_in['Wv'], 'L3_attn_Wo': _L3_attn_in['Wo'], 'L3_attn_bo': _L3_attn_in['bo'], 'L3_attn_q_gamma': _L3_attn_in['q_gamma'], 'L3_attn_q_beta': _L3_attn_in['q_beta'], 'L3_attn_k_gamma': _L3_attn_in['k_gamma'], 'L3_attn_k_beta': _L3_attn_in['k_beta'], 'L3_ffn_gate_w': _L3_ffn_in['gate_w'], 'L3_ffn_w1': _L3_ffn_in['w1'], 'L3_ffn_b1': _L3_ffn_in['b1'], 'L3_ffn_w2': _L3_ffn_in['w2'], 'L3_ffn_b2': _L3_ffn_in['b2']}

def reference(x, L0_tok_emb_2, L0_tok_emb_3, L0_tok_emb_4, L0_tok_proj_w, L0_tok_proj_b, L0_attn_w_k1, L0_attn_w_k2, L0_attn_w_v1, L0_attn_w_v2, L0_attn_w_q1, L0_attn_w_q2, L0_attn_conv_k_w, L0_attn_conv_k_b, L0_attn_conv_v_w, L0_attn_conv_v_b, L0_attn_conv_q_w, L0_attn_conv_q_b, L0_attn_gate_d_w, L0_attn_gate_d_b, L0_attn_gate_lr_w, L0_attn_gate_lr_b, L0_attn_gate_m_w, L0_attn_gate_m_b, L0_attn_w_out, L0_attn_mem_w1, L0_attn_mem_w2, L0_attn_mom1, L0_attn_mom2, L0_ffn_Wq, L0_ffn_bq, L0_ffn_ln_g, L0_ffn_ln_b, L0_ffn_keys0, L0_ffn_keys1, L0_ffn_expert_down, L0_ffn_expert_up, L1_attn_Wq, L1_attn_bq, L1_attn_Wk, L1_attn_bk, L1_attn_Wv, L1_attn_bv, L1_attn_Wo, L1_attn_bo, L1_ffn_w1, L1_ffn_b1, L1_ffn_w2, L1_ffn_b2, L1_ffn_router_w, L1_ffn_router_b, L2_attn_coords, L2_attn_ln_g, L2_attn_ln_b, L2_attn_wq, L2_attn_bq, L2_attn_wk, L2_attn_bk, L2_attn_wv, L2_attn_bv, L2_attn_wqp, L2_attn_bqp, L2_attn_wkp, L2_attn_bkp, L2_attn_wvp, L2_attn_bvp, L2_attn_wo, L2_attn_bo, L2_attn_pscale, L2_ffn_gate_w, L2_ffn_w1, L2_ffn_w2, L2_ffn_w3, L2_ffn_sw1, L2_ffn_sw2, L3_attn_Wq, L3_attn_Wk, L3_attn_Wv, L3_attn_Wo, L3_attn_bo, L3_attn_q_gamma, L3_attn_q_beta, L3_attn_k_gamma, L3_attn_k_beta, L3_ffn_gate_w, L3_ffn_w1, L3_ffn_b1, L3_ffn_w2, L3_ffn_b2):
    import jax
    import jax.numpy as jnp

    def _L0_tok_ref(byte_sequence, emb_2, emb_3, emb_4, proj_w, proj_b):
        import jax, jax.numpy as jnp
        import numpy as np
        NGRAM_SIZES = (2, 3, 4)
        HASH_VOCAB = 25000
        EMBED_DIM = 128
        BATCH, SEQ = (8, 1024)

        def _ngram_hash_ids(byte_sequence, n):
            L = byte_sequence.shape[1] - n + 1
            h = jnp.zeros((byte_sequence.shape[0], L), dtype=jnp.int64)
            for j in range(n):
                h = (h * 64 + byte_sequence[:, j:j + L]) % HASH_VOCAB
            return h

        def _ngram_embed(byte_sequence, table, n):
            B, S = byte_sequence.shape
            ids = _ngram_hash_ids(byte_sequence, n)
            emb = table[ids]
            out = jnp.zeros((B, S, table.shape[1]), dtype=table.dtype)
            c = n // 2
            return out.at[:, c:c + emb.shape[1]].set(emb)
        tables = (emb_2, emb_3, emb_4)
        combined = jnp.concatenate([_ngram_embed(byte_sequence, t, n) for t, n in zip(tables, NGRAM_SIZES)], axis=-1)
        return jnp.einsum('bsk,dk->bsd', combined, proj_w) + proj_b

    def _L0_attn_ref(x, w_k1, w_k2, w_v1, w_v2, w_q1, w_q2, conv_k_w, conv_k_b, conv_v_w, conv_v_b, conv_q_w, conv_q_b, gate_d_w, gate_d_b, gate_lr_w, gate_lr_b, gate_m_w, gate_m_b, w_out, mem_w1, mem_w2, mom1, mom2):
        import jax, jax.numpy as jnp
        import numpy as np
        B, S, DIM, HID, K = (4, 2048, 128, 256, 4)
        MEM_LR, MEM_MOM = (0.01, 0.9)
        EPS = 1e-12

        def _proj2(x, w1, w2):
            return jax.nn.silu(x @ w1.T) @ w2.T

        def _causal_dwconv(x, w, b):
            xp = jnp.pad(x, ((0, 0), (K - 1, 0), (0, 0)))
            kern = jnp.transpose(w, (2, 1, 0))
            out = jax.lax.conv_general_dilated(xp, kern, (1,), 'VALID', dimension_numbers=('NWC', 'WIO', 'NWC'), feature_group_count=x.shape[-1])
            return out + b

        def _l2norm(x):
            n = jnp.linalg.norm(x, axis=-1, keepdims=True)
            return x / jnp.maximum(n, EPS)

        def _mem_fwd(h, ws):
            for i, w in enumerate(ws):
                h = h @ w.T
                if i < len(ws) - 1:
                    h = jax.nn.silu(h)
            return h

        def _reference_tuple_inner(x, w_k1, w_k2, w_v1, w_v2, w_q1, w_q2, conv_k_w, conv_k_b, conv_v_w, conv_v_b, conv_q_w, conv_q_b, gate_d_w, gate_d_b, gate_lr_w, gate_lr_b, gate_m_w, gate_m_b, w_out, mem_w1, mem_w2, mom1, mom2):
            keys = _proj2(x, w_k1, w_k2)
            values = _proj2(x, w_v1, w_v2)
            queries = _proj2(x, w_q1, w_q2)
            keys = _causal_dwconv(keys, conv_k_w, conv_k_b)
            values = _causal_dwconv(values, conv_v_w, conv_v_b)
            queries = _causal_dwconv(queries, conv_q_w, conv_q_b)
            keys = _l2norm(jax.nn.silu(keys))
            values = jax.nn.silu(values)
            queries = _l2norm(jax.nn.silu(queries))
            retrieved = _mem_fwd(queries, (mem_w1, mem_w2))
            x_mean = jnp.mean(x, axis=1, keepdims=True)
            alpha = jnp.mean(jax.nn.sigmoid(x_mean @ gate_d_w.T + gate_d_b))
            theta = jnp.mean(jax.nn.sigmoid(x_mean @ gate_lr_w.T + gate_lr_b)) * MEM_LR
            eta = jnp.mean(jax.nn.sigmoid(x_mean @ gate_m_w.T + gate_m_b)) * MEM_MOM

            def loss_fn(ws):
                pred = _mem_fwd(keys, ws)
                return jnp.mean((pred - values) ** 2)
            g1, g2 = jax.grad(loss_fn)((mem_w1, mem_w2))
            s1 = eta * mom1 - theta * g1
            s2 = eta * mom2 - theta * g2
            nw1 = (1.0 - alpha) * mem_w1 + s1
            nw2 = (1.0 - alpha) * mem_w2 + s2
            output = retrieved @ w_out.T
            return (output, nw1, nw2, s1, s2)
        if __name__ == '__main__':
            out = reference(**setup_inputs())
            print([o.shape for o in out])
        return _reference_tuple_inner(x, w_k1, w_k2, w_v1, w_v2, w_q1, w_q2, conv_k_w, conv_k_b, conv_v_w, conv_v_b, conv_q_w, conv_q_b, gate_d_w, gate_d_b, gate_lr_w, gate_lr_b, gate_m_w, gate_m_b, w_out, mem_w1, mem_w2, mom1, mom2)[0]

    def _L0_ffn_ref(hidden_states, Wq, bq, ln_g, ln_b, keys0, keys1, expert_down, expert_up):
        import jax, jax.numpy as jnp
        import numpy as np
        B, S, D, O = (1, 512, 128, 128)
        H, QD, K, PK = (8, 64, 16, 64)
        N = PK * PK
        HALF = QD // 2

        def _l2norm(x):
            n = jnp.sqrt(jnp.sum(x * x, axis=-1, keepdims=True))
            return x / jnp.maximum(n, 1e-12)
        b, s, d = hidden_states.shape
        q = (hidden_states @ Wq.T + bq).reshape(b, s, H, QD)
        mu = jnp.mean(q, axis=-1, keepdims=True)
        var = jnp.mean((q - mu) ** 2, axis=-1, keepdims=True)
        q = (q - mu) / jnp.sqrt(var + 1e-05) * ln_g + ln_b
        q0, q1 = (q[..., :HALF], q[..., HALF:])
        s0 = jnp.einsum('bshq,eq->bshe', _l2norm(q0), _l2norm(keys0))
        s1 = jnp.einsum('bshq,eq->bshe', _l2norm(q1), _l2norm(keys1))
        sc0, ix0 = jax.lax.top_k(s0, K)
        sc1, ix1 = jax.lax.top_k(s1, K)
        cs = (sc0[..., :, None] + sc1[..., None, :]).reshape(b, s, H, K * K)
        ci = (ix0[..., :, None] + ix1[..., None, :]).reshape(b, s, H, K * K)
        fs, pos = jax.lax.top_k(cs, K)
        fi = jnp.take_along_axis(ci, pos, axis=-1)
        w = jax.nn.softmax(fs, axis=-1)
        down = expert_down[fi]
        up = expert_up[fi]
        inner = jnp.einsum('bsd,bshkd->bshk', hidden_states, down)
        act = jax.nn.gelu(inner, approximate=False)
        out = jnp.einsum('bshk,bshko->bso', act * w, up)
        return out

    def _L1_attn_ref(x, Wq, bq, Wk, bk, Wv, bv, Wo, bo):
        import jax, jax.numpy as jnp
        import numpy as np
        B, S, INP = (4, 512, 128)
        HIDDEN, NHEADS = (128, 8)
        DH = HIDDEN // NHEADS
        BASE = 10000.0

        def rope(x):
            b, s, h, d = x.shape
            d2 = d // 2
            theta = 1.0 / BASE ** (jnp.arange(0, d, 2, dtype=jnp.float32) / d)
            idx_theta = jnp.arange(s, dtype=jnp.float32)[:, None] * theta[None, :]
            idx_theta2 = jnp.concatenate([idx_theta, idx_theta], axis=1)
            neg_half = jnp.concatenate([-x[..., d2:], x[..., :d2]], axis=-1)
            cos = jnp.cos(idx_theta2)[None, :, None, :]
            sin = jnp.sin(idx_theta2)[None, :, None, :]
            return x * cos + neg_half * sin
        b, s, _ = x.shape
        scale = DH ** (-0.5)
        q = (x @ Wq + bq).reshape(b, s, NHEADS, DH)
        k = (x @ Wk + bk).reshape(b, s, NHEADS, DH)
        v = (x @ Wv + bv).reshape(b, s, NHEADS, DH)
        q = rope(q)
        k = rope(k)
        att = jnp.einsum('bihd,bjhd->bhij', q, v)
        att = jax.nn.softmax(att * scale, axis=-1)
        h = jnp.einsum('bhij,bjhd->bihd', att, v)
        h = h.reshape(b, s, HIDDEN)
        return h @ Wo + bo + x

    def _L1_ffn_ref(x, w1, b1, w2, b2, router_w, router_b):
        import jax, jax.numpy as jnp
        import numpy as np
        B, T, DIM = (2, 64, 128)
        E, H, K = (64, 256, 42)
        Bb, Tt, C = x.shape
        N = Bb * Tt
        logits = x @ router_w + router_b
        probs = jax.nn.softmax(logits, axis=-1)
        top_w, top_idx = jax.lax.top_k(probs, K)
        top_w = jax.nn.softmax(top_w, axis=-1)
        xt = x.reshape(N, C)
        top_w = top_w.reshape(N, K)
        top_idx = top_idx.reshape(N, K)
        comb = jnp.zeros((N, E), x.dtype).at[jnp.arange(N)[:, None], top_idx].set(top_w)
        h = jax.nn.gelu(jnp.einsum('td,edh->teh', xt, w1) + b1, approximate=False)
        y = jnp.einsum('teh,ehd->ted', h, w2) + b2
        out = jnp.einsum('ted,te->td', y, comb)
        return out.reshape(Bb, Tt, C)

    def _L2_attn_ref(features, coords, ln_g, ln_b, wq, bq, wk, bk, wv, bv, wqp, bqp, wkp, bkp, wvp, bvp, wo, bo, pscale):
        import jax, jax.numpy as jnp
        import numpy as np
        B, L, C = (2, 256, 128)
        H, P = (8, 4)
        D = C // H
        LN_EPS = 1e-05

        def _layernorm(x, g, b):
            mu = jnp.mean(x, axis=-1, keepdims=True)
            var = jnp.mean((x - mu) ** 2, axis=-1, keepdims=True)
            return (x - mu) * jax.lax.rsqrt(var + LN_EPS) * g + b
        b, l, c = features.shape
        h = pscale.shape[0]
        d = c // h
        p = wqp.shape[1] // (h * 3)
        x = _layernorm(features, ln_g, ln_b)
        q_s = (x @ wq + bq).reshape(b, l, h, d).transpose(0, 2, 1, 3)
        k_s = (x @ wk + bk).reshape(b, l, h, d).transpose(0, 2, 1, 3)
        v_s = (x @ wv + bv).reshape(b, l, h, d).transpose(0, 2, 1, 3)
        q_p = (x @ wqp + bqp).reshape(b, l, h, p, 3).transpose(0, 2, 1, 3, 4)
        k_p = (x @ wkp + bkp).reshape(b, l, h, p, 3).transpose(0, 2, 1, 3, 4)
        logits_s = jnp.einsum('bhid,bhjd->bhij', q_s, k_s) * d ** (-0.5)
        dot = jnp.einsum('bhipk,bhjpk->bhij', q_p, k_p)
        qsq = jnp.sum(q_p * q_p, axis=(-1, -2))
        ksq = jnp.sum(k_p * k_p, axis=(-1, -2))
        pdist2 = qsq[..., :, None] + ksq[..., None, :] - 2.0 * dot
        logits = logits_s - pdist2 * pscale[None, :, None, None]
        attn = jax.nn.softmax(logits, axis=-1)
        out_s = jnp.einsum('bhij,bhjd->bhid', attn, v_s)
        out_s = out_s.transpose(0, 2, 1, 3).reshape(b, l, c)
        out = out_s @ wo + bo
        return out

    def _L2_ffn_ref(x, gate_w, w1, w2, w3, sw1, sw2):
        import jax, jax.numpy as jnp
        import numpy as np
        E = 8
        K = 1
        D = 128
        I = 512
        B, T = (2, 512)
        xf = x.reshape(-1, D)
        logits = xf @ gate_w.T
        wts, idx = jax.lax.top_k(logits, K)
        wts = jax.nn.softmax(wts, axis=-1)
        comb = jnp.einsum('nke,nk->ne', jax.nn.one_hot(idx, E, dtype=xf.dtype), wts)
        h = jax.nn.silu(jnp.einsum('nd,eid->nei', xf, w1)) * jnp.einsum('nd,eid->nei', xf, w3)
        y = jnp.einsum('nei,edi->nd', h * comb[:, :, None], w2)
        y = y + jax.nn.gelu(xf @ sw1.T, approximate=False) @ sw2.T
        return y.reshape(x.shape)

    def _L3_attn_ref(x, Wq, Wk, Wv, Wo, bo, q_gamma, q_beta, k_gamma, k_beta):
        import jax, jax.numpy as jnp
        import numpy as np
        EMB = 128
        HEADS = 8
        HEAD_DIM = EMB // HEADS
        LN_EPS = 1e-05

        def _layernorm(v, gamma, beta):
            mu = jnp.mean(v, axis=-1, keepdims=True)
            var = jnp.var(v, axis=-1, keepdims=True)
            return (v - mu) * jax.lax.rsqrt(var + LN_EPS) * gamma + beta
        b, t, e = x.shape
        h, s = (HEADS, HEAD_DIM)
        q = (x @ Wq.T).reshape(b, t, h, s)
        k = (x @ Wk.T).reshape(b, t, h, s)
        v = (x @ Wv.T).reshape(b, t, h, s)
        q = _layernorm(q, q_gamma, q_beta)
        k = _layernorm(k, k_gamma, k_beta)
        scale = 1.0 / jnp.sqrt(jnp.float32(s))
        scores = jnp.einsum('bqhs,bkhs->bhqk', q, k) * scale
        rows = jnp.arange(t)[:, None]
        cols = jnp.arange(t)[None, :]
        scores = jnp.where(cols > rows, -jnp.inf, scores)
        attn = jax.nn.softmax(scores, axis=-1)
        out = jnp.einsum('bhqk,bkhs->bqhs', attn, v).reshape(b, t, e)
        return out @ Wo.T + bo

    def _L3_ffn_ref(x, gate_w, w1, b1, w2, b2):
        import jax, jax.numpy as jnp
        import numpy as np
        NUM_EXPERTS = 8
        TOP_K = 2
        D_MODEL = 128
        D_FF = 512
        xs = x.reshape(-1, x.shape[-1])
        gate_logits = jnp.einsum('td,ed->te', xs, gate_w)
        top_vals, sel = jax.lax.top_k(gate_logits, TOP_K)
        weights = jax.nn.softmax(top_vals.astype(jnp.float32), axis=1)
        combine = jnp.sum(jax.nn.one_hot(sel, NUM_EXPERTS, dtype=weights.dtype) * weights[..., None], axis=1)
        out = jnp.zeros_like(xs)
        for e in range(NUM_EXPERTS):
            h = jax.nn.relu(xs @ w1[e] + b1[e])
            y = h @ w2[e] + b2[e]
            out = out + combine[:, e:e + 1] * y
        return out.reshape(x.shape)
    h = _L0_tok_ref(x, L0_tok_emb_2, L0_tok_emb_3, L0_tok_emb_4, L0_tok_proj_w, L0_tok_proj_b)
    h = h + _L0_attn_ref(_layernorm(h, axis=-1), L0_attn_w_k1, L0_attn_w_k2, L0_attn_w_v1, L0_attn_w_v2, L0_attn_w_q1, L0_attn_w_q2, L0_attn_conv_k_w, L0_attn_conv_k_b, L0_attn_conv_v_w, L0_attn_conv_v_b, L0_attn_conv_q_w, L0_attn_conv_q_b, L0_attn_gate_d_w, L0_attn_gate_d_b, L0_attn_gate_lr_w, L0_attn_gate_lr_b, L0_attn_gate_m_w, L0_attn_gate_m_b, L0_attn_w_out, L0_attn_mem_w1, L0_attn_mem_w2, L0_attn_mom1, L0_attn_mom2)
    h = h + _L0_ffn_ref(_layernorm(h, axis=-1), L0_ffn_Wq, L0_ffn_bq, L0_ffn_ln_g, L0_ffn_ln_b, L0_ffn_keys0, L0_ffn_keys1, L0_ffn_expert_down, L0_ffn_expert_up)
    h = h + _L1_attn_ref(_layernorm(h, axis=-1), L1_attn_Wq, L1_attn_bq, L1_attn_Wk, L1_attn_bk, L1_attn_Wv, L1_attn_bv, L1_attn_Wo, L1_attn_bo)
    h = h + _L1_ffn_ref(_layernorm(h, axis=-1), L1_ffn_w1, L1_ffn_b1, L1_ffn_w2, L1_ffn_b2, L1_ffn_router_w, L1_ffn_router_b)
    h = h + _L2_attn_ref(_layernorm(h, axis=-1), L2_attn_coords, L2_attn_ln_g, L2_attn_ln_b, L2_attn_wq, L2_attn_bq, L2_attn_wk, L2_attn_bk, L2_attn_wv, L2_attn_bv, L2_attn_wqp, L2_attn_bqp, L2_attn_wkp, L2_attn_bkp, L2_attn_wvp, L2_attn_bvp, L2_attn_wo, L2_attn_bo, L2_attn_pscale)
    h = h + _L2_ffn_ref(_layernorm(h, axis=-1), L2_ffn_gate_w, L2_ffn_w1, L2_ffn_w2, L2_ffn_w3, L2_ffn_sw1, L2_ffn_sw2)
    h = h + _L3_attn_ref(_layernorm(h, axis=-1), L3_attn_Wq, L3_attn_Wk, L3_attn_Wv, L3_attn_Wo, L3_attn_bo, L3_attn_q_gamma, L3_attn_q_beta, L3_attn_k_gamma, L3_attn_k_beta)
    h = h + _L3_ffn_ref(_layernorm(h, axis=-1), L3_ffn_gate_w, L3_ffn_w1, L3_ffn_b1, L3_ffn_w2, L3_ffn_b2)
    return h

_drawn_inputs = setup_inputs


def setup_inputs(seed=0):
    import zlib

    import numpy as np

    out = dict(_drawn_inputs(seed))
    spreads = {'L0_attn_conv_k_b': (0.0, 0.1),
     'L0_attn_conv_v_b': (0.0, 0.1),
     'L0_attn_conv_q_b': (0.0, 0.8),
     'L0_attn_gate_d_b': (0.0, 0.1),
     'L0_attn_gate_lr_b': (0.0, 0.1),
     'L0_attn_gate_m_b': (0.0, 0.1),
     'L0_attn_mom1': (0.0, 0.1),
     'L0_attn_mom2': (0.0, 0.1),
     'L0_ffn_bq': (0.0, 0.8),
     'L0_ffn_ln_g': (1.0, 0.6),
     'L0_ffn_ln_b': (0.0, 0.8),
     'L2_attn_ln_g': (1.0, 0.6),
     'L2_attn_ln_b': (0.0, 0.8),
     'L2_attn_bq': (0.0, 0.8),
     'L2_attn_bk': (0.0, 2.0),
     'L2_attn_bv': (0.0, 0.417),
     'L2_attn_bqp': (0.0, 0.8),
     'L2_attn_bkp': (0.0, 0.8),
     'L2_attn_bvp': (0.0, 0.1),
     'L2_attn_bo': (0.0, 0.1),
     'L2_attn_pscale': (0.5, 0.6),
     'L3_attn_bo': (0.0, 0.1),
     'L3_attn_q_gamma': (1.0, 0.6),
     'L3_attn_q_beta': (0.0, 0.8),
     'L3_attn_k_gamma': (1.0, 0.6),
     'L3_attn_k_beta': (0.0, 2.0)}
    factors = {'L0_attn_w_q1': 8.0,
     'L0_attn_w_q2': 8.0,
     'L0_attn_conv_q_w': 8.0,
     'L0_attn_w_out': 8.0,
     'L0_attn_mem_w1': 8.0,
     'L0_attn_mem_w2': 8.0,
     'L0_ffn_Wq': 8.0,
     'L0_ffn_keys0': 7.766,
     'L0_ffn_keys1': 7.52,
     'L0_ffn_expert_down': 5.596,
     'L0_ffn_expert_up': 5.602,
     'L1_attn_bq': 8.0,
     'L1_ffn_b1': 8.0,
     'L1_ffn_b2': 7.914,
     'L1_ffn_router_w': 3.378,
     'L1_ffn_router_b': 7.302,
     'L2_attn_wq': 8.0,
     'L2_attn_wk': 8.0,
     'L2_attn_wv': 7.842,
     'L2_attn_wqp': 8.0,
     'L2_attn_wkp': 8.0,
     'L2_attn_wo': 2.874,
     'L2_ffn_gate_w': 5.613,
     'L2_ffn_w1': 4.987,
     'L2_ffn_w2': 5.253,
     'L2_ffn_w3': 4.94,
     'L3_attn_Wq': 6.69,
     'L3_attn_Wk': 6.599,
     'L3_attn_Wv': 5.207,
     'L3_attn_Wo': 4.77,
     'L3_ffn_b1': 5.262,
     'L3_ffn_b2': 4.292,
     'L2_ffn_sw1': 2.887,
     'L2_ffn_sw2': 3.133}
    for name, (base, spread) in spreads.items():
        noise = np.random.default_rng([zlib.crc32(name.encode()), seed]).standard_normal(out[name].shape)
        drawn = base * np.exp(spread * noise) if base else spread * noise
        out[name] = jnp.asarray(drawn.astype(out[name].dtype))
    for name, factor in factors.items():
        out[name] = (out[name] * factor).astype(out[name].dtype)
    return out
```

```python
from contextlib import ExitStack

import concourse.bass as bass
from concourse import mybir

F32 = mybir.dt.float32
BF16 = mybir.dt.bfloat16
F16 = mybir.dt.float16
I32 = mybir.dt.int32
U32 = mybir.dt.uint32
ALU = mybir.AluOpType
ACT = mybir.ActivationFunctionType
AX = mybir.AxisListType

D = 128
NB, S = 8, 512
NT = NB * S
NTT = NT // 128
VOCAB = 25000
LN_EPS = 1e-5
BIG = 1e30


def wait(eng, sem, value):
    if isinstance(value, int) and value <= 0:
        return
    eng.wait_ge(sem, value)


def turns(eng, count, body, peel=1):
    for i in range(min(peel, count)):
        body(i)
    if count > peel:
        with eng.Fori(peel, count) as i:
            body(i)


def skewed(eng, count, first, second):
    first(0)
    first(1)
    second(0)
    with eng.Fori(2, count) as i:
        first(i)
        second(i - 1)
    second(count - 1)


def cols(i, n=S):
    return bass.ds(i * n, n)


class Tower:

    def __init__(self, nc, ctx, dram, where):
        self.nc, self.ctx, self.dram, self.where = nc, ctx, dram, where
        self.h = self.sb(ctx, "h", [128, NT])
        self.xn = self.sb(ctx, "xn", [128, NT])
        self.base = self.sb(ctx, "base", [128, where["base"]["_width"]])
        self.ident = self.at(self.base, "base", "ident")
        self.mean = self.at(self.base, "base", "mean")
        self.eps = self.at(self.base, "base", "eps")
        self.stage_sems = []
        self.ln_done = 0
        self.ln_sems = {n: ctx.enter_context(nc.semaphore("ln_" + n)) for n in
                        ("mean", "centred", "square", "var", "std", "rstd", "norm")}

    def sb(self, ctx, name, shape, dt=F32):
        return ctx.enter_context(self.nc.sbuf_tensor(name, shape, dt))

    def ps(self, ctx, name, shape, dt=F32):
        return ctx.enter_context(self.nc.psum_tensor(name, shape, dt))

    def sem(self, name):
        self.stage_sems.append(self.nc.alloc_semaphore(name))
        return self.stage_sems[-1]

    def end_stage(self):
        with self.nc.Block() as block:
            @block.gpsimd
            def _(pool):
                self.nc.clear_and_free_semaphores(self.stage_sems)
        self.stage_sems = []

    def at(self, tile, pack, name):
        lo, hi = self.where[pack][name]
        return tile[:, lo:hi]


def load_base(t):
    nc = t.nc
    loaded = t.sem("base_loaded")
    with nc.Block() as block:
        @block.sync
        def _(sp):
            sp.dma_start(t.base[:, :], t.dram["base"]).then_inc(loaded, 16)
            sp.wait_ge(loaded, 16)


def layernorm(t):
    nc, h, xn = t.nc, t.h, t.xn
    q = t.ln_sems
    done = t.ln_done
    t.ln_done += NB
    with ExitStack() as ctx:
        n = f"ln{done}_"
        centred = t.sb(ctx, n + "centred", [128, 2, S])
        square = t.sb(ctx, n + "square", [128, 2, S])
        std = t.sb(ctx, n + "std", [128, 2, S])
        rstd = t.sb(ctx, n + "rstd", [128, S])
        ps_mean = t.ps(ctx, n + "ps_mean", [128, 2, S])
        ps_var = t.ps(ctx, n + "ps_var", [128, 2, S])
        block = ctx.enter_context(nc.Block())

        @block.tensor
        def _(pe):
            def mean(i):
                if not (isinstance(i, int) and i < 2):
                    pe.wait_ge(q["centred"], done + i - 1)
                pe.matmul(ps_mean[:, i % 2, :], t.mean, h[:, cols(i)], start=True, stop=True)\
                  .then_inc(q["mean"], 1)

            def var(i):
                pe.wait_ge(q["square"], done + i + 1)
                if not (isinstance(i, int) and i < 2):
                    pe.wait_ge(q["std"], done + i - 1)
                pe.matmul(ps_var[:, i % 2, :], t.mean, square[:, i % 2, :], start=True, stop=True)\
                  .then_inc(q["var"], 1)
            skewed(pe, NB, mean, var)

        @block.vector
        def _(dve):
            def centre(i):
                dve.wait_ge(q["mean"], done + i + 1)
                if not (isinstance(i, int) and i < 2):
                    dve.wait_ge(q["square"], done + i - 1)
                    dve.wait_ge(q["norm"], done + i - 1)
                dve.tensor_tensor(centred[:, i % 2, :], h[:, cols(i)], ps_mean[:, i % 2, :], ALU.subtract)\
                   .then_inc(q["centred"], 1)

            def norm(i):
                dve.wait_ge(q["std"], done + i + 1)
                if not (isinstance(i, int) and i < 1):
                    dve.wait_ge(q["norm"], done + i)
                dve.reciprocal(rstd[:, :], std[:, i % 2, :]).then_inc(q["rstd"], 1)
                dve.wait_ge(q["rstd"], done + i + 1)
                dve.tensor_tensor(xn[:, cols(i)], centred[:, i % 2, :], rstd[:, :], ALU.mult)\
                   .then_inc(q["norm"], 1)
            skewed(dve, NB, centre, norm)

        @block.scalar
        def _(act):
            def squares(i):
                act.wait_ge(q["centred"], done + i + 1)
                if not (isinstance(i, int) and i < 2):
                    act.wait_ge(q["var"], done + i - 1)
                act.activation(square[:, i % 2, :], centred[:, i % 2, :], ACT.Square).then_inc(q["square"], 1)

            def root(i):
                act.wait_ge(q["var"], done + i + 1)
                if not (isinstance(i, int) and i < 2):
                    act.wait_ge(q["rstd"], done + i - 1)
                act.activation(std[:, i % 2, :], ps_var[:, i % 2, :], ACT.Sqrt, bias=t.eps[:, 0:1])\
                   .then_inc(q["std"], 1)
            skewed(act, NB, squares, root)


def write_out(t, out):
    nc, h = t.nc, t.h
    with ExitStack() as ctx:
        hb = t.sb(ctx, "wo_hb", [128, 2, S])
        rows = t.sb(ctx, "wo_rows", [128, 2, S])
        ps_t = t.ps(ctx, "wo_ps", [128, 2, S])
        copied, turned, evacuated = t.sem("wo_copied"), t.sem("wo_turned"), t.sem("wo_evacuated")
        stored = [t.sem("wo_stored0"), t.sem("wo_stored1")]
        block = ctx.enter_context(nc.Block())

        @block.gpsimd
        def _(pool):
            def body(j):
                for s in range(2):
                    wait(pool, turned, 2 * j + s - 1)
                    pool.tensor_copy(hb[:, s, :], h[:, bass.ds(j * 2 * S + s * S, S)]).then_inc(copied, 1)
            turns(pool, NB // 2, body)

        @block.tensor
        def _(pe):
            def body(j):
                for s in range(2):
                    pe.wait_ge(copied, 2 * j + s + 1)
                    wait(pe, evacuated, 2 * j + s - 1)
                    for c in range(4):
                        last = pe.transpose(ps_t[:, s, 128 * c:128 * c + 128], hb[:, s, 128 * c:128 * c + 128],
                                            t.ident)
                    last.then_inc(turned, 1)
            turns(pe, NB // 2, body)

        @block.vector
        def _(dve):
            def body(j):
                for s in range(2):
                    dve.wait_ge(turned, 2 * j + s + 1)
                    wait(dve, stored[s], 16 * j)
                    dve.tensor_copy(rows[:, s, :], ps_t[:, s, :]).then_inc(evacuated, 1)
            turns(dve, NB // 2, body)

        @block.sync
        def _(sp):
            def body(j):
                for s in range(2):
                    sp.wait_ge(evacuated, 2 * j + s + 1)
                    sp.dma_start(out[bass.ds(j * 2 + s, 1), :, :].rearrange("a (c p) d -> p (a c) d", p=128),
                                 rows[:, s, :].rearrange("p (c d) -> p c d", c=4)).then_inc(stored[s], 16)
            turns(sp, NB // 2, body)
            for s in range(2):
                sp.wait_ge(stored[s], 16 * (NB // 2))


def embed(t):
    nc, h = t.nc, t.h
    with ExitStack() as ctx:
        sb = lambda n, shape, dt=F32: t.sb(ctx, "tok_" + n, shape, dt)
        sem = lambda n: t.sem("tok_" + n)
        w = sb("w", [128, t.where["tok"]["_width"]])
        proj, proj_b = t.at(w, "tok", "proj"), t.at(w, "tok", "proj_b")
        xi, xf = sb("xi", [NB, S], I32), sb("xf", [NB, S])
        v, r, fix = sb("v", [NB, S]), sb("r", [NB, S]), sb("fix", [NB, S])
        quot = sb("quot", [NB, S], I32)
        ids = sb("ids", [NB, 3, S])
        idx = sb("idx", [128, 3, 4, NB], U32)
        rows = sb("rows", [128, 2, 3, 4, 128])
        emb = sb("emb", [128, 3, S])
        ps_i = t.ps(ctx, "tok_ps_i", [128, S])
        ps_t = t.ps(ctx, "tok_ps_t", [128, 3, S])
        ps_p = t.ps(ctx, "tok_ps_p", [128, 2, S])
        loaded, zeroed, x_in, chain = sem("loaded"), sem("zeroed"), sem("x_in"), sem("chain")
        ids_ready, ids_turned, idx_ready = sem("ids_ready"), sem("ids_turned"), sem("idx_ready")
        gathered = [sem("gathered0"), sem("gathered1")]
        turned, emb_ready, projected, h_ready = sem("turned"), sem("emb_ready"), sem("projected"), sem("h_ready")
        block = ctx.enter_context(nc.Block())

        @block.sync
        def _(sp):
            sp.dma_start(xi[:, :], t.dram["x"]).then_inc(x_in, 16)
            sp.dma_start(w[:, :], t.dram["tok"]).then_inc(loaded, 16)
            sp.wait_ge(loaded, 16)

        @block.vector
        def _(dve):
            steps = [0]

            def then(ins):
                steps[0] += 1
                ins.then_inc(chain, 1)
                dve.wait_ge(chain, steps[0])

            def modulo(n):
                then(dve.tensor_scalar(quot[:, 0:n], v[:, 0:n], 1.0 / VOCAB, None, ALU.mult))
                then(dve.scalar_tensor_tensor(r[:, 0:n], quot[:, 0:n], -float(VOCAB), v[:, 0:n], ALU.mult, ALU.add))
                then(dve.tensor_scalar(fix[:, 0:n], r[:, 0:n], 0.0, float(VOCAB), ALU.is_lt, ALU.mult))
                then(dve.tensor_tensor(r[:, 0:n], r[:, 0:n], fix[:, 0:n], ALU.add))
                then(dve.tensor_scalar(fix[:, 0:n], r[:, 0:n], float(VOCAB), -float(VOCAB), ALU.is_ge, ALU.mult))
                then(dve.tensor_tensor(r[:, 0:n], r[:, 0:n], fix[:, 0:n], ALU.add))

            dve.memset(ids[:, :, :], 0.0).then_inc(zeroed, 1)
            dve.wait_ge(x_in, 16)
            then(dve.tensor_copy(xf[:, :], xi[:, :]))
            then(dve.tensor_copy(v[:, :], xf[:, :]))
            modulo(S)
            dve.wait_ge(zeroed, 1)
            for n in range(2, 5):
                m, c = S - n + 1, n // 2
                then(dve.scalar_tensor_tensor(v[:, 0:m], r[:, 0:m], 64.0, xf[:, n - 1:n - 1 + m], ALU.mult, ALU.add))
                modulo(m)
                then(dve.tensor_copy(ids[:, n - 2, c:c + m], r[:, 0:m]))
            dve.sem_inc(ids_ready, 1)
            dve.wait_ge(ids_turned, 1)
            dve.tensor_copy(idx[:, :, :, :].rearrange("p a c b -> p (a c b)"), ps_i[:, 0:96]).then_inc(idx_ready, 1)

            def body(b):
                dve.wait_ge(turned, b + 1)
                wait(dve, projected, b)
                dve.tensor_copy(emb[:, 0, 1:S], ps_t[:, 0, 1:S]).then_inc(emb_ready, 1)
                dve.tensor_copy(emb[:, 1, 1:S - 1], ps_t[:, 1, 1:S - 1]).then_inc(emb_ready, 1)
                dve.tensor_copy(emb[:, 2, 2:S - 1], ps_t[:, 2, 2:S - 1]).then_inc(emb_ready, 1)
            dve.memset(emb[:, :, 0:2], 0.0).then_inc(zeroed, 1)
            dve.memset(emb[:, :, S - 1:S], 0.0).then_inc(zeroed, 1)
            dve.wait_ge(zeroed, 3)
            turns(dve, NB, body)

        @block.gpsimd
        def _(pool):
            pool.wait_ge(idx_ready, 1)
            for b in range(NB):
                wait(pool, turned, b - 1)
                for n in range(3):
                    for c in range(4):
                        pool.indirect_dma_start(
                            rows[:, b % 2, n, c, :], None, t.dram[f"emb{n + 2}"],
                            bass.IndirectOffsetOnAxis(ap=idx[:, n, c, b:b + 1], axis=0),
                            ).then_inc(gathered[b % 2], 16)

        @block.scalar
        def _(act):
            act.wait_ge(loaded, 16)

            def body(b):
                act.wait_ge(projected, b + 1)
                act.activation(h[:, cols(b)], ps_p[:, b % 2, :], ACT.Identity, bias=proj_b).then_inc(h_ready, 1)
            turns(act, NB, body)

        @block.tensor
        def _(pe):
            pe.wait_ge(ids_ready, 1)
            for n in range(3):
                for c in range(4):
                    at = 32 * n + 8 * c
                    last = pe.transpose(ps_i[:, at:at + 8], ids[:, n, 128 * c:128 * c + 128], t.ident[0:NB, 0:NB])
            last.then_inc(ids_turned, 1)
            pe.wait_ge(loaded, 16)

            def body(j):
                for s in range(2):
                    b = 2 * j + s
                    pe.wait_ge(gathered[s], 16 * 12 * (j + 1))
                    wait(pe, emb_ready, 3 * b)
                    for n in range(3):
                        for c in range(4):
                            last = pe.transpose(ps_t[:, n, 128 * c:128 * c + 128], rows[:, s, n, c, :], t.ident)
                    last.then_inc(turned, 1)
                    pe.wait_ge(emb_ready, 3 * b + 3)
                    wait(pe, h_ready, b - 1)
                    for n in range(3):
                        last = pe.matmul(ps_p[:, s, :], proj[:, 128 * n:128 * n + 128], emb[:, n, :],
                                         start=(n == 0), stop=(n == 2))
                    last.then_inc(projected, 1)
            turns(pe, NB // 2, body)


def memory_mixer(t):
    nc, h, xn = t.nc, t.h, t.xn
    with ExitStack() as ctx:
        sb = lambda n, shape, dt=F32: t.sb(ctx, "l0a_" + n, shape, dt)
        sem = lambda n: t.sem("l0a_" + n)
        w = sb("w", [128, t.where["l0a"]["_width"]])
        at = lambda n: t.at(w, "l0a", n)
        s1, qp, conv = sb("s1", [128, S]), sb("qp", [128, S + 3]), sb("conv", [128, S])
        s2, sq = sb("s2", [128, 2, S]), sb("sq", [128, 2, S])
        norm, rnorm, qn = sb("norm", [128, S]), sb("rnorm", [128, S]), sb("qn", [128, S])
        u, r = sb("u", [128, 2, S]), sb("r", [128, S])
        ps_1, ps_2 = t.ps(ctx, "l0a_ps1", [128, S]), t.ps(ctx, "l0a_ps2", [128, S])
        ps_n, ps_u = t.ps(ctx, "l0a_psn", [128, S]), t.ps(ctx, "l0a_psu", [128, 2, S])
        ps_r, ps_o = t.ps(ctx, "l0a_psr", [128, S]), t.ps(ctx, "l0a_pso", [128, S])
        loaded, zeroed = sem("loaded"), sem("zeroed")
        p1, s1_ready, p2, qp_ready, tapped = sem("p1"), sem("s1_ready"), sem("p2"), sem("qp_ready"), sem("tapped")
        s2_ready, sq_ready, summed, norm_ready = sem("s2_ready"), sem("sq_ready"), sem("summed"), sem("norm_ready")
        guarded, inverted, qn_ready = sem("guarded"), sem("inverted"), sem("qn_ready")
        up, u_ready, down, r_ready, outp, h_ready = [sem(n) for n in
                                                    ("up", "u_ready", "down", "r_ready", "outp", "h_ready")]
        block = ctx.enter_context(nc.Block())

        @block.sync
        def _(sp):
            sp.dma_start(w[:, :], t.dram["l0a"]).then_inc(loaded, 16)
            sp.wait_ge(loaded, 16)

        @block.tensor
        def _(pe):
            pe.wait_ge(loaded, 16)

            def first(b):
                wait(pe, s1_ready, b)
                pe.matmul(ps_1[:, :], at("q1"), xn[:, cols(b)], start=True, stop=True).then_inc(p1, 1)
                pe.wait_ge(s1_ready, b + 1)
                wait(pe, qp_ready, b)
                pe.matmul(ps_2[:, :], at("q2"), s1[:, :], start=True, stop=True).then_inc(p2, 1)

            def second(b):
                pe.wait_ge(sq_ready, b + 1)
                wait(pe, norm_ready, b)
                pe.matmul(ps_n[:, :], at("ones"), sq[:, b % 2, :], start=True, stop=True).then_inc(summed, 1)
                pe.wait_ge(qn_ready, b + 1)
                wait(pe, u_ready, b)
                for c in range(2):
                    last = pe.matmul(ps_u[:, c, :], at("m1")[:, 128 * c:128 * c + 128], qn[:, :], start=True, stop=True)
                last.then_inc(up, 1)
                pe.wait_ge(u_ready, b + 1)
                wait(pe, r_ready, b)
                for c in range(2):
                    last = pe.matmul(ps_r[:, :], at("m2")[:, 128 * c:128 * c + 128], u[:, c, :],
                                     start=(c == 0), stop=(c == 1))
                last.then_inc(down, 1)
                pe.wait_ge(r_ready, b + 1)
                wait(pe, h_ready, b)
                pe.matmul(ps_o[:, :], at("out"), r[:, :], start=True, stop=True).then_inc(outp, 1)
            skewed(pe, NB, first, second)

        @block.scalar
        def _(act):
            act.wait_ge(zeroed, 1)

            def first(b):
                act.wait_ge(p1, b + 1)
                wait(act, p2, b)
                act.activation(s1[:, :], ps_1[:, :], ACT.Silu).then_inc(s1_ready, 1)
                act.wait_ge(p2, b + 1)
                wait(act, tapped, 4 * b)
                act.activation(qp[:, 3:S + 3], ps_2[:, :], ACT.Copy).then_inc(qp_ready, 1)
                act.wait_ge(tapped, 4 * b + 4)
                if not (isinstance(b, int) and b < 2):
                    act.wait_ge(qn_ready, b - 1)
                    act.wait_ge(summed, b - 1)
                act.activation(s2[:, b % 2, :], conv[:, :], ACT.Silu).then_inc(s2_ready, 1)
                act.wait_ge(s2_ready, b + 1)
                act.activation(sq[:, b % 2, :], s2[:, b % 2, :], ACT.Square).then_inc(sq_ready, 1)

            def second(b):
                act.wait_ge(summed, b + 1)
                wait(act, qn_ready, b)
                act.activation(norm[:, :], ps_n[:, :], ACT.Sqrt).then_inc(norm_ready, 1)
                act.wait_ge(up, b + 1)
                wait(act, down, b)
                act.activation(u[:, :, :], ps_u[:, :, :], ACT.Silu).then_inc(u_ready, 1)
                act.wait_ge(down, b + 1)
                wait(act, outp, b)
                act.activation(r[:, :], ps_r[:, :], ACT.Copy).then_inc(r_ready, 1)
            skewed(act, NB, first, second)

        @block.vector
        def _(dve):
            dve.memset(qp[:, 0:3], 0.0).then_inc(zeroed, 1)
            dve.wait_ge(zeroed, 1)
            dve.wait_ge(loaded, 16)

            def first(b):
                dve.wait_ge(qp_ready, b + 1)
                wait(dve, s2_ready, b)
                dve.tensor_scalar(conv[:, :], qp[:, 0:S], at("conv_w")[:, 0:1], at("conv_b"), ALU.mult, ALU.add)\
                   .then_inc(tapped, 1)
                for j in range(1, 4):
                    dve.wait_ge(tapped, 4 * b + j)
                    dve.scalar_tensor_tensor(conv[:, :], qp[:, j:S + j], at("conv_w")[:, j:j + 1], conv[:, :],
                                             ALU.mult, ALU.add).then_inc(tapped, 1)

            def second(b):
                dve.wait_ge(norm_ready, b + 1)
                dve.tensor_scalar(norm[:, :], norm[:, :], 1e-12, None, ALU.max).then_inc(guarded, 1)
                dve.wait_ge(guarded, b + 1)
                wait(dve, qn_ready, b)
                dve.reciprocal(rnorm[:, :], norm[:, :]).then_inc(inverted, 1)
                dve.wait_ge(inverted, b + 1)
                dve.wait_ge(s2_ready, b + 1)
                wait(dve, up, b)
                dve.tensor_tensor(qn[:, :], s2[:, b % 2, :], rnorm[:, :], ALU.mult).then_inc(qn_ready, 1)
                dve.wait_ge(outp, b + 1)
                dve.tensor_tensor(h[:, cols(b)], h[:, cols(b)], ps_o[:, :], ALU.add).then_inc(h_ready, 1)
            skewed(dve, NB, first, second)


def attention(t, name, prepare, uses, causal=False, scale=0.25, plus_input=False):
    nc = t.nc
    G, U = 2, 8
    with ExitStack() as ctx:
        sb = lambda n, shape, dt=F32: t.sb(ctx, f"{name}_{n}", shape, dt)
        sem = lambda n: t.sem(f"{name}_{n}")
        w = sb("w", [128, t.where[name]["_width"]])
        at = lambda n: t.at(w, name, n)
        a = {"w": w, "at": at, "sb": sb, "sem": sem, "name": name}
        x = a["x"] = sb("x", [128, S])
        q = a["q"] = sb("q", [128, G, S])
        k = a["k"] = sb("k", [128, G, S])
        q2 = sb("q2", [128, G, S])
        v = sb("v", [128, 4, 8, 32])
        probs = sb("probs", [128, 2, 2, S])
        maxima = sb("maxima", [128, G, 4, 128])
        o = sb("o", [128, G, S])
        o_norm = sb("o_norm", [128, G, S])
        rden = sb("rden", [128, S])
        mask = sb("mask", [128, 2, 128]) if causal else None
        ps_s = t.ps(ctx, name + "_ps_s", [128, 2, 2, S])
        ps_m = t.ps(ctx, name + "_ps_m", [128, S])
        ps_o = t.ps(ctx, name + "_ps_o", [128, S])
        pj = a["pj"] = t.ps(ctx, name + "_pj", [128, 2, S])
        loaded, zeroed = sem("loaded"), sem("zeroed")
        x_ready = a["x_ready"] = sem("x_ready")
        q_ready, k_ready, v_ready = sem("q_ready"), sem("k_ready"), sem("v_ready")
        a["q_ready"], a["k_ready"] = q_ready, k_ready
        filled = a["filled"] = [sem("filled0"), sem("filled1")]
        emptied = a["emptied"] = [sem("emptied0"), sem("emptied1")]
        scored, maxed, turned, q2_ready = sem("scored"), sem("maxed"), sem("turned"), sem("q2_ready")
        exped, mixed, o_ready, inverted = sem("exped"), sem("mixed"), sem("o_ready"), sem("inverted")
        o_normed, h_ready, x_added = sem("o_normed"), sem("h_ready"), sem("x_added")
        N0, N1 = uses[0] + 2, uses[1] + 2
        a["N"] = (N0, N1)
        a["scored"], a["h_ready"] = scored, h_ready
        pre = prepare(t, a)
        wv, wo, den, bv, bo = at("v"), at("o"), at("den"), at("bv"), at("bo")
        block = ctx.enter_context(nc.Block())

        def span(tile, as_keys):
            if not causal:
                return 0, S
            return (128 * tile, S) if as_keys else (0, 128 * tile + 128)

        @block.sync
        def _(sp):
            sp.dma_start(w[:, :], t.dram[name]).then_inc(loaded, 16)
            if causal:
                sp.dma_start(mask[:, :, :], t.dram["causal"].rearrange("p (a c) -> p a c", a=2)).then_inc(loaded, 16)
            sp.wait_ge(loaded, 32 if causal else 16)

        @block.gpsimd
        def _(pool):
            pool.memset(maxima[:, :, :, :], 0.0).then_inc(zeroed, 1)
            pool.memset(v[:, :, :, 16:32], 0.0).then_inc(zeroed, 1)
            pool.wait_ge(zeroed, 2)
            pool.memset(v[:, :, :, 16:17], 1.0).then_inc(zeroed, 1)
            if "pool" in pre:
                turns(pool, NB, lambda b: pre["pool"](pool, b))

        @block.scalar
        def _(act):
            act.wait_ge(loaded, 32 if causal else 16)

            def body(b):
                pre["act"](act, b)
                for g in range(G):
                    for u in range(U):
                        lo, hi = span(u // 2, True)
                        act.wait_ge(scored, 32 * b + 16 * g + 8 + u + 1)
                        wait(act, mixed, 16 * b + 8 * g + u - 1)
                        act.activation(probs[:, u % 2, :, lo:hi], ps_s[:, u % 2, :, lo:hi], ACT.Exp, scale=scale)\
                           .then_inc(exped, 1)
            turns(act, NB, body)

        @block.vector
        def _(dve):
            dve.wait_ge(loaded, 32 if causal else 16)
            dve.wait_ge(zeroed, 3)

            def body(b):
                pre["dve"](dve, b)
                dve.wait_ge(filled[0], N0 * b + uses[0] + 1)
                wait(dve, mixed, 16 * b)
                dve.tensor_tensor(v[:, :, :, 0:16], pj[:, 0, :].rearrange("p (c h d) -> p c h d", c=4, d=16),
                                  bv.rearrange("p (a h d) -> p a h d", a=1, d=16).to_broadcast([128, 4, 8, 16]),
                                  ALU.add).then_inc(v_ready, 1)
                dve.wait_ge(v_ready, b + 1)
                dve.sem_inc(emptied[0], 1)
                for g in range(G):
                    wait(dve, turned, 2 * b + g - 1)
                    for u in range(U):
                        lo, hi = span(u // 2, False)
                        dve.wait_ge(scored, 32 * b + 16 * g + u + 1)
                        r = 64 * (u % 2) + 31
                        dve.tensor_reduce(maxima[:, g, u // 2, r:r + 33:32], ps_s[:, u % 2, :, lo:hi], AX.X, ALU.max)\
                           .then_inc(maxed, 1)
                    dve.wait_ge(turned, 2 * b + g + 1)
                    wait(dve, scored, 32 * b)
                    dve.scalar_tensor_tensor(q2[:, g, :], ps_m[:, :], -1.0, q[:, g, :], ALU.mult, ALU.add)\
                       .then_inc(q2_ready, 1)
                    dve.wait_ge(mixed, 16 * b + 8 * g + 8)
                    dve.tensor_copy(o[:, g, :], ps_o[:, :]).then_inc(o_ready, 1)
                for g in range(G):
                    dve.wait_ge(filled[1], N1 * b + uses[1] + g + 1)
                    wait(dve, o_normed, 2 * b + g)
                    dve.reciprocal(rden[:, :], pj[:, 1, :]).then_inc(emptied[1], 1)
                    dve.wait_ge(emptied[1], N1 * b + uses[1] + g + 1)
                    dve.wait_ge(o_ready, 2 * b + g + 1)
                    wait(dve, h_ready, b)
                    dve.tensor_tensor(o_norm[:, g, :], o[:, g, :], rden[:, :], ALU.mult).then_inc(o_normed, 1)
                hb = t.h[:, cols(b)]
                if plus_input:
                    dve.wait_ge(x_ready, b + 1)
                    dve.tensor_tensor(hb, hb, x[:, :], ALU.add).then_inc(x_added, 1)
                    dve.wait_ge(x_added, b + 1)
                dve.wait_ge(filled[0], N0 * b + uses[0] + 2)
                dve.scalar_tensor_tensor(hb, pj[:, 0, :], bo, hb, ALU.add, ALU.add).then_inc(h_ready, 1)
                dve.wait_ge(h_ready, b + 1)
                dve.sem_inc(emptied[0], 1)
            turns(dve, NB, body)

        @block.tensor
        def _(pe):
            pe.wait_ge(loaded, 32 if causal else 16)

            def body(b):
                pre["pe"](pe, b)
                wait(pe, emptied[0], N0 * b + uses[0])
                for c in range(4):
                    last = pe.matmul(pj[:, 0, 128 * c:128 * c + 128], x[:, 128 * c:128 * c + 128], wv,
                                     start=True, stop=True)
                last.then_inc(filled[0], 1)
                pe.wait_ge(q_ready, 2 * b + 2)
                pe.wait_ge(k_ready, 2 * b + 2)
                for g in range(G):
                    for u in range(U):
                        lo, hi = span(u // 2, False)
                        if u < 2:
                            wait(pe, exped, 16 * b + 8 * g + u - 1)
                        else:
                            pe.wait_ge(maxed, 16 * b + 8 * g + u - 1)
                        d = 128 * (u // 2)
                        for j in range(2):
                            r = 32 * (2 * (u % 2) + j)
                            last = pe.matmul(ps_s[:, u % 2, j, lo:hi], q[r:r + 32, g, d:d + 128],
                                             k[r:r + 32, g, lo:hi], start=True, stop=not causal)
                        if causal:
                            for j in range(2):
                                last = pe.matmul(ps_s[:, u % 2, j, d:d + 128], t.ident, mask[:, 0, :],
                                                 start=False, stop=True)
                        last.then_inc(scored, 1)
                    pe.wait_ge(maxed, 16 * b + 8 * g + 8)
                    wait(pe, q2_ready, 2 * b + g)
                    for c in range(4):
                        last = pe.transpose(ps_m[:, 128 * c:128 * c + 128], maxima[:, g, c, :], t.ident)
                    last.then_inc(turned, 1)
                    pe.wait_ge(q2_ready, 2 * b + g + 1)

                    def mix(u):
                        lo, hi = span(u // 2, True)
                        pe.wait_ge(exped, 16 * b + 8 * g + u + 1)
                        for j in range(2):
                            hd = 2 * (u % 2) + j
                            last = pe.matmul(ps_o[32 * hd:32 * hd + 32, lo:hi], v[:, u // 2, 4 * g + hd, :],
                                             probs[:, u % 2, j, lo:hi], start=(u < 2), stop=(u >= 6))
                        last.then_inc(mixed, 1)

                    for u in range(U):
                        lo, hi = span(u // 2, True)
                        if u >= 2:
                            pe.wait_ge(exped, 16 * b + 8 * g + u - 1)
                        d = 128 * (u // 2)
                        for j in range(2):
                            r = 32 * (2 * (u % 2) + j)
                            last = pe.matmul(ps_s[:, u % 2, j, lo:hi], k[r:r + 32, g, d:d + 128],
                                             q2[r:r + 32, g, lo:hi], start=True, stop=not causal)
                        if causal:
                            for j in range(2):
                                last = pe.matmul(ps_s[:, u % 2, j, d:d + 128], t.ident, mask[:, 1, :],
                                                 start=False, stop=True)
                        last.then_inc(scored, 1)
                        if u == 0:
                            pe.wait_ge(v_ready, b + 1)
                            wait(pe, o_ready, 2 * b + g)
                        else:
                            mix(u - 1)
                    mix(U - 1)
                for g in range(G):
                    pe.wait_ge(o_ready, 2 * b + g + 1)
                    wait(pe, emptied[1], N1 * b + uses[1] + g)
                    pe.matmul(pj[:, 1, :], den, o[:, g, :], start=True, stop=True).then_inc(filled[1], 1)
                pe.wait_ge(o_normed, 2 * b + 2)
                wait(pe, emptied[0], N0 * b + uses[0] + 1)
                for g in range(G):
                    last = pe.matmul(pj[:, 0, :], wo[:, 128 * g:128 * g + 128], o_norm[:, g, :],
                                     start=(g == 0), stop=(g == 1))
                last.then_inc(filled[0], 1)
            turns(pe, NB, body)


def project_heads(a, pe, b, uses_before=0, step=1):
    pj, x = a["pj"], a["x"]
    for g in range(2):
        for s, wn in ((0, "wq"), (1, "wk")):
            wait(pe, a["emptied"][s], a["N"][s] * b + g * step)
            pe.matmul(pj[:, s, :], a["at"](wn)[:, 128 * g:128 * g + 128], x[:, :], start=True, stop=True)\
              .then_inc(a["filled"][s], 1)


def l1_attention(t):
    def prepare(t, a):
        sb, at, pj, x, q, k = a["sb"], a["at"], a["pj"], a["x"], a["q"], a["k"]
        N0, N1 = a["N"]
        lin = sb("lin", [128, 2, S])
        qcos, qsin = sb("qcos", [128, 2, S]), sb("qsin", [128, 2, S])
        lin_ready, cos_ready = a["sem"]("lin_ready"), a["sem"]("cos_ready")
        filled, emptied = a["filled"], a["emptied"]

        def pool(e, b):
            wait(e, a["h_ready"], b)
            e.tensor_copy(x[:, :], t.xn[:, cols(b)]).then_inc(a["x_ready"], 1)

        def pe(e, b):
            e.wait_ge(a["x_ready"], b + 1)
            project_heads(a, e, b)
            for g in range(2):
                e.wait_ge(lin_ready, 2 * b + g + 1)
                e.wait_ge(emptied[g], a["N"][g] * b + 2)
                e.matmul(pj[:, g, :], at("rot"), lin[:, g, :], start=True, stop=True).then_inc(filled[g], 1)

        def act(e, b):
            for g in range(2):
                e.wait_ge(filled[0], N0 * b + g + 1)
                wait(e, cos_ready, 2 * b + g - 1)
                wait(e, a["q_ready"], 2 * b)
                e.activation(lin[:, g, :], pj[:, 0, :], ACT.Identity, bias=at("bq")[:, g:g + 1])\
                 .then_inc(lin_ready, 1)
                e.wait_ge(lin_ready, 2 * b + g + 1)
                e.sem_inc(emptied[0], 1)
                e.wait_ge(filled[1], N1 * b + g + 1)
                wait(e, a["scored"], 32 * b)
                e.activation(k[:, g, :], pj[:, 1, :], ACT.Identity, bias=at("bk")[:, g:g + 1])\
                 .then_inc(a["k_ready"], 1)
                e.wait_ge(a["k_ready"], 2 * b + g + 1)
                e.sem_inc(emptied[1], 1)

        def dve(e, b):
            for g in range(2):
                e.wait_ge(lin_ready, 2 * b + g + 1)
                e.tensor_tensor(qcos[:, g, :], lin[:, g, :], at("cos"), ALU.mult).then_inc(cos_ready, 1)
                e.wait_ge(filled[g], a["N"][g] * b + 3)
                e.tensor_tensor(qsin[:, g, :], pj[:, g, :], at("sin"), ALU.mult).then_inc(emptied[g], 1)
                e.wait_ge(emptied[g], a["N"][g] * b + 3)
                e.wait_ge(cos_ready, 2 * b + g + 1)
                wait(e, a["scored"], 32 * b)
                e.tensor_tensor(q[:, g, :], qcos[:, g, :], qsin[:, g, :], ALU.add).then_inc(a["q_ready"], 1)

        return {"pool": pool, "pe": pe, "act": act, "dve": dve}
    attention(t, "l1a", prepare, (3, 3), plus_input=True)


def l2_attention(t):
    def prepare(t, a):
        sb, at, pj, x, q, k = a["sb"], a["at"], a["pj"], a["x"], a["q"], a["k"]
        N0, N1 = a["N"]
        lin = [sb("q_lin", [128, 2, S]), sb("k_lin", [128, 2, S])]
        sq = [sb("q_sq", [128, 2, S]), sb("k_sq", [128, 2, S])]
        q_scaled = sb("q_scaled", [128, 2, S])
        q_scale, minus_ps = sb("q_scale", [128, 2]), sb("minus_ps", [128, 2])
        lin_ready = [a["sem"]("q_lin_ready"), a["sem"]("k_lin_ready")]
        sq_ready = [a["sem"]("q_sq_ready"), a["sem"]("k_sq_ready")]
        scaled, constants, x_scaled = a["sem"]("scaled"), a["sem"]("constants"), a["x_ready"]
        filled, emptied = a["filled"], a["emptied"]

        def pe(e, b):
            e.wait_ge(x_scaled, b + 1)
            project_heads(a, e, b)
            for g in range(2):
                for s, wn in ((0, "sum_q"), (1, "sum_k")):
                    e.wait_ge(sq_ready[s], 2 * b + g + 1)
                    e.wait_ge(emptied[s], a["N"][s] * b + 2 + g)
                    e.matmul(pj[:, s, :], at(wn), sq[s][:, g, :], start=True, stop=True).then_inc(filled[s], 1)

        def act(e, b):
            for g in range(2):
                for s, bn in ((0, "bq"), (1, "bk")):
                    e.wait_ge(filled[s], a["N"][s] * b + g + 1)
                    wait(e, a["q_ready" if s == 0 else "k_ready"], 2 * b)
                    wait(e, scaled, 2 * b)
                    e.activation(lin[s][:, g, :], pj[:, s, :], ACT.Identity, bias=at(bn)[:, g:g + 1])\
                     .then_inc(lin_ready[s], 1)
                    e.wait_ge(lin_ready[s], 2 * b + g + 1)
                    e.sem_inc(emptied[s], 1)
                    e.activation(sq[s][:, g, :], lin[s][:, g, :], ACT.Square).then_inc(sq_ready[s], 1)

        def dve(e, b):
            if isinstance(b, int) and b == 0:
                for g in range(2):
                    e.scalar_tensor_tensor(q_scale[:, g:g + 1], at("ps")[:, g:g + 1], at("two_on_points"), at("rest"),
                                           ALU.mult, ALU.add).then_inc(constants, 1)
                e.tensor_scalar(minus_ps[:, :], at("ps"), -1.0, None, ALU.mult).then_inc(constants, 1)
                e.wait_ge(constants, 3)
            wait(e, filled[0], N0 * b)
            e.tensor_scalar(x[:, :], t.xn[:, cols(b)], at("ln_g"), at("ln_b"), ALU.mult, ALU.add)\
             .then_inc(x_scaled, 1)
            for g in range(2):
                e.wait_ge(lin_ready[0], 2 * b + g + 1)
                wait(e, a["q_ready"], 2 * b)
                e.tensor_scalar(q_scaled[:, g, :], lin[0][:, g, :], q_scale[:, g:g + 1], None, ALU.mult)\
                 .then_inc(scaled, 1)
                e.wait_ge(scaled, 2 * b + g + 1)
                wait(e, a["scored"], 32 * b)
                for s, to, other, ready in ((0, q, q_scaled, "q_ready"), (1, k, lin[1], "k_ready")):
                    e.wait_ge(filled[s], a["N"][s] * b + 3 + g)
                    e.scalar_tensor_tensor(to[:, g, :], pj[:, s, :], minus_ps[:, g:g + 1], other[:, g, :],
                                           ALU.mult, ALU.add).then_inc(a[ready], 1)
                    e.wait_ge(a[ready], 2 * b + g + 1)
                    e.sem_inc(emptied[s], 1)

        return {"pe": pe, "act": act, "dve": dve}
    attention(t, "l2a", prepare, (4, 4), scale=1.0)


def l3_attention(t):
    def prepare(t, a):
        sb, at, pj, x, q, k = a["sb"], a["at"], a["pj"], a["x"], a["q"], a["k"]
        lin = [sb("q_lin", [128, S]), sb("k_lin", [128, S])]
        cen = [sb("q_cen", [128, S]), sb("k_cen", [128, S])]
        sq = [sb("q_sq", [128, S]), sb("k_sq", [128, S])]
        std = [sb("q_std", [128, S]), sb("k_std", [128, S])]
        rstd, unit = sb("rstd", [128, S]), sb("unit", [128, S])
        names = ("lin", "cen", "sq", "std")
        done = {n: [a["sem"](f"{p}_{n}_ready") for p in "qk"] for n in names}
        rstd_ready, unit_ready = a["sem"]("rstd_ready"), a["sem"]("unit_ready")
        filled, emptied = a["filled"], a["emptied"]
        final = (a["q_ready"], a["k_ready"])

        def pool(e, b):
            wait(e, filled[0], a["N"][0] * b)
            wait(e, filled[1], a["N"][1] * b)
            e.tensor_copy(x[:, :], t.xn[:, cols(b)]).then_inc(a["x_ready"], 1)

        def pe(e, b):
            e.wait_ge(a["x_ready"], b + 1)
            for g in range(2):
                for s, wn in ((0, "wq"), (1, "wk")):
                    wait(e, emptied[s], a["N"][s] * b + 3 * g)
                    e.matmul(pj[:, s, :], at(wn)[:, 128 * g:128 * g + 128], x[:, :], start=True, stop=True)\
                     .then_inc(filled[s], 1)
                for m, (mat, src, ready) in enumerate((("head_centre", lin, "lin"), ("head_mean", sq, "sq"))):
                    for s in range(2):
                        e.wait_ge(done[ready][s], 2 * b + g + 1)
                        e.wait_ge(emptied[s], a["N"][s] * b + 3 * g + 1 + m)
                        e.matmul(pj[:, s, :], at(mat), src[s][:, :], start=True, stop=True).then_inc(filled[s], 1)

        def act(e, b):
            for g in range(2):
                for s in range(2):
                    e.wait_ge(filled[s], a["N"][s] * b + 3 * g + 1)
                    e.activation(lin[s][:, :], pj[:, s, :], ACT.Copy).then_inc(done["lin"][s], 1)
                    e.wait_ge(done["lin"][s], 2 * b + g + 1)
                    e.sem_inc(emptied[s], 1)
                for s in range(2):
                    e.wait_ge(done["cen"][s], 2 * b + g + 1)
                    e.activation(sq[s][:, :], cen[s][:, :], ACT.Square).then_inc(done["sq"][s], 1)
                for s in range(2):
                    e.wait_ge(filled[s], a["N"][s] * b + 3 * g + 3)
                    wait(e, final[s], 2 * b + g)
                    e.activation(std[s][:, :], pj[:, s, :], ACT.Sqrt, bias=t.eps[:, 0:1]).then_inc(done["std"][s], 1)
                    e.wait_ge(done["std"][s], 2 * b + g + 1)
                    e.sem_inc(emptied[s], 1)

        def dve(e, b):
            for g in range(2):
                for s in range(2):
                    e.wait_ge(filled[s], a["N"][s] * b + 3 * g + 2)
                    e.tensor_copy(cen[s][:, :], pj[:, s, :]).then_inc(done["cen"][s], 1)
                    e.wait_ge(done["cen"][s], 2 * b + g + 1)
                    e.sem_inc(emptied[s], 1)
                for s, n in enumerate("qk"):
                    e.wait_ge(done["std"][s], 2 * b + g + 1)
                    wait(e, unit_ready, 4 * b + 2 * g + s)
                    e.reciprocal(rstd[:, :], std[s][:, :]).then_inc(rstd_ready, 1)
                    e.wait_ge(rstd_ready, 4 * b + 2 * g + s + 1)
                    if s or g or not (isinstance(b, int) and b == 0):
                        e.wait_ge(final[1 - s], 2 * b + g + s)
                    e.tensor_tensor(unit[:, :], cen[s][:, :], rstd[:, :], ALU.mult).then_inc(unit_ready, 1)
                    e.wait_ge(unit_ready, 4 * b + 2 * g + s + 1)
                    wait(e, a["scored"], 32 * b)
                    e.tensor_scalar((q, k)[s][:, g, :], unit[:, :], at(n + "_gamma")[:, g:g + 1],
                                    at(n + "_beta")[:, g:g + 1], ALU.mult, ALU.add).then_inc(final[s], 1)

        return {"pool": pool, "pe": pe, "act": act, "dve": dve}
    attention(t, "l3a", prepare, (6, 6), causal=True)


class Chain:

    def __init__(self, eng, sem, idle=None):
        self.eng, self.sem, self.idle, self.per, self.turn, self.k = eng, sem, idle, None, 0, 0

    def start(self, turn):
        if not (isinstance(turn, int) and turn == 0) and self.per is None:
            self.per = self.k
        self.turn, self.k = turn, 0

    def value(self):
        return self.k if self.per is None else self.turn * self.per + self.k

    def then(self, ins):
        self.k += 1
        ins.then_inc(self.sem, 1)
        self.eng.wait_ge(self.sem, self.value())

    def then_alone(self, ins):
        self.then(ins)
        self.eng.sem_inc(self.idle, 1)


def route(t, ctx, name, n_exp, top):
    nc = t.nc
    E, drop = n_exp, top < 0
    rounds = (-top + 7) // 8 if drop else 1
    pads = 8 * rounds - abs(top)
    weights = t.sb(ctx, name + "_weights", [128, NT])
    part12 = t.sb(ctx, name + "_part12", [128, NT], BF16)
    part3 = t.sb(ctx, name + "_part3", [128, NT], BF16)
    with ExitStack() as own:
        sb = lambda n, shape, dt=F32: t.sb(own, f"{name}r_{n}", shape, dt)
        sem = lambda n: t.sem(f"{name}r_{n}")
        wr, br = sb("wr", [128, E]), sb("br", [128, E])
        x = sb("x", [128, S])
        lg, ex, e2, mask = (sb(n, [128, 4, E]) for n in ("lg", "ex", "e2", "mask"))
        prob = sb("prob", [128, 4, E])
        key = sb("key", [128, 4, E + pads])
        top8 = sb("top8", [128, 8])
        mx, sm, rs = (sb(n, [128, 4]) for n in ("mx", "sm", "rs"))
        comb = sb("comb", [128, 4, 128])
        p1, r1 = sb("p1", [128, S], BF16), sb("r1", [128, S])
        p2 = sb("p2", [128, S], BF16)
        ps_l = t.ps(own, name + "r_psl", [128, 4, E])
        ps_t = t.ps(own, name + "r_pst", [128, S])
        loaded, zeroed, x_ready, scored, shifted, exped, shifted2, exped2, comb_ready, turned, parted, chain = [
            sem(n) for n in ("loaded", "zeroed", "x_ready", "scored", "shifted", "exped", "shifted2", "exped2",
                             "comb_ready", "turned", "parted", "chain")]
        block = own.enter_context(nc.Block())
        n_loads = 2 if drop else 1

        def wide(tile):
            return tile.rearrange("p (c a) -> p c a", a=1).to_broadcast([128, 4, E])

        @block.sync
        def _(sp):
            sp.dma_start(wr[:, :], t.dram[name + "_router"]).then_inc(loaded, 16)
            if drop:
                sp.dma_start(br[:, :], t.dram[name + "_router_b"]).then_inc(loaded, 16)
            sp.wait_ge(loaded, 16 * n_loads)

        @block.gpsimd
        def _(pool):
            pool.memset(comb[:, :, :], 0.0).then_inc(zeroed, 1)
            pool.memset(part3[:, :], 0.0).then_inc(zeroed, 1)

            def body(b):
                wait(pool, scored, b)
                pool.tensor_copy(x[:, :], t.xn[:, cols(b)]).then_inc(x_ready, 1)
            turns(pool, NB, body)

        @block.tensor
        def _(pe):
            pe.wait_ge(loaded, 16 * n_loads)

            def body(b):
                pe.wait_ge(x_ready, b + 1)
                wait(pe, shifted, b)
                for c in range(4):
                    last = pe.matmul(ps_l[:, c, :], x[:, 128 * c:128 * c + 128], wr[:, :], start=True, stop=True)
                last.then_inc(scored, 1)
                pe.wait_ge(comb_ready, b + 1)
                wait(pe, parted, b)
                for c in range(4):
                    last = pe.transpose(ps_t[:, 128 * c:128 * c + 128], comb[:, c, :], t.ident)
                last.then_inc(turned, 1)
            turns(pe, NB, body)

        @block.scalar
        def _(act):
            def body(b):
                act.wait_ge(shifted, b + 1)
                wait(act, comb_ready, b)
                act.activation(ex[:, :, :], lg[:, :, :], ACT.Exp).then_inc(exped, 1)
                if drop:
                    act.wait_ge(shifted2, b + 1)
                    act.activation(e2[:, :, :], prob[:, :, :], ACT.Exp).then_inc(exped2, 1)
            turns(act, NB, body)

        @block.vector
        def _(dve):
            dve.wait_ge(loaded, 16 * n_loads)
            dve.wait_ge(zeroed, 2)
            ch = Chain(dve, chain, t.sem(name + "r_idle"))

            def body(b):
                ch.start(b)
                then, then_alone = ch.then, ch.then_alone
                dve.wait_ge(scored, b + 1)
                if drop:
                    then(dve.tensor_tensor(lg[:, :, :], ps_l[:, :, :],
                                           br[:, :].rearrange("p (a e) -> p a e", a=1).to_broadcast([128, 4, E]), ALU.add))
                else:
                    then(dve.tensor_copy(lg[:, :, :], ps_l[:, :, :]))
                then(dve.tensor_reduce(mx[:, :], lg[:, :, :], AX.X, ALU.max))
                if not drop:
                    then(dve.tensor_copy(key[:, :, 0:E], lg[:, :, :]))
                then(dve.tensor_tensor(lg[:, :, :], lg[:, :, :], wide(mx[:, :]), ALU.subtract))
                dve.sem_inc(shifted, 1)
                if drop:
                    dve.wait_ge(exped, b + 1)
                    then(dve.tensor_reduce(sm[:, :], ex[:, :, :], AX.X, ALU.add))
                    then(dve.reciprocal(rs[:, :], sm[:, :]))
                    then(dve.tensor_tensor(prob[:, :, :], ex[:, :, :], wide(rs[:, :]), ALU.mult))
                    then(dve.tensor_scalar(key[:, :, 0:E], prob[:, :, :], -1.0, None, ALU.mult))
                    then(dve.tensor_tensor(prob[:, :, :], prob[:, :, :], wide(rs[:, :]), ALU.subtract))
                    dve.sem_inc(shifted2, 1)
                then_alone(dve.memset(key[:, :, E:E + pads], BIG))
                for c in range(4):
                    for _ in range(rounds):
                        then_alone(dve.max(top8[:, :], key[:, c, :]))
                        then_alone(dve.match_replace(key[:, c, :], top8[:, :], key[:, c, :], -BIG))
                then(dve.tensor_scalar(mask[:, :, :], key[:, :, 0:E], -0.5 * BIG, None, ALU.is_ge if drop else ALU.is_lt))
                dve.wait_ge(exped2 if drop else exped, b + 1)
                then(dve.tensor_tensor(mask[:, :, :], mask[:, :, :], (e2 if drop else ex)[:, :, :], ALU.mult))
                then(dve.tensor_reduce(sm[:, :], mask[:, :, :], AX.X, ALU.add))
                then(dve.reciprocal(rs[:, :], sm[:, :]))
                wait(dve, turned, b)
                then(dve.tensor_tensor(comb[:, :, 0:E], mask[:, :, :], wide(rs[:, :]), ALU.mult))
                then(dve.tensor_copy(comb[:, :, 64:64 + E], comb[:, :, 0:E]))
                dve.sem_inc(comb_ready, 1)
                dve.wait_ge(turned, b + 1)
                then(dve.tensor_copy(weights[:, cols(b)], ps_t[:, :]))
                then(dve.tensor_copy(p1[:, :], ps_t[:, :]))
                then(dve.tensor_tensor(r1[:, :], ps_t[:, :], p1[:, :], ALU.subtract))
                dve.sem_inc(parted, 1)
                then(dve.tensor_copy(p2[:, :], r1[:, :]))
                then(dve.tensor_tensor(part3[0:64, cols(b)], r1[0:64, :], p2[0:64, :], ALU.subtract))
                then(dve.tensor_copy(part12[0:64, cols(b)], p1[0:64, :]))
                then(dve.tensor_copy(part12[64:128, cols(b)], p2[64:128, :]))
            turns(dve, NB, body)
    return weights, part12, part3


def experts(t, name, n_exp, hidden, func, top, acc_tiles, biased=False, gated=False, shared=False):
    nc, h, xn = t.nc, t.h, t.xn
    nch = hidden // 128
    passes = NB // acc_tiles
    upe = acc_tiles * nch
    upp = 2 * upe
    with ExitStack() as ctx:
        weights, part12, part3 = route(t, ctx, name, n_exp, top)
        sb = lambda n, shape, dt=F32: t.sb(ctx, f"{name}_{n}", shape, dt)
        sem = lambda n: t.sem(f"{name}_{n}")
        w1 = sb("w1", [128, 2, hidden])
        w2 = sb("w2", [128, 2, hidden])
        w3 = sb("w3", [128, 2, hidden]) if gated else None
        b1 = sb("b1", [128, n_exp * nch]) if biased else None
        b2 = sb("b2", [n_exp, D]) if biased else None
        onehot = sb("onehot", [128, 64], BF16)
        acted = sb("acted", [128, 4, S])
        gate = sb("gate", [128, 2, S]) if gated else None
        prod = sb("prod", [128, 4, S])
        ps_acc = t.ps(ctx, name + "_acc", [128, acc_tiles, S])
        ps_h = t.ps(ctx, name + "_ps_h", [128, 2, S])
        ps_g = t.ps(ctx, name + "_ps_g", [128, 2, S]) if gated else None
        ps_b = t.ps(ctx, name + "_ps_b", [128, 2, S])
        loaded, cast, idle = sem("loaded"), sem("cast"), sem("idle")
        w_in = [sem("w_in0"), sem("w_in1")]
        hid, acted_ready, gate_ready, prod_ready = sem("hid"), sem("acted"), sem("gate"), sem("prod")
        spread, mixed, drained = sem("spread"), sem("mixed"), sem("drained")
        n_dma = 3 if gated else 2
        per_pass = n_exp * upe + (upe if shared else 0)
        spread_per_pass = n_exp * acc_tiles
        loads = [n_exp // 2 + (1 if shared else 0), n_exp // 2]
        block = ctx.enter_context(nc.Block())

        @block.sync
        def _(sp):
            if biased:
                sp.dma_start(b1[:, :], t.dram[name + "_b1"].rearrange("p e c -> p (e c)")).then_inc(loaded, 16)
                sp.dma_start(b2[:, :], t.dram[name + "_b2"]).then_inc(loaded, 16)

            def load(e, slot, used):
                wait(sp, mixed, used)
                e = bass.ds(e, 1)
                sp.dma_start(w1[:, slot, :], t.dram[name + "_w1"][e, :, :].rearrange("a p n -> p (a n)"))\
                  .then_inc(w_in[slot], 16)
                sp.dma_start(w2[:, slot, :], t.dram[name + "_w2"][e, :, :, :].rearrange("a p c n -> p (a c n)"))\
                  .then_inc(w_in[slot], 16)
                if gated:
                    sp.dma_start(w3[:, slot, :], t.dram[name + "_w3"][e, :, :].rearrange("a p n -> p (a n)"))\
                      .then_inc(w_in[slot], 16)

            for p in range(passes):
                def pair(j):
                    for s in range(2):
                        first = isinstance(j, int) and j == 0
                        if first:
                            used = per_pass * p - ((1 - s) * upe if not shared else s * 0)
                            if shared and s == 1:
                                used = per_pass * p - upe
                        else:
                            used = per_pass * p + upp * j - (1 - s) * upe
                        load(2 * j + s, s, used)
                turns(sp, n_exp // 2, pair)
                if shared:
                    sp.wait_ge(mixed, per_pass * p + n_exp * upe - upe)
                    sp.dma_start(w1[:, 0, :], t.dram[name + "_sw1"]).then_inc(w_in[0], 16)
                    sp.dma_start(w2[:, 0, :], t.dram[name + "_sw2"].rearrange("p c n -> p (c n)"))\
                      .then_inc(w_in[0], 16)

        w_per_pass = [16 * n_dma * (n_exp // 2) + (32 if shared else 0), 16 * n_dma * (n_exp // 2)]

        @block.gpsimd
        def _(pool):
            pool.tensor_copy(onehot[0:64, :], t.ident[0:64, 0:64]).then_inc(cast, 1)
            pool.tensor_copy(onehot[64:128, :], t.ident[64:128, 64:128]).then_inc(cast, 1)

        def units():
            return [(c, k) for c in range(acc_tiles) for k in range(nch)]

        @block.tensor
        def _(pe):
            pe.wait_ge(cast, 2)
            if biased:
                pe.wait_ge(loaded, 32)

            def mix(n, u, slot, first):
                c, k = units()[u % upe]
                pe.wait_ge(prod_ready, n + 1)
                pe.matmul(ps_acc[:, c, :], w2[:, slot, 128 * k:128 * k + 128], prod[:, u % 4, :],
                          start=(first and k == 0 and not biased), stop=False, skip_group_check=True)\
                  .then_inc(mixed, 1)

            def expert(p, n0, e, slot, spreads, in_loads, late, is_shared=False, before=None):
                pe.wait_ge(w_in[slot], in_loads)
                for u, (c, k) in enumerate(units()):
                    tile = acc_tiles * p + c
                    if k == 0 and not is_shared:
                        m = spreads + c
                        if not (isinstance(m, int) and m < 2):
                            pe.wait_ge(prod_ready, before(c - 2))
                        oh = onehot[:, bass.ds(e, 1)].to_broadcast([128, 128])
                        pe.matmul(ps_b[:, c % 2, :], oh, part12[:, S * tile:S * tile + S], start=True, stop=False)
                        pe.matmul(ps_b[:, c % 2, :], oh, part3[:, S * tile:S * tile + S], start=False, stop=True)\
                          .then_inc(spread, 1)
                    n = n0 + u
                    if not (isinstance(n, int) and n < 2):
                        pe.wait_ge(acted_ready, n - 1)
                        if gated:
                            pe.wait_ge(prod_ready, n - 1)
                    x = xn[:, S * tile:S * tile + S]
                    last = pe.matmul(ps_h[:, u % 2, :], w1[:, slot, 128 * k:128 * k + 128], x, start=True, stop=True)
                    if gated and not is_shared:
                        last = pe.matmul(ps_g[:, u % 2, :], w3[:, slot, 128 * k:128 * k + 128], x, start=True, stop=True)
                    last.then_inc(hid, 1)
                    if u < 2:
                        if late is not None:
                            mix(n - 2, upe - 2 + u, late[0], late[1])
                    else:
                        mix(n - 2, u - 2, slot, isinstance(e, int) and e == 0 and not is_shared)

            for p in range(passes):
                wait(pe, drained, acc_tiles * p)
                if biased:
                    for c in range(acc_tiles):
                        tile = acc_tiles * p + c
                        pe.matmul(ps_acc[:, c, :], b2[:, :], weights[0:n_exp, S * tile:S * tile + S],
                                  start=True, stop=False, skip_group_check=True)

                def pair(j):
                    for s in range(2):
                        n0 = per_pass * p + upp * j + upe * s
                        first = isinstance(j, int) and j == 0
                        if first and s == 0:
                            late = None
                        else:
                            late = (1 - s, first and s == 1)
                        m = spread_per_pass * p + acc_tiles * (2 * j + s)

                        def before(c, n0=n0, first=first, s=s):
                            if c < 0 and first and s == 0 and shared:
                                return n0 - upe + nch * (c + 1)
                            return n0 + nch * (c + 1)
                        expert(p, n0, 2 * j + s, s, m, w_per_pass[s] * p + 16 * n_dma * (j + 1), late, before=before)
                turns(pe, n_exp // 2, pair)
                n_end = per_pass * p + n_exp * upe
                if shared:
                    expert(p, n_end, 0, 0, 0, w_per_pass[0] * (p + 1), (1, False), is_shared=True)
                    n_end += upe
                for i in (2, 1):
                    mix(n_end - i, upe - i, 0 if shared else 1, False)

        @block.scalar
        def _(act):
            if biased:
                act.wait_ge(loaded, 32)

            def expert(n0, e, f):
                for u, (c, k) in enumerate(units()):
                    n = n0 + u
                    act.wait_ge(hid, n + 1)
                    if not (isinstance(n, int) and n < 4):
                        act.wait_ge(prod_ready, n - 3)
                    if biased:
                        act.sem_inc(idle, 1)
                    kw = {"bias": b1[:, bass.ds(e * nch + k, 1)]} if biased else {}
                    act.activation(acted[:, u % 4, :], ps_h[:, u % 2, :], f, **kw).then_inc(acted_ready, 1)
            for p in range(passes):
                def pair(j):
                    for s in range(2):
                        expert(per_pass * p + upp * j + upe * s, 2 * j + s, func)
                turns(act, n_exp // 2, pair)
                if shared:
                    expert(per_pass * p + n_exp * upe, 0, ACT.Gelu)

        @block.vector
        def _(dve):
            def expert(n0, m0, g0):
                for u, (c, k) in enumerate(units()):
                    n = n0 + u
                    dve.wait_ge(acted_ready, n + 1)
                    src = acted[:, u % 4, :]
                    if gated:
                        dve.wait_ge(hid, n + 1)
                        if not (isinstance(n, int) and n < 2):
                            dve.wait_ge(prod_ready, n - 1)
                        dve.tensor_tensor(gate[:, u % 2, :], acted[:, u % 4, :], ps_g[:, u % 2, :], ALU.mult)\
                           .then_inc(gate_ready, 1)
                        dve.wait_ge(gate_ready, g0 + u + 1)
                        src = gate[:, u % 2, :]
                    if k == 0:
                        dve.wait_ge(spread, m0 + c + 1)
                    if not (isinstance(n, int) and n < 4):
                        dve.wait_ge(mixed, n - 3)
                    dve.tensor_tensor(prod[:, u % 4, :], src, ps_b[:, c % 2, :], ALU.mult).then_inc(prod_ready, 1)
            for p in range(passes):
                def pair(j):
                    for s in range(2):
                        expert(per_pass * p + upp * j + upe * s, spread_per_pass * p + acc_tiles * (2 * j + s),
                               n_exp * upe * p + upp * j + upe * s)
                turns(dve, n_exp // 2, pair)
                if shared:
                    for u in range(upe):
                        n = per_pass * p + n_exp * upe + u
                        dve.wait_ge(acted_ready, n + 1)
                        dve.wait_ge(mixed, n - 3)
                        dve.tensor_copy(prod[:, u % 4, :], acted[:, u % 4, :]).then_inc(prod_ready, 1)
                dve.wait_ge(mixed, per_pass * (p + 1))
                for c in range(acc_tiles):
                    tile = acc_tiles * p + c
                    dve.tensor_tensor(h[:, S * tile:S * tile + S], h[:, S * tile:S * tile + S], ps_acc[:, c, :], ALU.add)\
                       .then_inc(drained, 1)


def l1_experts(t):
    experts(t, "l1f", 64, 256, ACT.Gelu, -22, 4, biased=True)


def l2_experts(t):
    experts(t, "l2f", 8, 512, ACT.Silu, 1, 2, gated=True, shared=True)


def l3_experts(t):
    experts(t, "l3f", 8, 512, ACT.Relu, 2, 4, biased=True)


TOP = 16
RECTS = ((0, 1, 16), (1, 1, 8), (2, 2, 5), (4, 4, 3), (8, 8, 1))
CAND = sum(ra * rb for _, ra, rb in RECTS)
HEADS, KEYS = 8, 64
CCH = 4
CP = HEADS * CAND // CCH
MAJ, MIN = 16, 8


def product_key_ffn(t):
    nc, h, xn = t.nc, t.h, t.xn
    NG = 128 // 8
    with ExitStack() as ctx:
        sb = lambda n, shape, dt=F32: t.sb(ctx, "l0f_" + n, shape, dt)
        sem = lambda n: t.sem("l0f_" + n)
        w = sb("w", [128, t.where["l0f"]["_width"]])
        at = lambda n: t.at(w, "l0f", n)
        wq = sb("wq", [128, 4, 128])
        bq = sb("bq", [128, 4])
        keys, keys_sq, keys_norm = sb("keys", [128, 256]), sb("keys_sq", [128, 256]), sb("keys_norm", [128, 256])
        iota = sb("iota", [CP, MAJ, 128], BF16)
        cen, sq, std, y1, y, sq2 = (sb(n, [128, 4, 128]) for n in ("cen", "sq", "std", "y1", "y", "sq2"))
        std_t, norm_t, rnorm_t = sb("std_t", [128, 8]), sb("norm_t", [128, 8, 2]), sb("rnorm_t", [128, 16])
        s, rep = sb("s", [128, 16, KEYS]), sb("rep", [128, 16, KEYS])
        v, vi = sb("v", [128, HEADS, 2, TOP]), sb("vi", [128, HEADS, 2, TOP], U32)
        cand, c2, c3 = (sb(n, [128, HEADS, CAND]) for n in ("cand", "c2", "c3"))
        ci, cm = sb("ci", [128, HEADS, CAND], U32), sb("cm", [128, 2, HEADS, CAND], U32)
        majmin = sb("majmin", [128, 2, HEADS * CAND], BF16)
        m1, m2 = sb("m1", [128, HEADS, 8]), sb("m2", [128, HEADS, 8])
        shifted, ex, wt = (sb(n, [128, HEADS, CAND]) for n in ("shifted", "ex", "wt"))
        zsum, rz = sb("zsum", [128, HEADS]), sb("rz", [128, HEADS])
        mm_t = sb("mm_t", [CP, 2, CCH, 128], BF16)
        p1, p2, p3 = (sb(n, [CP, CCH, 128], BF16) for n in ("p1", "p2", "p3"))
        r1 = sb("r1", [CP, CCH, 128])
        hot_maj = sb("hot_maj", [CP, CCH * NG, MAJ, 8], BF16)
        hot_min = sb("hot_min", [CP, CCH, MIN, 128], BF16)
        hw = [sb(f"hw{p}", [CP, CCH, MIN, 128], BF16) for p in range(3)]
        diag = sb("diag", [128, NG, MIN, 8])
        g, z = sb("g", [128, 128]), sb("z", [128, 128])
        ps_q = t.ps(ctx, "l0f_psq", [128, 4, 128])
        ps_s = t.ps(ctx, "l0f_pss", [128, 16, KEYS])
        ps_m = t.ps(ctx, "l0f_psm", [128, 4, 128])
        ps_w = t.ps(ctx, "l0f_psw", [CP, CCH, 128])
        ps_i = t.ps(ctx, "l0f_psi", [CP, 2, CCH, 128], BF16)
        ps_d = t.ps(ctx, "l0f_psd", [128, NG, MIN, 8])
        identb = sb("identb", [128, 128], BF16)
        names = ("loaded consts setup_mm setup_act ch_set q_mm cen sq var_mm std y1 y sq2 score_mm norm_act s_ready "
                 "vi_ready ci_ready cm_ready majmin shifted ex wt w_turned p1 r1 p2 p3 mm_t hot_min hw0 group_mm "
                 "diag a_mm g_mm g_act z out_mm h_ready idle ch_top ch_back hots k_sq k_std").split()
        q = {n: sem(n) for n in names}
        block = ctx.enter_context(nc.Block())

        def tok(T):
            return bass.ds(T * 128, 128)

        def later(T, k=0):
            return not (isinstance(T, int) and T <= k)

        @block.sync
        def _(sp):
            sp.dma_start(w[:, :], t.dram["l0f"]).then_inc(q["loaded"], 16)
            sp.wait_ge(q["loaded"], 16)

        @block.gpsimd
        def _(pool):
            pool.tensor_copy(identb[:, :], t.ident).then_inc(q["consts"], 1)
            pool.iota(iota[:, :, :], [[1, MAJ], [0, 128]], base=0, channel_multiplier=0,
                      allow_small_or_imprecise_dtypes=True).then_inc(q["consts"], 1)

            def front(T):
                pool.wait_ge(q["vi_ready"], T + 1)
                if later(T):
                    pool.wait_ge(q["cm_ready"], T)
                off = 0
                for a0, ra, rb in RECTS:
                    last = pool.tensor_tensor(
                        ci[:, :, off:off + ra * rb].rearrange("p h (a b) -> p h a b", b=rb),
                        vi[:, :, 0, a0:a0 + ra].rearrange("p h (a o) -> p h a o", o=1).to_broadcast([128, HEADS, ra, rb]),
                        vi[:, :, 1, 0:rb].rearrange("p h (o b) -> p h o b", o=1).to_broadcast([128, HEADS, ra, rb]), ALU.add)
                    off += ra * rb
                last.then_inc(q["ci_ready"], 1)

            def back(T):
                pool.wait_ge(q["p2"], T + 1)
                if later(T):
                    pool.wait_ge(q["hw0"], T)
                pool.tensor_tensor(p3[:, :, :], r1[:, :, :], p2[:, :, :], ALU.subtract).then_inc(q["p3"], 1)
                pool.wait_ge(q["p3"], T + 1)
                pool.wait_ge(q["hot_min"], T + 1)
                if later(T):
                    pool.wait_ge(q["group_mm"], T)
                for m in range(MIN):
                    last = pool.tensor_tensor(hw[2][:, :, m, :], hot_min[:, :, m, :], p3[:, :, :], ALU.mult)
                last.then_inc(q["hw0"], 1)
            front(0)
            front(1)
            back(0)
            with pool.Fori(2, NTT) as T:
                front(T)
                back(T - 1)
            back(NTT - 1)

        @block.tensor
        def _(pe):
            pe.wait_ge(q["loaded"], 16)
            for c in range(4):
                pe.matmul(ps_q[:, c, :], at("wq")[:, 128 * c:128 * c + 128], at("head_centre"), start=True, stop=True)
            pe.matmul(ps_m[:, 0, 0:4], at("head_centre"), at("bq"), start=True, stop=True).then_inc(q["setup_mm"], 1)
            pe.wait_ge(q["k_sq"], 1)
            pe.matmul(ps_s[:, 0:4, :], at("ones"), keys_sq[:, :], start=True, stop=True).then_inc(q["setup_mm"], 1)
            pe.wait_ge(q["ch_set"], 6)
            pe.wait_ge(q["consts"], 2)

            def front(T):
                if later(T):
                    pe.wait_ge(q["norm_act"], 2 * T)
                for c in range(4):
                    last = pe.matmul(ps_q[:, c, :], wq[:, c, :], xn[:, tok(T)], start=True, stop=True)
                last.then_inc(q["q_mm"], 1)
                pe.wait_ge(q["sq"], T + 1)
                pe.matmul(ps_q[:, :, :], at("head_mean"), sq[:, :, :], start=True, stop=True).then_inc(q["var_mm"], 1)
                pe.wait_ge(q["sq2"], T + 1)
                if later(T):
                    pe.wait_ge(q["s_ready"], T)
                for c in range(4):
                    pe.matmul(ps_q[:, 0, 16 + 2 * c:18 + 2 * c], sq[:, c, :], at("head_mean")[:, 0:128:64],
                              start=True, stop=True)
                    pe.matmul(ps_q[:, 0, 4 * c:4 * c + 4], sq2[:, c, :], at("quarter")[:, 0:128:32], start=True, stop=True)
                for c in range(4):
                    last = pe.matmul(ps_s[:, 4 * c:4 * c + 4, :], y[:, c, :], keys[:, :], start=True, stop=True)
                last.then_inc(q["score_mm"], 1)

            def turn(T):
                pe.wait_ge(q["wt"], T + 1)
                if later(T):
                    pe.wait_ge(q["r1"], T)
                    pe.wait_ge(q["mm_t"], T)
                wf = wt[:, :, :].rearrange("p h c -> p (h c)")
                for c in range(CCH):
                    pe.transpose(ps_w[:, c, :], wf[:, CP * c:CP * c + CP], t.ident)
                pe.wait_ge(q["majmin"], 2 * T + 2)
                for k in range(2):
                    for c in range(CCH):
                        last = pe.transpose(ps_i[:, k, c, :], majmin[:, k, CP * c:CP * c + CP], identb[:, :])
                last.then_inc(q["w_turned"], 1)

            def back(T):
                pe.wait_ge(q["hots"], T + 1)
                pe.wait_ge(q["hw0"], T + 1)
                if later(T):
                    pe.wait_ge(q["diag"], T)
                for k in range(NG):
                    n = 0
                    for c in range(CCH):
                        for p in range(3):
                            last = pe.matmul(ps_d[:, k, :, :], hot_maj[:, NG * c + k, :, :].rearrange("p m t -> p (m t)"),
                                             hw[p][:, c, :, 8 * k:8 * k + 8], start=(n == 0), stop=(n == 3 * CCH - 1))
                            n += 1
                last.then_inc(q["group_mm"], 1)
                if later(T):
                    pe.wait_ge(q["h_ready"], T)
                pe.matmul(ps_m[:, 2, :], at("down"), xn[:, tok(T)], start=True, stop=True).then_inc(q["g_mm"], 1)
                pe.wait_ge(q["diag"], T + 1)
                pe.wait_ge(q["g_act"], T + 1)
                for m in range(MIN):
                    last = pe.matmul(ps_m[:, 1, :], at("place")[:, 128 * m:128 * m + 128], diag[:, :, m, :],
                                     start=(m == 0), stop=(m == MIN - 1))
                last.then_inc(q["a_mm"], 1)
                pe.wait_ge(q["z"], T + 1)
                pe.matmul(ps_m[:, 3, :], at("up"), z[:, :], start=True, stop=True).then_inc(q["out_mm"], 1)

            front(0)
            front(1)
            turn(0)
            front(2)
            back(0)
            with pe.Fori(2, NTT - 1) as T:
                turn(T - 1)
                front(T + 1)
                back(T - 1)
            turn(NTT - 2)
            back(NTT - 2)
            turn(NTT - 1)
            back(NTT - 1)

        @block.scalar
        def _(act):
            act.wait_ge(q["loaded"], 16)
            act.activation(keys_sq[:, :], at("keys"), ACT.Square).then_inc(q["k_sq"], 1)
            act.wait_ge(q["setup_mm"], 2)
            act.activation(keys_norm[:, :], ps_s[:, 0:4, :].rearrange("p a b -> p (a b)"), ACT.Sqrt).then_inc(q["k_std"], 1)

            def front(T):
                act.wait_ge(q["cen"], T + 1)
                if later(T):
                    act.wait_ge(q["score_mm"], T)
                act.activation(sq[:, :, :], cen[:, :, :], ACT.Square).then_inc(q["sq"], 1)
                if later(T):
                    act.wait_ge(q["y"], T)
                act.activation(y1[:, :, :], cen[:, :, :], ACT.Copy, scale=at("ln_g")).then_inc(q["y1"], 1)
                act.wait_ge(q["var_mm"], T + 1)
                act.activation(std[:, :, :], ps_q[:, :, :], ACT.Sqrt, bias=t.eps[:, 0:1]).then_inc(q["std"], 1)
                act.wait_ge(q["y"], T + 1)
                act.activation(sq2[:, :, :], y[:, :, :], ACT.Square).then_inc(q["sq2"], 1)
                act.wait_ge(q["score_mm"], T + 1)
                if later(T):
                    act.wait_ge(q["s_ready"], T)
                act.activation(norm_t[:, :, :].rearrange("p h k -> p (h k)"), ps_q[:, 0, 0:16], ACT.Sqrt)\
                   .then_inc(q["norm_act"], 1)
                act.activation(std_t[:, :], ps_q[:, 0, 16:24], ACT.Sqrt, bias=t.eps[:, 0:1]).then_inc(q["norm_act"], 1)

            def middle(T):
                act.wait_ge(q["cm_ready"], T + 1)
                if later(T):
                    act.wait_ge(q["w_turned"], T)
                for k in range(2):
                    act.activation(majmin[:, k, :], cm[:, k, :, :].rearrange("p h c -> p (h c)"), ACT.Copy)\
                       .then_inc(q["majmin"], 1)
                act.wait_ge(q["shifted"], T + 1)
                if later(T):
                    act.wait_ge(q["wt"], T)
                act.activation(ex[:, :, :], shifted[:, :, :], ACT.Exp).then_inc(q["ex"], 1)

            def back(T):
                act.wait_ge(q["w_turned"], T + 1)
                if later(T):
                    act.wait_ge(q["hots"], T)
                    act.wait_ge(q["p3"], T)
                act.activation(p1[:, :, :], ps_w[:, :, :], ACT.Copy).then_inc(q["p1"], 1)
                act.activation(mm_t[:, :, :, :], ps_i[:, :, :, :], ACT.Copy).then_inc(q["mm_t"], 1)
                act.wait_ge(q["r1"], T + 1)
                act.activation(p2[:, :, :], r1[:, :, :], ACT.Copy).then_inc(q["p2"], 1)
                act.wait_ge(q["g_mm"], T + 1)
                if later(T):
                    act.wait_ge(q["z"], T)
                act.activation(g[:, :], ps_m[:, 2, :], ACT.Gelu).then_inc(q["g_act"], 1)
            front(0)
            front(1)
            middle(0)
            front(2)
            back(0)
            middle(1)
            with act.Fori(2, NTT - 1) as T:
                front(T + 1)
                back(T - 1)
                middle(T)
            back(NTT - 2)
            middle(NTT - 1)
            back(NTT - 1)

        @block.vector
        def _(dve):
            dve.wait_ge(q["loaded"], 16)
            dve.wait_ge(q["setup_mm"], 2)
            k = [0]

            def once(ins):
                k[0] += 1
                ins.then_inc(q["ch_set"], 1)
                dve.wait_ge(q["ch_set"], k[0])
            once(dve.tensor_copy(wq[:, :, :], ps_q[:, :, :]))
            once(dve.tensor_copy(bq[:, :], ps_m[:, 0, 0:4]))
            dve.wait_ge(q["k_std"], 1)
            once(dve.tensor_scalar(keys_norm[:, :], keys_norm[:, :], 1e-12, None, ALU.max))
            once(dve.reciprocal(keys_sq[:, :], keys_norm[:, :]))
            once(dve.tensor_tensor(keys[:, :], at("keys"), keys_sq[:, :], ALU.mult))
            once(dve.tensor_copy(z[:, 0:8], wq[:, 0, 0:8]))
            dve.wait_ge(q["consts"], 2)
            top, bk = Chain(dve, q["ch_top"], q["idle"]), Chain(dve, q["ch_back"], q["idle"])

            def centre(T):
                dve.wait_ge(q["q_mm"], T + 1)
                if later(T):
                    dve.wait_ge(q["y1"], T)
                dve.tensor_tensor(cen[:, :, :], ps_q[:, :, :],
                                  bq[:, :].rearrange("p (c o) -> p c o", o=1).to_broadcast([128, 4, 128]), ALU.add)\
                   .then_inc(q["cen"], 1)

            def scaled(T):
                dve.wait_ge(q["std"], T + 1)
                dve.wait_ge(q["y1"], T + 1)
                if later(T):
                    dve.wait_ge(q["score_mm"], T)
                dve.scalar_tensor_tensor(y[:, :, :], std[:, :, :], at("ln_b"), y1[:, :, :], ALU.mult, ALU.add)\
                   .then_inc(q["y"], 1)

            def middle(T, with_front=True, back=None):
                top.start(T)
                then, alone = top.then, top.then_alone
                if with_front:
                    centre(T + 1)
                dve.wait_ge(q["norm_act"], 2 * T + 2)
                then(dve.scalar_tensor_tensor(norm_t[:, :, :],
                                              std_t[:, :].rearrange("p (h o) -> p h o", o=1).to_broadcast([128, 8, 2]),
                                              1e-12, norm_t[:, :, :], ALU.mult, ALU.max))
                then(dve.reciprocal(rnorm_t[:, :], norm_t[:, :, :].rearrange("p h k -> p (h k)")))
                dve.wait_ge(q["score_mm"], T + 1)
                then(dve.tensor_tensor(s[:, :, :], ps_s[:, :, :],
                                       rnorm_t[:, :].rearrange("p (r o) -> p r o", o=1).to_broadcast([128, 16, KEYS]),
                                       ALU.mult))
                dve.sem_inc(q["s_ready"], 1)
                halves = [(r // 2, r % 2, r) for r in range(16)]
                for hd, k, r in halves:
                    last = dve.max(v[:, hd, k, 0:8], s[:, r, :])
                alone(last)
                for hd, k, r in halves:
                    last = dve.match_replace(rep[:, r, :], v[:, hd, k, 0:8], s[:, r, :], -BIG)
                alone(last)
                for hd, k, r in halves:
                    last = dve.max(v[:, hd, k, 8:16], rep[:, r, :])
                alone(last)
                if later(T):
                    dve.wait_ge(q["ci_ready"], T)
                    dve.sem_inc(q["idle"], 1)
                for hd, k, r in halves:
                    dve.max_index(vi[:, hd, k, 0:8], v[:, hd, k, 0:8], s[:, r, :])
                    last = dve.max_index(vi[:, hd, k, 8:16], v[:, hd, k, 8:16], rep[:, r, :])
                last.then_inc(q["vi_ready"], 1)
                if with_front:
                    scaled(T + 1)
                off = 0
                for a0, ra, rb in RECTS:
                    last = dve.tensor_tensor(
                        cand[:, :, off:off + ra * rb].rearrange("p h (a b) -> p h a b", b=rb),
                        v[:, :, 0, a0:a0 + ra].rearrange("p h (a o) -> p h a o", o=1).to_broadcast([128, HEADS, ra, rb]),
                        v[:, :, 1, 0:rb].rearrange("p h (o b) -> p h o b", o=1).to_broadcast([128, HEADS, ra, rb]), ALU.add)
                    off += ra * rb
                alone(last)
                for hd in range(HEADS):
                    last = dve.max(m1[:, hd, :], cand[:, hd, :])
                alone(last)
                for hd in range(HEADS):
                    last = dve.match_replace(c2[:, hd, :], m1[:, hd, :], cand[:, hd, :], -BIG)
                alone(last)
                for hd in range(HEADS):
                    last = dve.max(m2[:, hd, :], c2[:, hd, :])
                alone(last)
                for hd in range(HEADS):
                    last = dve.match_replace(c3[:, hd, :], m2[:, hd, :], c2[:, hd, :], -BIG)
                then(last)
                then(dve.tensor_tensor(shifted[:, :, :], cand[:, :, :],
                                       m1[:, :, 0:1].to_broadcast([128, HEADS, CAND]), ALU.subtract))
                dve.sem_inc(q["shifted"], 1)
                dve.wait_ge(q["ci_ready"], T + 1)
                if later(T):
                    dve.wait_ge(q["majmin"], 2 * T)
                dve.tensor_scalar(cm[:, 0, :, :], ci[:, :, :], 3, None, ALU.logical_shift_right)
                dve.tensor_scalar(cm[:, 1, :, :], ci[:, :, :], 7, None, ALU.bitwise_and).then_inc(q["cm_ready"], 1)
                if back is not None:
                    back(T - 1)
                dve.wait_ge(q["ex"], T + 1)
                then(dve.scalar_tensor_tensor(c2[:, :, :], c3[:, :, :], -0.5 * BIG, ex[:, :, :], ALU.is_lt, ALU.mult))
                then(dve.tensor_reduce(zsum[:, :], c2[:, :, :], AX.X, ALU.add))
                then(dve.reciprocal(rz[:, :], zsum[:, :]))
                if later(T):
                    dve.wait_ge(q["w_turned"], T)
                dve.tensor_tensor(wt[:, :, :], c2[:, :, :],
                                  rz[:, :].rearrange("p (h o) -> p h o", o=1).to_broadcast([128, HEADS, CAND]), ALU.mult)\
                   .then_inc(q["wt"], 1)

            def back(T):
                bk.start(T)
                then = bk.then
                dve.wait_ge(q["p1"], T + 1)
                if later(T):
                    dve.wait_ge(q["p3"], T)
                dve.tensor_tensor(r1[:, :, :], ps_w[:, :, :], p1[:, :, :], ALU.subtract).then_inc(q["r1"], 1)
                dve.wait_ge(q["mm_t"], T + 1)
                if later(T):
                    dve.wait_ge(q["group_mm"], T)
                    dve.wait_ge(q["hw0"], T)

                dve.tensor_tensor(
                    hot_min[:, :, :, :],
                    mm_t[:, 1, :, :].rearrange("p c (o t) -> p c o t", o=1).to_broadcast([CP, CCH, MIN, 128]),
                    iota[:, 0:MIN, :].rearrange("p (o m) t -> p o m t", o=1).to_broadcast([CP, CCH, MIN, 128]),
                    ALU.is_equal).then_inc(q["hot_min"], 1)
                dve.tensor_tensor(
                    hot_maj[:, :, :, :],
                    mm_t[:, 0, :, :].rearrange("p c (g o t) -> p (c g) o t", o=1, t=8).to_broadcast([CP, CCH * NG, MAJ, 8]),
                    iota[:, :, 0:8].rearrange("p (o m) t -> p o m t", o=1).to_broadcast([CP, CCH * NG, MAJ, 8]),
                    ALU.is_equal)
                dve.wait_ge(q["hot_min"], T + 1)
                dve.wait_ge(q["p2"], T + 1)
                for p, part in ((0, p1), (1, p2)):
                    last = dve.tensor_tensor(
                        hw[p][:, :, :, :], hot_min[:, :, :, :],
                        part[:, :, :].rearrange("p c (o t) -> p c o t", o=1).to_broadcast([CP, CCH, MIN, 128]), ALU.mult)
                last.then_inc(q["hots"], 1)
                dve.wait_ge(q["group_mm"], T + 1)
                if later(T):
                    dve.wait_ge(q["a_mm"], T)
                dve.tensor_tensor(diag[:, :, :, :].rearrange("p g m t -> p (g m) t"),
                                  ps_d[:, :, :, :].rearrange("p g m t -> p (g m) t"),
                                  at("own").rearrange("p (o t) -> p o t", o=1).to_broadcast([128, NG * MIN, 8]), ALU.mult)\
                   .then_inc(q["diag"], 1)
                dve.wait_ge(q["a_mm"], T + 1)
                dve.wait_ge(q["g_act"], T + 1)
                if later(T):
                    dve.wait_ge(q["out_mm"], T)
                dve.tensor_tensor(z[:, :], g[:, :], ps_m[:, 1, :], ALU.mult).then_inc(q["z"], 1)
                dve.wait_ge(q["out_mm"], T + 1)
                dve.tensor_tensor(h[:, tok(T)], h[:, tok(T)], ps_m[:, 3, :], ALU.add).then_inc(q["h_ready"], 1)
            centre(0)
            scaled(0)
            middle(0)
            middle(1, back=back)
            with dve.Fori(2, NTT - 1) as T:
                middle(T, back=back)
            middle(NTT - 1, with_front=False, back=back)
            back(NTT - 1)


STAGES = ("tok", "l0_attn", "l0_ffn", "l1_attn", "l1_ffn", "l2_attn", "l2_ffn", "l3_attn", "l3_ffn")


def build_tower(nc, dram, where, out, stages=STAGES, h_in=None):
    with ExitStack() as ctx:
        t = Tower(nc, ctx, dram, where)
        load_base(t)
        if h_in is not None:
            loaded = t.sem("h_loaded")
            with nc.Block() as block:
                @block.sync
                def _(sp):
                    sp.dma_start(t.h[:, :], h_in).then_inc(loaded, 16)
                    sp.wait_ge(loaded, 16)
        steps = {"tok": embed, "l0_attn": memory_mixer, "l0_ffn": product_key_ffn,
                 "l1_attn": l1_attention, "l1_ffn": l1_experts, "l2_attn": l2_attention,
                 "l2_ffn": l2_experts, "l3_attn": l3_attention, "l3_ffn": l3_experts}
        for name in stages:
            if name != "tok":
                layernorm(t)
            steps[name](t)
            t.end_stage()
        write_out(t, out)


class Pack:

    def __init__(self):
        self.parts, self.where, self.width = [], {}, 0

    def add(self, name, a):
        import numpy as np
        a = np.asarray(a)
        a = a.reshape(a.shape[0], -1)
        assert a.shape[0] == 128, (name, a.shape)
        self.where[name] = (self.width, self.width + a.shape[1])
        self.parts.append(a)
        self.width += a.shape[1]

    def array(self):
        import numpy as np
        self.where["_width"] = self.width
        return np.ascontiguousarray(np.concatenate(self.parts, axis=1))


def heads32(a, fill=None):
    import numpy as np
    out = np.zeros((*a.shape[:-1], 2, 4, 32), a.dtype)
    out[..., :16] = a.reshape(*a.shape[:-1], 2, 4, 16)
    for row, value in (fill or {}).items():
        out[..., row] = value
    return out


def head_columns(a, fill=None):
    import numpy as np
    return np.ascontiguousarray(heads32(a, fill).reshape(2, 128).T)


def lay_out(x):
    import numpy as np
    f = np.float32
    eye = np.eye(128, dtype=f)
    arrays, where = {}, {}

    base = Pack()
    base.add("ident", eye)
    base.add("mean", np.full((128, 128), 1.0 / D, f))
    base.add("eps", np.full((128, 1), LN_EPS, f))
    arrays["base"] = base.array()
    where["base"] = base.where

    p = Pack()
    p.add("proj", x["L0_tok_proj_w"].reshape(D, 3, D).transpose(2, 1, 0))
    p.add("proj_b", x["L0_tok_proj_b"].reshape(D, 1))
    arrays["tok"], where["tok"] = p.array(), p.where
    arrays["x"] = np.ascontiguousarray(x["x"])
    for n in (2, 3, 4):
        arrays[f"emb{n}"] = np.ascontiguousarray(x[f"L0_tok_emb_{n}"])

    p = Pack()
    p.add("q1", x["L0_attn_w_q1"].T)
    p.add("q2", x["L0_attn_w_q2"].T)
    p.add("m1", x["L0_attn_mem_w1"].T)
    p.add("m2", x["L0_attn_mem_w2"].T.reshape(2, 128, 128).transpose(1, 0, 2))
    p.add("out", x["L0_attn_w_out"].T)
    p.add("ones", np.ones((128, 128), f))
    p.add("conv_w", x["L0_attn_conv_q_w"].reshape(128, 4))
    p.add("conv_b", x["L0_attn_conv_q_b"].reshape(128, 1))
    arrays["l0a"], where["l0a"] = p.array(), p.where

    rows = np.arange(128)
    same = (rows[:, None] // 32) == (rows[None, :] // 32)
    r32 = rows % 32
    den = (same & (r32[:, None] == 16)).astype(f)

    def attention_pack(name, wv, bv, wo, bo):
        p = Pack()
        p.add("v", wv)
        p.add("o", heads32(np.ascontiguousarray(wo.T)).reshape(128, 2, 128).transpose(2, 1, 0))
        p.add("den", den)
        p.add("bv", np.broadcast_to(bv[None, :], (128, 128)))
        p.add("bo", bo.reshape(128, 1))
        return p

    p = attention_pack("l1a", x["L1_attn_Wv"], x["L1_attn_bv"], x["L1_attn_Wo"], x["L1_attn_bo"])
    p.add("wq", heads32(x["L1_attn_Wq"]))
    p.add("wk", heads32(x["L1_attn_Wv"]))
    p.add("bq", head_columns(x["L1_attn_bq"]))
    p.add("bk", head_columns(x["L1_attn_bv"], {31: 1.0}))
    rot = np.zeros((128, 128), f)
    for r in range(128):
        if r % 32 < 8:
            rot[r + 8, r] = -1.0
        elif r % 32 < 16:
            rot[r - 8, r] = 1.0
    p.add("rot", rot)
    theta = (1.0 / 10000.0 ** (np.arange(0, 16, 2, dtype=f) / f(16))).astype(f)
    angle = (np.arange(S, dtype=f)[:, None] * theta[None, :]).astype(f)
    angle = np.concatenate([angle, angle], axis=1).T
    for n, fn in (("cos", np.cos), ("sin", np.sin)):
        table = np.zeros((4, 32, S), f)
        table[:, :16] = fn(angle.astype(np.float64)).astype(f)
        p.add(n, table.reshape(128, S))
    arrays["l1a"], where["l1a"] = p.array(), p.where

    def with_points(a, ap, fill=None):
        out = np.zeros((*a.shape[:-1], 2, 4, 32), f)
        out[..., :16] = a.reshape(*a.shape[:-1], 2, 4, 16)
        out[..., 16:28] = ap.reshape(*a.shape[:-1], 2, 4, 12)
        for row, value in (fill or {}).items():
            out[..., row] = value
        return out

    p = attention_pack("l2a", x["L2_attn_wv"], x["L2_attn_bv"], x["L2_attn_wo"], x["L2_attn_bo"])
    p.add("wq", with_points(x["L2_attn_wq"], x["L2_attn_wqp"]))
    p.add("wk", with_points(x["L2_attn_wk"], x["L2_attn_wkp"]))
    p.add("bq", with_points(x["L2_attn_bq"], x["L2_attn_bqp"], {29: 1.0}).reshape(2, 128).T)
    p.add("bk", with_points(x["L2_attn_bk"], x["L2_attn_bkp"], {28: 1.0, 31: 1.0}).reshape(2, 128).T)
    p.add("ln_g", x["L2_attn_ln_g"].reshape(128, 1))
    p.add("ln_b", x["L2_attn_ln_b"].reshape(128, 1))
    p.add("ps", np.repeat(x["L2_attn_pscale"], 32).reshape(2, 128).T)
    points = (r32[:, None] >= 16) & (r32[:, None] < 28) & same
    p.add("sum_q", (points & (r32[None, :] == 28)).astype(f))
    p.add("sum_k", (points & (r32[None, :] == 29)).astype(f))
    p.add("two_on_points", np.where((r32 >= 16) & (r32 < 28), 2.0, 0.0).astype(f).reshape(128, 1))
    p.add("rest", np.where(r32 < 16, 0.25, np.where(r32 == 29, 1.0, 0.0)).astype(f).reshape(128, 1))
    arrays["l2a"], where["l2a"] = p.array(), p.where

    p = attention_pack("l3a", np.ascontiguousarray(x["L3_attn_Wv"].T), np.zeros(128, f),
                       np.ascontiguousarray(x["L3_attn_Wo"].T), x["L3_attn_bo"])
    p.add("wq", heads32(np.ascontiguousarray(x["L3_attn_Wq"].T)))
    p.add("wk", heads32(np.ascontiguousarray(x["L3_attn_Wk"].T)))
    real = same & (r32[:, None] < 16) & (r32[None, :] < 16)
    p.add("head_mean", real.astype(f) / f(16))
    p.add("head_centre", (eye * (r32 < 16)).astype(f) - real.astype(f) / f(16))
    for n in "qk":
        for what in ("gamma", "beta"):
            a = np.tile(x[f"L3_attn_{n}_{what}"], 8)
            p.add(f"{n}_{what}", head_columns(a, {31: 1.0} if (n, what) == ("k", "beta") else None))
    arrays["l3a"], where["l3a"] = p.array(), p.where
    ij = rows[:, None] - rows[None, :]
    arrays["causal"] = np.concatenate([np.where(ij < 0, -BIG, 0.0), np.where(ij > 0, -BIG, 0.0)],
                                      axis=1).astype(f)

    p = Pack()
    p.add("wq", x["L0_ffn_Wq"].reshape(4, 128, 128).transpose(1, 0, 2))
    p.add("bq", x["L0_ffn_bq"].reshape(4, 128).T)
    half = (rows[:, None] // 64) == (rows[None, :] // 64)
    quarter = (rows[:, None] // 32) == (rows[None, :] // 32)
    p.add("head_mean", half.astype(f) / f(64))
    p.add("head_centre", eye - half.astype(f) / f(64))
    p.add("quarter", quarter.astype(f))
    p.add("ln_g", np.tile(x["L0_ffn_ln_g"], 2).reshape(128, 1))
    p.add("ln_b", np.tile(x["L0_ffn_ln_b"], 2).reshape(128, 1))
    keys = np.zeros((2, 2, 32, 4, 64), f)
    for hh in range(2):
        keys[hh, 0, :, 2 * hh, :] = x["L0_ffn_keys0"].T
        keys[hh, 1, :, 2 * hh + 1, :] = x["L0_ffn_keys1"].T
    p.add("keys", keys.reshape(128, 256))
    p.add("down", x["L0_ffn_expert_down"][0:128].T)
    p.add("up", x["L0_ffn_expert_up"][0:128])
    p.add("ones", np.ones((128, 128), f))
    p.add("own", (r32[:, None] % 8 == np.arange(8)[None, :]).astype(f))
    p.add("place", np.concatenate([(rows[:, None] // 8 * 8 + m == rows[None, :]).astype(f) for m in range(8)], axis=1))
    arrays["l0f"], where["l0f"] = p.array(), p.where

    def experts(name, w1, w2, b1=None, b2=None, w3=None):
        n_exp, _, hidden = w1.shape
        nch = hidden // 128
        arrays[name + "_w1"] = np.ascontiguousarray(w1)
        arrays[name + "_w2"] = np.ascontiguousarray(w2.reshape(n_exp, nch, 128, D).transpose(0, 2, 1, 3))
        if w3 is not None:
            arrays[name + "_w3"] = np.ascontiguousarray(w3)
        if b1 is not None:
            arrays[name + "_b1"] = np.ascontiguousarray(b1.reshape(n_exp, nch, 128).transpose(2, 0, 1))
            arrays[name + "_b2"] = np.ascontiguousarray(b2)

    experts("l1f", x["L1_ffn_w1"][::-1], x["L1_ffn_w2"][::-1], x["L1_ffn_b1"][::-1], x["L1_ffn_b2"][::-1])
    arrays["l1f_router"] = np.ascontiguousarray(x["L1_ffn_router_w"][:, ::-1])
    arrays["l1f_router_b"] = np.ascontiguousarray(np.broadcast_to(x["L1_ffn_router_b"][::-1][None, :], (128, 64)))
    experts("l2f", x["L2_ffn_w1"].transpose(0, 2, 1), x["L2_ffn_w2"].transpose(0, 2, 1),
            w3=x["L2_ffn_w3"].transpose(0, 2, 1))
    arrays["l2f_router"] = np.ascontiguousarray(x["L2_ffn_gate_w"].T)
    arrays["l2f_sw1"] = np.ascontiguousarray(x["L2_ffn_sw1"].T)
    arrays["l2f_sw2"] = np.ascontiguousarray(x["L2_ffn_sw2"].T.reshape(4, 128, D).transpose(1, 0, 2))
    experts("l3f", x["L3_ffn_w1"], x["L3_ffn_w2"], x["L3_ffn_b1"], x["L3_ffn_b2"])
    arrays["l3f_router"] = np.ascontiguousarray(x["L3_ffn_gate_w"].T)
    return arrays, where


def kernel(**inputs):
    import numpy as np
    import concourse.bacc as bacc
    from concourse.bass_utils import run_bass_kernel_spmd

    x = {k: np.asarray(v) for k, v in inputs.items()}
    arrays, where = lay_out(x)
    nc = bacc.Bacc("TRN2", target_bir_lowering=False, num_devices=1)
    dram = {n: nc.dram_tensor(f"in_{n}", a.shape, mybir.dt.from_np(a.dtype), kind="ExternalInput").ap()
            for n, a in arrays.items()}
    out = nc.dram_tensor("out_0", (NB, S, D), F32, kind="ExternalOutput").ap()
    build_tower(nc, dram, where, out)
    r = run_bass_kernel_spmd(nc, [{f"in_{n}": a for n, a in arrays.items()}], core_ids=[0])
    return r.results[0]["out_0"]
```

```python
from contextlib import ExitStack

import concourse.bass as bass
from concourse import mybir

F32 = mybir.dt.float32
BF16 = mybir.dt.bfloat16
F16 = mybir.dt.float16
I32 = mybir.dt.int32
U32 = mybir.dt.uint32
ALU = mybir.AluOpType
ACT = mybir.ActivationFunctionType
AX = mybir.AxisListType

D = 128
NB, S = 8, 512
NT = NB * S
NTT = NT // 128
VOCAB = 25000
LN_EPS = 1e-5
BIG = 1e30
SCALE = 4096.0


def wait(eng, sem, value):
    if isinstance(value, int) and value <= 0:
        return
    eng.wait_ge(sem, value)


def turns(eng, count, body, peel=1):
    for i in range(min(peel, count)):
        body(i)
    if count > peel:
        with eng.Fori(peel, count) as i:
            body(i)


def skewed(eng, count, first, second):
    first(0)
    first(1)
    second(0)
    with eng.Fori(2, count) as i:
        first(i)
        second(i - 1)
    second(count - 1)


def cols(i, n=S):
    return bass.ds(i * n, n)


class Tower:

    def __init__(self, nc, ctx, dram, where):
        self.nc, self.ctx, self.dram, self.where = nc, ctx, dram, where
        self.h = self.sb(ctx, "h", [128, NT])
        self.xn = self.sb(ctx, "xn", [128, NT])
        self.base = self.sb(ctx, "base", [128, where["base"]["_width"]])
        self.ident = self.at(self.base, "base", "ident")
        self.mean = self.at(self.base, "base", "mean")
        self.eps = self.at(self.base, "base", "eps")
        self.stage_sems = []
        self.mean_every = self.at(self.base, "base", "mean_every")
        self.ln_count = 0
        self.ln_sems = {n: ctx.enter_context(nc.semaphore("ln_" + n)) for n in
                        ("mean", "centred", "square", "var", "std", "rstd", "spread", "norm")}

    def sb(self, ctx, name, shape, dt=F32):
        return ctx.enter_context(self.nc.sbuf_tensor(name, shape, dt))

    def ps(self, ctx, name, shape, dt=F32):
        return ctx.enter_context(self.nc.psum_tensor(name, shape, dt))

    def sem(self, name):
        self.stage_sems.append(self.nc.alloc_semaphore(name))
        return self.stage_sems[-1]

    def end_stage(self):
        with self.nc.Block() as block:
            @block.gpsimd
            def _(pool):
                self.nc.clear_and_free_semaphores(self.stage_sems)
        self.stage_sems = []

    def at(self, tile, pack, name):
        lo, hi = self.where[pack][name]
        return tile[:, lo:hi]


def load_base(t):
    nc = t.nc
    loaded = t.sem("base_loaded")
    with nc.Block() as block:
        @block.sync
        def _(sp):
            sp.dma_start(t.base[:, :], t.dram["base"]).then_inc(loaded, 16)
            sp.wait_ge(loaded, 16)


def layernorm(t):
    nc, h, xn = t.nc, t.h, t.xn
    q = t.ln_sems
    k = t.ln_count
    t.ln_count += 1
    with ExitStack() as ctx:
        n = f"ln{k}_"
        square = t.sb(ctx, n + "square", [128, 2, S])
        std, rstd = t.sb(ctx, n + "std", [128, S]), t.sb(ctx, n + "rstd", [128, S])
        ps_mean = t.ps(ctx, n + "ps_mean", [128, 3, S])
        ps_var = t.ps(ctx, n + "ps_var", [128, S])
        ps_b = t.ps(ctx, n + "ps_b", [128, 4, S])
        block = ctx.enter_context(nc.Block())

        @block.tensor
        def _(pe):
            def mean(i):
                if i >= 3:
                    pe.wait_ge(q["centred"], NB * k + i - 2)
                pe.matmul(ps_mean[:, i % 3, :], t.mean, h[:, cols(i)], start=True, stop=True).then_inc(q["mean"], 1)

            def var(i):
                pe.wait_ge(q["square"], NB * k + i + 1)
                pe.matmul(ps_var[:, :], t.mean_every[:, NB - 1 - i:NB - 1 - i + 128], square[:, i % 2, :],
                          start=(i == 0), stop=(i == NB - 1)).then_inc(q["var"], 1)
            mean(0)
            mean(1)
            for i in range(2, NB):
                mean(i)
                var(i - 2)
            var(NB - 2)
            var(NB - 1)
            pe.wait_ge(q["rstd"], k + 1)
            for i in range(NB):
                if i >= 4:
                    pe.wait_ge(q["norm"], NB * k + i - 3)
                pe.matmul(ps_b[:, i % 4, :], t.ident[:, i:i + 1].to_broadcast([128, 128]), rstd[:, :],
                          start=True, stop=True).then_inc(q["spread"], 1)

        @block.vector
        def _(dve):
            for i in range(NB):
                dve.wait_ge(q["mean"], NB * k + i + 1)
                dve.tensor_tensor(xn[:, cols(i)], h[:, cols(i)], ps_mean[:, i % 3, :], ALU.subtract)\
                   .then_inc(q["centred"], 1)
            dve.wait_ge(q["std"], k + 1)
            dve.reciprocal(rstd[:, :], std[:, :]).then_inc(q["rstd"], 1)
            for i in range(NB):
                dve.wait_ge(q["spread"], NB * k + i + 1)
                if i == 0:
                    dve.wait_ge(q["square"], NB * k + NB)
                dve.tensor_tensor(xn[:, cols(i)], xn[:, cols(i)], ps_b[:, i % 4, :], ALU.mult).then_inc(q["norm"], 1)

        @block.scalar
        def _(act):
            for i in range(NB):
                act.wait_ge(q["centred"], NB * k + i + 1)
                if i >= 2:
                    act.wait_ge(q["var"], NB * k + i - 1)
                act.activation(square[:, i % 2, :], xn[:, cols(i)], ACT.Square).then_inc(q["square"], 1)
            act.wait_ge(q["var"], NB * k + NB)
            act.activation(std[:, :], ps_var[:, :], ACT.Sqrt, bias=t.eps[:, 0:1]).then_inc(q["std"], 1)


def write_out(t, out):
    nc, h = t.nc, t.h
    with ExitStack() as ctx:
        hb = t.sb(ctx, "wo_hb", [128, 2, S])
        rows = t.sb(ctx, "wo_rows", [128, 2, S])
        ps_t = t.ps(ctx, "wo_ps", [128, 2, S])
        copied, turned, evacuated = t.sem("wo_copied"), t.sem("wo_turned"), t.sem("wo_evacuated")
        stored = [t.sem("wo_stored0"), t.sem("wo_stored1")]
        block = ctx.enter_context(nc.Block())

        @block.gpsimd
        def _(pool):
            def body(j):
                for s in range(2):
                    wait(pool, turned, 2 * j + s - 1)
                    pool.tensor_copy(hb[:, s, :], h[:, bass.ds(j * 2 * S + s * S, S)]).then_inc(copied, 1)
            turns(pool, NB // 2, body)

        @block.tensor
        def _(pe):
            def body(j):
                for s in range(2):
                    pe.wait_ge(copied, 2 * j + s + 1)
                    wait(pe, evacuated, 2 * j + s - 1)
                    for c in range(4):
                        last = pe.transpose(ps_t[:, s, 128 * c:128 * c + 128], hb[:, s, 128 * c:128 * c + 128],
                                            t.ident)
                    last.then_inc(turned, 1)
            turns(pe, NB // 2, body)

        @block.vector
        def _(dve):
            def body(j):
                for s in range(2):
                    dve.wait_ge(turned, 2 * j + s + 1)
                    wait(dve, stored[s], 16 * j)
                    dve.tensor_copy(rows[:, s, :], ps_t[:, s, :]).then_inc(evacuated, 1)
            turns(dve, NB // 2, body)

        @block.sync
        def _(sp):
            def body(j):
                for s in range(2):
                    sp.wait_ge(evacuated, 2 * j + s + 1)
                    sp.dma_start(out[bass.ds(j * 2 + s, 1), :, :].rearrange("a (c p) d -> p (a c) d", p=128),
                                 rows[:, s, :].rearrange("p (c d) -> p c d", c=4)).then_inc(stored[s], 16)
            turns(sp, NB // 2, body)
            for s in range(2):
                sp.wait_ge(stored[s], 16 * (NB // 2))


def embed(t):
    nc, h = t.nc, t.h
    with ExitStack() as ctx:
        sb = lambda n, shape, dt=F32: t.sb(ctx, "tok_" + n, shape, dt)
        sem = lambda n: t.sem("tok_" + n)
        w = sb("w", [128, t.where["tok"]["_width"]])
        proj, proj_b = t.at(w, "tok", "proj"), t.at(w, "tok", "proj_b")
        xi, xf = sb("xi", [NB, S], I32), sb("xf", [NB, S])
        v, r, fix = sb("v", [NB, S]), sb("r", [NB, S]), sb("fix", [NB, S])
        quot = sb("quot", [NB, S], I32)
        ids = sb("ids", [NB, 3, S])
        idx = sb("idx", [128, 3, 4, NB], U32)
        rows = sb("rows", [128, 2, 3, 4, 128])
        emb = sb("emb", [128, 3, S])
        ps_i = t.ps(ctx, "tok_ps_i", [128, S])
        ps_t = t.ps(ctx, "tok_ps_t", [128, 3, S])
        ps_p = t.ps(ctx, "tok_ps_p", [128, 2, S])
        loaded, zeroed, x_in, chain = sem("loaded"), sem("zeroed"), sem("x_in"), sem("chain")
        ids_ready, ids_turned, idx_ready = sem("ids_ready"), sem("ids_turned"), sem("idx_ready")
        gathered = [sem("gathered0"), sem("gathered1")]
        turned, emb_ready, projected, h_ready = sem("turned"), sem("emb_ready"), sem("projected"), sem("h_ready")
        block = ctx.enter_context(nc.Block())

        @block.sync
        def _(sp):
            sp.dma_start(xi[:, :], t.dram["x"]).then_inc(x_in, 16)
            sp.dma_start(w[:, :], t.dram["tok"]).then_inc(loaded, 16)
            sp.wait_ge(loaded, 16)

        @block.vector
        def _(dve):
            steps = [0]

            def then(ins):
                steps[0] += 1
                ins.then_inc(chain, 1)
                dve.wait_ge(chain, steps[0])

            def modulo(n):
                then(dve.tensor_scalar(quot[:, 0:n], v[:, 0:n], 1.0 / VOCAB, None, ALU.mult))
                then(dve.scalar_tensor_tensor(r[:, 0:n], quot[:, 0:n], -float(VOCAB), v[:, 0:n], ALU.mult, ALU.add))
                then(dve.tensor_scalar(fix[:, 0:n], r[:, 0:n], 0.0, float(VOCAB), ALU.is_lt, ALU.mult))
                then(dve.tensor_tensor(r[:, 0:n], r[:, 0:n], fix[:, 0:n], ALU.add))
                then(dve.tensor_scalar(fix[:, 0:n], r[:, 0:n], float(VOCAB), -float(VOCAB), ALU.is_ge, ALU.mult))
                then(dve.tensor_tensor(r[:, 0:n], r[:, 0:n], fix[:, 0:n], ALU.add))

            dve.memset(ids[:, :, :], 0.0).then_inc(zeroed, 1)
            dve.wait_ge(x_in, 16)
            then(dve.tensor_copy(xf[:, :], xi[:, :]))
            then(dve.tensor_copy(v[:, :], xf[:, :]))
            modulo(S)
            dve.wait_ge(zeroed, 1)
            for n in range(2, 5):
                m, c = S - n + 1, n // 2
                then(dve.scalar_tensor_tensor(v[:, 0:m], r[:, 0:m], 64.0, xf[:, n - 1:n - 1 + m], ALU.mult, ALU.add))
                modulo(m)
                then(dve.tensor_copy(ids[:, n - 2, c:c + m], r[:, 0:m]))
            dve.sem_inc(ids_ready, 1)
            dve.wait_ge(ids_turned, 1)
            dve.tensor_copy(idx[:, :, :, :].rearrange("p a c b -> p (a c b)"), ps_i[:, 0:96]).then_inc(idx_ready, 1)

            def body(b):
                dve.wait_ge(turned, b + 1)
                wait(dve, projected, b)
                dve.tensor_copy(emb[:, 0, 1:S], ps_t[:, 0, 1:S]).then_inc(emb_ready, 1)
                dve.tensor_copy(emb[:, 1, 1:S - 1], ps_t[:, 1, 1:S - 1]).then_inc(emb_ready, 1)
                dve.tensor_copy(emb[:, 2, 2:S - 1], ps_t[:, 2, 2:S - 1]).then_inc(emb_ready, 1)
            dve.memset(emb[:, :, 0:2], 0.0).then_inc(zeroed, 1)
            dve.memset(emb[:, :, S - 1:S], 0.0).then_inc(zeroed, 1)
            dve.wait_ge(zeroed, 3)
            turns(dve, NB, body)

        @block.gpsimd
        def _(pool):
            pool.wait_ge(idx_ready, 1)
            for b in range(NB):
                wait(pool, turned, b - 1)
                for n in range(3):
                    for c in range(4):
                        pool.indirect_dma_start(
                            rows[:, b % 2, n, c, :], None, t.dram[f"emb{n + 2}"],
                            bass.IndirectOffsetOnAxis(ap=idx[:, n, c, b:b + 1], axis=0),
                            ).then_inc(gathered[b % 2], 16)

        @block.scalar
        def _(act):
            act.wait_ge(loaded, 16)

            def body(b):
                act.wait_ge(projected, b + 1)
                act.activation(h[:, cols(b)], ps_p[:, b % 2, :], ACT.Identity, bias=proj_b).then_inc(h_ready, 1)
            turns(act, NB, body)

        @block.tensor
        def _(pe):
            pe.wait_ge(ids_ready, 1)
            for n in range(3):
                for c in range(4):
                    at = 32 * n + 8 * c
                    last = pe.transpose(ps_i[:, at:at + 8], ids[:, n, 128 * c:128 * c + 128], t.ident[0:NB, 0:NB])
            last.then_inc(ids_turned, 1)
            pe.wait_ge(loaded, 16)

            def body(j):
                for s in range(2):
                    b = 2 * j + s
                    pe.wait_ge(gathered[s], 16 * 12 * (j + 1))
                    wait(pe, emb_ready, 3 * b)
                    for n in range(3):
                        for c in range(4):
                            last = pe.transpose(ps_t[:, n, 128 * c:128 * c + 128], rows[:, s, n, c, :], t.ident)
                    last.then_inc(turned, 1)
                    pe.wait_ge(emb_ready, 3 * b + 3)
                    wait(pe, h_ready, b - 1)
                    for n in range(3):
                        last = pe.matmul(ps_p[:, s, :], proj[:, 128 * n:128 * n + 128], emb[:, n, :],
                                         start=(n == 0), stop=(n == 2))
                    last.then_inc(projected, 1)
            turns(pe, NB // 2, body)


def memory_mixer(t):
    nc, h, xn = t.nc, t.h, t.xn
    with ExitStack() as ctx:
        sb = lambda n, shape, dt=F32: t.sb(ctx, "l0a_" + n, shape, dt)
        sem = lambda n: t.sem("l0a_" + n)
        w = sb("w", [128, t.where["l0a"]["_width"]])
        at = lambda n: t.at(w, "l0a", n)
        s1, qp, conv = sb("s1", [128, S]), sb("qp", [128, S + 3]), sb("conv", [128, S])
        s2, sq = sb("s2", [128, 2, S]), sb("sq", [128, 2, S])
        norm, rnorm, qn = sb("norm", [128, S]), sb("rnorm", [128, S]), sb("qn", [128, S])
        u, r = sb("u", [128, 2, S]), sb("r", [128, S])
        ps_1, ps_2 = t.ps(ctx, "l0a_ps1", [128, S]), t.ps(ctx, "l0a_ps2", [128, S])
        ps_n, ps_u = t.ps(ctx, "l0a_psn", [128, S]), t.ps(ctx, "l0a_psu", [128, 2, S])
        ps_r, ps_o = t.ps(ctx, "l0a_psr", [128, S]), t.ps(ctx, "l0a_pso", [128, S])
        loaded, zeroed = sem("loaded"), sem("zeroed")
        p1, s1_ready, p2, qp_ready, tapped = sem("p1"), sem("s1_ready"), sem("p2"), sem("qp_ready"), sem("tapped")
        s2_ready, sq_ready, summed, norm_ready = sem("s2_ready"), sem("sq_ready"), sem("summed"), sem("norm_ready")
        guarded, inverted, qn_ready = sem("guarded"), sem("inverted"), sem("qn_ready")
        up, u_ready, down, r_ready, outp, h_ready = [sem(n) for n in
                                                    ("up", "u_ready", "down", "r_ready", "outp", "h_ready")]
        block = ctx.enter_context(nc.Block())

        @block.sync
        def _(sp):
            sp.dma_start(w[:, :], t.dram["l0a"]).then_inc(loaded, 16)
            sp.wait_ge(loaded, 16)

        @block.tensor
        def _(pe):
            pe.wait_ge(loaded, 16)

            def first(b):
                wait(pe, s1_ready, b)
                pe.matmul(ps_1[:, :], at("q1"), xn[:, cols(b)], start=True, stop=True).then_inc(p1, 1)
                pe.wait_ge(s1_ready, b + 1)
                wait(pe, qp_ready, b)
                pe.matmul(ps_2[:, :], at("q2"), s1[:, :], start=True, stop=True).then_inc(p2, 1)

            def second(b):
                pe.wait_ge(sq_ready, b + 1)
                wait(pe, norm_ready, b)
                pe.matmul(ps_n[:, :], at("ones"), sq[:, b % 2, :], start=True, stop=True).then_inc(summed, 1)
                pe.wait_ge(qn_ready, b + 1)
                wait(pe, u_ready, b)
                for c in range(2):
                    last = pe.matmul(ps_u[:, c, :], at("m1")[:, 128 * c:128 * c + 128], qn[:, :], start=True, stop=True)
                last.then_inc(up, 1)
                pe.wait_ge(u_ready, b + 1)
                wait(pe, r_ready, b)
                for c in range(2):
                    last = pe.matmul(ps_r[:, :], at("m2")[:, 128 * c:128 * c + 128], u[:, c, :],
                                     start=(c == 0), stop=(c == 1))
                last.then_inc(down, 1)
                pe.wait_ge(r_ready, b + 1)
                wait(pe, h_ready, b)
                pe.matmul(ps_o[:, :], at("out"), r[:, :], start=True, stop=True).then_inc(outp, 1)
            skewed(pe, NB, first, second)

        @block.scalar
        def _(act):
            act.wait_ge(zeroed, 1)

            def first(b):
                act.wait_ge(p1, b + 1)
                wait(act, p2, b)
                act.activation(s1[:, :], ps_1[:, :], ACT.Silu).then_inc(s1_ready, 1)
                act.wait_ge(p2, b + 1)
                wait(act, tapped, 4 * b)
                act.activation(qp[:, 3:S + 3], ps_2[:, :], ACT.Copy).then_inc(qp_ready, 1)
                act.wait_ge(tapped, 4 * b + 4)
                if not (isinstance(b, int) and b < 2):
                    act.wait_ge(qn_ready, b - 1)
                    act.wait_ge(summed, b - 1)
                act.activation(s2[:, b % 2, :], conv[:, :], ACT.Silu).then_inc(s2_ready, 1)
                act.wait_ge(s2_ready, b + 1)
                act.activation(sq[:, b % 2, :], s2[:, b % 2, :], ACT.Square).then_inc(sq_ready, 1)

            def second(b):
                act.wait_ge(summed, b + 1)
                wait(act, qn_ready, b)
                act.activation(norm[:, :], ps_n[:, :], ACT.Sqrt).then_inc(norm_ready, 1)
                act.wait_ge(up, b + 1)
                wait(act, down, b)
                act.activation(u[:, :, :], ps_u[:, :, :], ACT.Silu).then_inc(u_ready, 1)
                act.wait_ge(down, b + 1)
                wait(act, outp, b)
                act.activation(r[:, :], ps_r[:, :], ACT.Copy).then_inc(r_ready, 1)
            skewed(act, NB, first, second)

        @block.vector
        def _(dve):
            dve.memset(qp[:, 0:3], 0.0).then_inc(zeroed, 1)
            dve.wait_ge(zeroed, 1)
            dve.wait_ge(loaded, 16)

            def first(b):
                dve.wait_ge(qp_ready, b + 1)
                wait(dve, s2_ready, b)
                dve.tensor_scalar(conv[:, :], qp[:, 0:S], at("conv_w")[:, 0:1], at("conv_b"), ALU.mult, ALU.add)\
                   .then_inc(tapped, 1)
                for j in range(1, 4):
                    dve.wait_ge(tapped, 4 * b + j)
                    dve.scalar_tensor_tensor(conv[:, :], qp[:, j:S + j], at("conv_w")[:, j:j + 1], conv[:, :],
                                             ALU.mult, ALU.add).then_inc(tapped, 1)

            def second(b):
                dve.wait_ge(norm_ready, b + 1)
                dve.tensor_scalar(norm[:, :], norm[:, :], 1e-12, None, ALU.max).then_inc(guarded, 1)
                dve.wait_ge(guarded, b + 1)
                wait(dve, qn_ready, b)
                dve.reciprocal(rnorm[:, :], norm[:, :]).then_inc(inverted, 1)
                dve.wait_ge(inverted, b + 1)
                dve.wait_ge(s2_ready, b + 1)
                wait(dve, up, b)
                dve.tensor_tensor(qn[:, :], s2[:, b % 2, :], rnorm[:, :], ALU.mult).then_inc(qn_ready, 1)
                dve.wait_ge(outp, b + 1)
                dve.tensor_tensor(h[:, cols(b)], h[:, cols(b)], ps_o[:, :], ALU.add).then_inc(h_ready, 1)
            skewed(dve, NB, first, second)


TURNS = 2
FIRST = 4


def per_turn(f, b, j):
    if isinstance(j, int):
        return f(b)
    return j * (f(b + 2) - f(b)) + f(b)


def wait_turn(eng, sem, f, b, j):
    if f(b) <= 0:
        assert isinstance(j, int), "a loop's wait has to be above zero in its first turn"
        return
    eng.wait_ge(sem, per_turn(f, b, j))


class Banks:

    def __init__(self, items, sems):
        self.number, self.count, self.sems, self.before = {}, {}, sems, []
        counts = {"act": 0, "dve": 0}
        for n in range(-2, 18):
            for slot, kind, b, reader in items(n):
                counts[reader] += 1
                self.number[kind, b] = len(self.before)
                self.count[kind, b] = (reader, counts[reader])
                self.before.append((reader, counts[reader]))

    def bank(self, kind, b):
        return self.number[kind, b] % 2

    def wait_free(self, pe, kind, b, j):
        if self.number[kind, b] >= 2:
            reader, _ = self.before[self.number[kind, b] - 2]
            def value(b):
                r, count = self.before[self.number[kind, b] - 2]
                assert r == reader
                return count
            wait_turn(pe, self.sems[reader], value, b, j)

    def wait_filled(self, eng, kind, b, j):
        wait_turn(eng, self.sems["filled"], lambda b: self.number[kind, b] + 1, b, j)

    def wait_read(self, eng, kind, b, j):
        reader, _ = self.count[kind, b]
        wait_turn(eng, self.sems[reader], lambda b: self.count[kind, b][1], b, j)


def attention(t, name, prepare, preps, stacks, sel, n_tiles=1, causal=False, scale=0.25, plus_input=False,
              once=()):
    nc = t.nc
    GROUPS, LAST = 2 * NB, 20
    NST = len(stacks)
    MAX0 = stacks[-1][0]
    heads_per_tile = 8 // n_tiles
    with ExitStack() as ctx:
        sb = lambda n, shape, dt=F32: t.sb(ctx, f"{name}_{n}", shape, dt)
        sem = lambda n: t.sem(f"{name}_{n}")
        w = sb("w", [128, t.where[name]["_width"]])
        at = lambda n: t.at(w, name, n)
        sel_w = t.where[sel]["_width"]
        select = [sb("select_q", [128, sel_w // 2], BF16), sb("select_k", [128, sel_w // 2], BF16)]
        x = sb("x", [128, S])
        qk = [sb("q", [128, n_tiles, S]), sb("k", [128, n_tiles, S])]
        rest = sb("rest", [128, S])
        parts = [sb("q_parts", [128, 2, 3, n_tiles, S], BF16), sb("k_parts", [128, 2, 3, n_tiles, S], BF16)]
        stack = [sb("q_stack", [128, NST, 4, 4, S], BF16), sb("k_stack", [128, NST, 4, 4, S], BF16)]
        maxima = sb("maxima", [128, 4, 4])
        max_rest = sb("max_rest", [128, 2, 4, 4])
        max_parts = sb("max_parts", [128, 4, 128], BF16)
        v = sb("v", [128, 2, 4, 8, 32])
        probs = sb("probs", [128, 8, S])
        o = sb("o", [128, 2, S])
        o_norm = sb("o_norm", [128, 2, S])
        rden = sb("rden", [128, S])
        identb = sb("identb", [128, 128], BF16)
        mask, maskb = (sb("mask", [128, 2, 128]), sb("maskb", [128, 2, 128], BF16)) if causal else (None, None)
        ps_1 = t.ps(ctx, name + "_ps_1", [128, 2, S])
        ps_2 = t.ps(ctx, name + "_ps_2", [128, 2, S])
        ps_o = t.ps(ctx, name + "_ps_o", [128, S])
        ps_m = t.ps(ctx, name + "_ps_m", [128, 1024], BF16)
        pj = t.ps(ctx, name + "_pj", [128, 2, S])
        idle = sem("idle")
        loaded, sel_in, sel_cast, zeroed, filled_in = sem("loaded"), sem("sel_in"), sem("sel_cast"), sem("zeroed"), sem("filled_in")
        x_ready, v_ready = sem("x_ready"), sem("v_ready")
        final = [sem("q_final"), sem("k_final")]
        split = [sem("q_split"), sem("k_split")]
        scored1, maxed, max_split, turned, shift_ready = [sem(n) for n in
                                                          ("scored1", "maxed", "max_split", "turned", "shift_ready")]
        scored2, exped, mixed, o_ready = sem("scored2"), sem("exped"), sem("mixed"), sem("o_ready")
        o_normed, h_ready = sem("o_normed"), sem("h_ready")
        reads = {"filled": sem("filled"), "act": sem("read_act"), "dve": sem("read_dve")}
        n_loads = 32 if causal else 16

        sels = [("sel", hd, s, st) for hd in range(4) for s in range(2) for st in range(NST)]

        def items(n):
            out = []
            if n % 2 == 0:
                if n == -2:
                    out += [(0, use, 0, "act") for use in once]
                out += [(place, use, n // 2 + 1, reader) for place, use, reader in preps if n // 2 + 1 < NB]
            else:
                if n // 2 + 1 < NB:
                    out += [(0, "v", n // 2 + 1, "dve")]
                if n // 2 - 1 >= 0:
                    out += [(p, use, n // 2 - 1, "dve") for p, use in ((3, "den0"), (7, "den1"), (11, "out"))]
            if 0 <= n + 1 < GROUPS:
                first, room = 4, LAST - 4
                out += [(first + i * room // len(sels), (*u, (n + 1) % 2), (n + 1) // 2, ("act", "dve")[u[2]])
                        for i, u in enumerate(sels)]
            return sorted(out, key=lambda item: item[0])

        banks = Banks(items, reads)
        a = {"at": at, "sb": sb, "sem": sem, "x": x, "qk": qk, "pj": pj, "x_ready": x_ready, "final": final,
             "split": split, "banks": banks, "reads": reads}
        pre = prepare(t, a)
        wv, wo, den, bv, bo = at("v"), at("o"), at("den"), at("bv"), at("bo")
        block = ctx.enter_context(nc.Block())

        def steps(eng, step):
            for n in range(-2, FIRST):
                step(n, 0)
            with eng.Fori(0, TURNS) as j:
                for n in range(FIRST, FIRST + 4):
                    step(n, j)
            for n in range(FIRST + 4 * TURNS, GROUPS + 2):
                step(n, 0)

        def span(tile, as_keys):
            if not causal:
                return 0, S
            return (128 * tile, S) if as_keys else (0, 128 * tile + 128)

        def cols_turn(b, j):
            return cols(b) if isinstance(j, int) else bass.ds(j * (2 * S) + b * S, S)

        @block.sync
        def _(sp):
            sp.dma_start(w[:, :], t.dram[name]).then_inc(loaded, 16)
            if causal:
                sp.dma_start(mask[:, :, :], t.dram["causal"].rearrange("p (a c) -> p a c", a=2)).then_inc(loaded, 16)
            for s in range(2):
                wait(sp, sel_cast, s)
                sp.dma_start(probs[:, :, :].rearrange("p a s -> p (a s)")[:, 0:sel_w // 2],
                             t.dram[sel][:, s * (sel_w // 2):(s + 1) * (sel_w // 2)]).then_inc(sel_in, 16)
            sp.wait_ge(loaded, n_loads)
            sp.wait_ge(sel_in, 32)

        @block.gpsimd
        def _(pool):
            pool.memset(max_parts[:, :, :], 0.0).then_inc(zeroed, 1)
            pool.memset(v[:, :, :, :, 16:32], 0.0).then_inc(zeroed, 1)
            pool.wait_ge(zeroed, 2)
            pool.memset(v[:, :, :, :, 16:17], 1.0).then_inc(zeroed, 1)
            pool.wait_ge(loaded, n_loads)

            def body(jj):
                for parity in range(2):
                    b = 2 * jj + parity
                    wait(pool, v_ready, b)
                    pre["input"](pool, b)
                    for i in range(n_tiles):
                        for s in range(2):
                            m = n_tiles * b + i
                            pool.wait_ge(final[s], m + 1)
                            wait(pool, scored1, 32 * b - 32)
                            pool.sem_inc(idle, 1)
                            p, tile = parts[s][:, parity, :, i, :], qk[s][:, i, :]
                            pool.tensor_copy(p[:, 0, :], tile).then_inc(split[s], 1)
                            pool.wait_ge(split[s], 4 * m + 1)
                            pool.tensor_tensor(rest[:, :], tile, p[:, 0, :], ALU.subtract).then_inc(split[s], 1)
                            pool.wait_ge(split[s], 4 * m + 2)
                            pool.sem_inc(idle, 1)
                            pool.tensor_copy(p[:, 1, :], rest[:, :]).then_inc(split[s], 1)
                            pool.wait_ge(split[s], 4 * m + 3)
                            pool.tensor_tensor(p[:, 2, :], rest[:, :], p[:, 1, :], ALU.subtract).then_inc(split[s], 1)
                            pool.wait_ge(split[s], 4 * m + 4)
            turns(pool, NB // 2, body, peel=2)

        @block.scalar
        def _(act):
            for s in range(2):
                act.wait_ge(sel_in, 16 * s + 16)
                act.activation(select[s][:, :], probs[:, :, :].rearrange("p a s -> p (a s)")[:, 0:sel_w // 2], ACT.Copy)\
                   .then_inc(sel_cast, 1)
            act.wait_ge(sel_cast, 2)
            act.wait_ge(loaded, n_loads)

            def step(n, j):
                m, bm, gm = n - 1, (n - 1) // 2, (n - 1) % 2
                todo = items(n)
                for place in range(LAST + 1):
                    u = place - 3
                    if 0 <= m < GROUPS and 0 <= u < 16:
                        lo, hi = span(u // 4, True)
                        wait_turn(act, scored2, lambda b: 16 * (2 * b + gm) + u + 1, bm, j)
                        wait_turn(act, mixed, lambda b: 4 * (2 * b + gm) + u // 4 - 1, bm, j)
                        act.activation(probs[:, u % 8, lo:hi], ps_2[:, u % 2, lo:hi], ACT.Exp, scale=scale)\
                           .then_inc(exped, 1)
                    for _, use, b, reader in [item for item in todo if item[0] == place]:
                        if use[0] == "sel":
                            _, hd, s, st, g = use
                            if reader == "act":
                                banks.wait_filled(act, use, b, j)
                                M = stacks[st][0]
                                act.activation(stack[s][0:M, st, (2 * b + g) % 4, hd, :], pj[0:M, banks.bank(use, b), :],
                                               ACT.Copy).then_inc(reads["act"], 1)
                        elif use in pre["act"]:
                            pre["act"][use](act, b, j)
                    if place == 18 and 0 <= n < GROUPS:
                        wait_turn(act, turned, lambda b: 2 * b + n % 2 + 1, n // 2, j)
                        act.activation(stack[0][MAX0:MAX0 + 32, NST - 1, n % 4, :, :],
                                       ps_m[MAX0:MAX0 + 32, 0:S].rearrange("p (o s) -> p o s", o=1).to_broadcast([32, 4, S]),
                                       ACT.Copy).then_inc(shift_ready, 1)
            steps(act, step)

        @block.vector
        def _(dve):
            dve.wait_ge(loaded, n_loads)
            for i in range(4):
                dve.tensor_copy(stack[1][MAX0:MAX0 + 32, NST - 1, i, :, :],
                                at("minus")[MAX0:MAX0 + 32, :].rearrange("p (h o) -> p h o", o=1).to_broadcast([32, 4, S]))\
                   .then_inc(filled_in, 1)
            dve.tensor_copy(identb[:, :], t.ident).then_inc(filled_in, 1)
            if causal:
                dve.tensor_copy(maskb[:, :, :], mask[:, :, :]).then_inc(filled_in, 1)
            dve.wait_ge(filled_in, 6 if causal else 5)
            dve.wait_ge(zeroed, 3)
            if "setup" in pre:
                pre["setup"](dve)

            def step(n, j):
                bn, g = n // 2, n % 2
                todo = items(n)
                for place in range(LAST + 1):
                    u = place
                    if 0 <= n < GROUPS and u < 16:
                        hd, c = u // 4, u % 4
                        lo, hi = span(c, False)
                        wait_turn(dve, scored1, lambda b: 16 * (2 * b + g) + u + 1, bn, j)
                        dve.tensor_reduce(maxima[:, c, hd:hd + 1], ps_1[:, u % 2, lo:hi], AX.X, ALU.max).then_inc(maxed, 1)
                    if place == 2 and 0 <= n - 2 < GROUPS:
                        wait_turn(dve, mixed, lambda b: 4 * (2 * b + g) + 4, bn - 1, j)
                        dve.tensor_copy(o[:, g, :], ps_o[:, :]).then_inc(o_ready, 1)
                    for _, use, b, reader in [item for item in todo if item[0] == place]:
                        if use[0] == "sel":
                            _, hd, s, st, sg = use
                            if reader == "dve":
                                banks.wait_filled(dve, use, b, j)
                                M = stacks[st][0]
                                dve.tensor_copy(stack[s][0:M, st, (2 * b + sg) % 4, hd, :], pj[0:M, banks.bank(use, b), :])\
                                   .then_inc(reads["dve"], 1)
                        elif use == "v":
                            banks.wait_filled(dve, use, b, j)
                            dve.tensor_tensor(v[:, b % 2, :, :, 0:16],
                                              pj[:, banks.bank(use, b), :].rearrange("p (c h d) -> p c h d", c=4, d=16),
                                              bv.rearrange("p (a h d) -> p a h d", a=1, d=16).to_broadcast([128, 4, 8, 16]),
                                              ALU.add).then_inc(reads["dve"], 1)
                            banks.wait_read(dve, use, b, j)
                            dve.sem_inc(v_ready, 1)
                        elif use in ("den0", "den1"):
                            i = int(use[3])
                            banks.wait_filled(dve, use, b, j)
                            wait_turn(dve, o_normed, lambda b: 2 * b + i, b, j)
                            dve.reciprocal(rden[:, :], pj[:, banks.bank(use, b), :]).then_inc(reads["dve"], 1)
                            banks.wait_read(dve, use, b, j)
                            wait_turn(dve, o_ready, lambda b: 2 * b + i + 1, b, j)
                            wait_turn(dve, h_ready, lambda b: (2 if plus_input else 1) * b, b, j)
                            dve.tensor_tensor(o_norm[:, i, :], o[:, i, :], rden[:, :], ALU.mult).then_inc(o_normed, 1)
                        elif use == "out":
                            hb = t.h[:, cols_turn(b, j)]
                            banks.wait_filled(dve, use, b, j)
                            dve.scalar_tensor_tensor(hb, pj[:, banks.bank(use, b), :], bo, hb, ALU.add, ALU.add)\
                               .then_inc(reads["dve"], 1)
                            banks.wait_read(dve, use, b, j)
                            dve.sem_inc(h_ready, 1)
                            if plus_input:
                                dve.tensor_tensor(hb, hb, t.xn[:, cols_turn(b, j)], ALU.add).then_inc(h_ready, 1)
                        elif use in pre["dve"]:
                            pre["dve"][use](dve, b, j)
                    if place == 16 and 0 <= n < GROUPS:
                        wait_turn(dve, maxed, lambda b: 16 * (2 * b + g) + 16, bn, j)
                        wait_turn(dve, turned, lambda b: 2 * b + g, bn, j)
                        into = lambda i: max_parts[:, :, MAX0 + 4 * i:MAX0 + 4 * i + 4]
                        done = lambda i: wait_turn(dve, max_split, lambda b: 5 * (2 * b + g) + i, bn, j)
                        dve.tensor_copy(into(0), maxima[:, :, :]).then_inc(max_split, 1)
                        done(1)
                        dve.tensor_tensor(max_rest[:, 0, :, :], maxima[:, :, :], into(0), ALU.subtract).then_inc(max_split, 1)
                        done(2)
                        dve.tensor_copy(into(1), max_rest[:, 0, :, :]).then_inc(max_split, 1)
                        done(3)
                        dve.tensor_tensor(max_rest[:, 1, :, :], max_rest[:, 0, :, :], into(1), ALU.subtract)\
                           .then_inc(max_split, 1)
                        done(4)
                        dve.tensor_copy(into(2), max_rest[:, 1, :, :]).then_inc(max_split, 1)
            steps(dve, step)

        @block.tensor
        def _(pe):
            pe.wait_ge(loaded, n_loads)
            pe.wait_ge(sel_cast, 2)
            pe.wait_ge(filled_in, 6 if causal else 5)

            def step(n, j):
                bn, g = n // 2, n % 2
                m, bm, gm = n - 1, (n - 1) // 2, (n - 1) % 2
                todo = items(n)
                for place in range(LAST + 1):
                    u = place
                    if 0 <= n < GROUPS and u < 16:
                        hd, c = u // 4, u % 4
                        lo, hi = span(c, False)
                        if c == 0:
                            for s in range(2):
                                banks.wait_read(pe, ("sel", hd, s, NST - 1, g), bn, j)
                        wait_turn(pe, maxed, lambda b: 16 * (2 * b + g) + u - 1, bn, j)
                        M, d = stacks[0][0], 128 * c
                        last = pe.matmul(ps_1[:, u % 2, lo:hi], stack[0][0:M, 0, n % 4, hd, d:d + 128],
                                         stack[1][0:M, 0, n % 4, hd, lo:hi], start=True, stop=not causal)
                        if causal:
                            last = pe.matmul(ps_1[:, u % 2, d:d + 128], identb[:, :], maskb[:, 0, :], start=False, stop=True)
                        last.then_inc(scored1, 1)
                    u = place - 3
                    if 0 <= m < GROUPS and 0 <= u < 16:
                        c, hd = u // 4, u % 4
                        lo, hi = span(c, True)
                        if u == 0:
                            wait_turn(pe, shift_ready, lambda b: 2 * b + gm + 1, bm, j)
                        wait_turn(pe, exped, lambda b: 16 * (2 * b + gm) + u - 1, bm, j)
                        d = 128 * c
                        for st in range(NST):
                            M = MAX0 + 32 if st == NST - 1 else stacks[st][0]
                            last = pe.matmul(ps_2[:, u % 2, lo:hi], stack[1][0:M, st, m % 4, hd, d:d + 128],
                                             stack[0][0:M, st, m % 4, hd, lo:hi], start=(st == 0),
                                             stop=(st == NST - 1 and not causal))
                        if causal:
                            last = pe.matmul(ps_2[:, u % 2, d:d + 128], identb[:, :], maskb[:, 1, :], start=False, stop=True)
                        last.then_inc(scored2, 1)
                    if 0 <= m < GROUPS and place >= 8 and place % 4 == 0:
                        c = (place - 8) // 4
                        lo, hi = span(c, True)
                        if c == 0:
                            wait_turn(pe, v_ready, lambda b: b + 1, bm, j)
                            wait_turn(pe, o_ready, lambda b: 2 * b + gm, bm, j)
                        wait_turn(pe, exped, lambda b: 16 * (2 * b + gm) + 4 * c + 4, bm, j)
                        for hd in range(4):
                            last = pe.matmul(ps_o[32 * hd:32 * hd + 32, lo:hi], v[:, bm % 2, c, 4 * gm + hd, :],
                                             probs[:, (4 * c + hd) % 8, lo:hi], start=(c == 0), stop=(c == 3))
                        last.then_inc(mixed, 1)
                    for _, use, b, reader in [item for item in todo if item[0] == place]:
                        banks.wait_free(pe, use, b, j)
                        to = pj[:, banks.bank(use, b), :]
                        if use[0] == "sel":
                            _, hd, s, st, sg = use
                            M, used = stacks[st][0], stacks[st][1 + s]
                            head = 4 * sg + hd
                            tile, head = head // heads_per_tile, head % heads_per_tile
                            wait_turn(pe, split[s], lambda b: 4 * (n_tiles * b + tile + 1), b, j)
                            lo = sum(len(stacks[i][1 + s]) * heads_per_tile * stacks[i][0] for i in range(st))
                            for i, p in enumerate(used):
                                at_ = lo + (i * heads_per_tile + head) * M
                                last = pe.matmul(to[0:M, :], select[s][:, at_:at_ + M], parts[s][:, b % 2, p, tile, :],
                                                 start=(i == 0), stop=(i == len(used) - 1))
                        elif use == "v":
                            for c in range(4):
                                last = pe.matmul(to[:, 128 * c:128 * c + 128], x[:, 128 * c:128 * c + 128], wv,
                                                 start=True, stop=True)
                        elif use in ("den0", "den1"):
                            i = int(use[3])
                            wait_turn(pe, o_ready, lambda b: 2 * b + i + 1, b, j)
                            last = pe.matmul(to, den, o[:, i, :], start=True, stop=True)
                        elif use == "out":
                            wait_turn(pe, o_normed, lambda b: 2 * b + 2, b, j)
                            for i in range(2):
                                last = pe.matmul(to, wo[:, 128 * i:128 * i + 128], o_norm[:, i, :],
                                                 start=(i == 0), stop=(i == 1))
                        else:
                            last = pre["pe"][use](pe, b, j, to)
                        last.then_inc(reads["filled"], 1)
                    if place == 17 and 0 <= n < GROUPS:
                        wait_turn(pe, max_split, lambda b: 5 * (2 * b + g) + 5, bn, j)
                        wait_turn(pe, shift_ready, lambda b: 2 * b + g, bn, j)
                        for c in range(4):
                            last = pe.transpose(ps_m[:, 128 * c:128 * c + 128], max_parts[:, c, :], identb[:, :])
                        last.then_inc(turned, 1)
            steps(pe, step)


STACK16 = [(96, (0, 1, 2), (0, 1, 2))]
Q16, K16 = (0, 0, 0, 1, 1, 2), (0, 1, 2, 0, 1, 0)
STACK32 = [(128, (0, 1), (0, 1)), (64, (0, 2), (0, 2))]
Q32, K32 = ((0, 0, 1, 1), (0, 2)), ((0, 1, 0, 1), (2, 0))


def copy_input(t, a):
    def copy(pool, b):
        pool.tensor_copy(a["x"][:, :], t.xn[:, cols(b)]).then_inc(a["x_ready"], 1)
    return copy


def l1_attention(t):
    def prepare(t, a):
        sb, at, pj, x, banks, reads = a["sb"], a["at"], a["pj"], a["x"], a["banks"], a["reads"]
        q, k = a["qk"]
        lin, qcos, qsin = sb("lin", [128, S]), sb("qcos", [128, S]), sb("qsin", [128, S])
        cos_ready = a["sem"]("cos_ready")

        def project(wn):
            def f(pe, b, j, to):
                wait_turn(pe, a["x_ready"], lambda b: b + 1, b, j)
                return pe.matmul(to, at(wn), x[:, :], start=True, stop=True)
            return f

        def rotate(pe, b, j, to):
            banks.wait_read(pe, "q", b, j)
            return pe.matmul(to, at("rot"), lin[:, :], start=True, stop=True)

        def act_q(act, b, j):
            banks.wait_filled(act, "q", b, j)
            wait_turn(act, a["final"][0], lambda b: b, b, j)
            act.activation(lin[:, :], pj[:, banks.bank("q", b), :], ACT.Identity, bias=at("bq")).then_inc(reads["act"], 1)

        def act_k(act, b, j):
            banks.wait_filled(act, "k", b, j)
            wait_turn(act, a["split"][1], lambda b: 4 * b, b, j)
            act.activation(k[:, 0, :], pj[:, banks.bank("k", b), :], ACT.Identity, bias=at("bk")).then_inc(reads["act"], 1)
            banks.wait_read(act, "k", b, j)
            act.sem_inc(a["final"][1], 1)

        def dve_rot(dve, b, j):
            banks.wait_read(dve, "q", b, j)
            dve.tensor_tensor(qcos[:, :], lin[:, :], at("cos"), ALU.mult).then_inc(cos_ready, 1)
            banks.wait_filled(dve, "rot", b, j)
            dve.tensor_tensor(qsin[:, :], pj[:, banks.bank("rot", b), :], at("sin"), ALU.mult).then_inc(reads["dve"], 1)
            banks.wait_read(dve, "rot", b, j)
            wait_turn(dve, cos_ready, lambda b: b + 1, b, j)
            wait_turn(dve, a["split"][0], lambda b: 4 * b, b, j)
            dve.tensor_tensor(q[:, 0, :], qcos[:, :], qsin[:, :], ALU.add).then_inc(a["final"][0], 1)

        return {"input": copy_input(t, a), "pe": {"q": project("wq"), "k": project("wk"), "rot": rotate},
                "act": {"q": act_q, "k": act_k}, "dve": {"rot": dve_rot}}
    attention(t, "l1a", prepare, [(1, "q", "act"), (2, "k", "act"), (4, "rot", "dve")], STACK16, "sel16",
              plus_input=True)


def l2_attention(t):
    def prepare(t, a):
        sb, at, pj, x, banks, reads = a["sb"], a["at"], a["pj"], a["x"], a["banks"], a["reads"]
        final, split = a["final"], a["split"]
        lin = [sb("q_lin", [128, 2, S]), sb("k_lin", [128, 2, S])]
        sq = [sb("q_sq", [128, 2, S]), sb("k_sq", [128, 2, S])]
        q_scaled = sb("q_scaled", [128, 2, S])
        q_scale, minus_ps = sb("q_scale", [128, 2]), sb("minus_ps", [128, 2])
        normed, copied, idle = sb("normed", [128, S]), a["sem"]("copied"), a["sem"]("idle_input")
        squared, scaled, constants = a["sem"]("squared"), a["sem"]("scaled"), a["sem"]("constants")

        def input_scaled(pool, b):
            pool.tensor_copy(normed[:, :], t.xn[:, cols(b)]).then_inc(copied, 1)
            pool.wait_ge(copied, b + 1)
            pool.sem_inc(idle, 1)
            pool.tensor_scalar(x[:, :], normed[:, :], at("ln_g"), at("ln_b"), ALU.mult, ALU.add)\
                .then_inc(a["x_ready"], 1)

        def setup(dve):
            for g in range(2):
                dve.scalar_tensor_tensor(q_scale[:, g:g + 1], at("ps")[:, g:g + 1], at("two_on_points"), at("rest"),
                                         ALU.mult, ALU.add).then_inc(constants, 1)
            dve.tensor_scalar(minus_ps[:, :], at("ps"), -1.0, None, ALU.mult).then_inc(constants, 1)
            dve.wait_ge(constants, 3)

        pe_uses, act_uses, dve_uses = {}, {}, {}
        for g in range(2):
            for s, n in enumerate("qk"):
                def project(pe, b, j, to, n=n, g=g):
                    wait_turn(pe, a["x_ready"], lambda b: b + 1, b, j)
                    return pe.matmul(to, at("w" + n)[:, 128 * g:128 * g + 128], x[:, :], start=True, stop=True)

                def linear(act, b, j, n=n, s=s, g=g):
                    use = f"{n}{g}"
                    banks.wait_filled(act, use, b, j)
                    wait_turn(act, final[s], lambda b: 2 * b, b, j)
                    act.activation(lin[s][:, g, :], pj[:, banks.bank(use, b), :], ACT.Identity,
                                   bias=at("b" + n)[:, g:g + 1]).then_inc(reads["act"], 1)
                    banks.wait_read(act, use, b, j)
                    act.activation(sq[s][:, g, :], lin[s][:, g, :], ACT.Square).then_inc(squared, 1)

                def norms(pe, b, j, to, n=n, s=s, g=g):
                    wait_turn(pe, squared, lambda b: 4 * b + 2 * g + s + 1, b, j)
                    return pe.matmul(to, at("sum_" + n), sq[s][:, g, :], start=True, stop=True)

                def combine(dve, b, j, n=n, s=s, g=g):
                    use = f"{n}sum{g}"
                    other = lin[1]
                    banks.wait_read(dve, f"{n}{g}", b, j)
                    if s == 0:
                        other = q_scaled
                        dve.tensor_scalar(q_scaled[:, g, :], lin[0][:, g, :], q_scale[:, g:g + 1], None, ALU.mult)\
                           .then_inc(scaled, 1)
                        wait_turn(dve, scaled, lambda b: 2 * b + g + 1, b, j)
                    banks.wait_filled(dve, use, b, j)
                    wait_turn(dve, split[s], lambda b: 4 * (2 * b - 1 + g), b, j)
                    dve.scalar_tensor_tensor(a["qk"][s][:, g, :], pj[:, banks.bank(use, b), :], minus_ps[:, g:g + 1],
                                             other[:, g, :], ALU.mult, ALU.add).then_inc(reads["dve"], 1)
                    banks.wait_read(dve, use, b, j)
                    dve.sem_inc(final[s], 1)
                pe_uses[f"{n}{g}"], pe_uses[f"{n}sum{g}"] = project, norms
                act_uses[f"{n}{g}"], dve_uses[f"{n}sum{g}"] = linear, combine
        return {"input": input_scaled, "pe": pe_uses, "act": act_uses, "dve": dve_uses, "setup": setup}
    preps = [(0, "q0", "act"), (1, "k0", "act"), (2, "q1", "act"), (3, "k1", "act"),
             (4, "qsum0", "dve"), (6, "ksum0", "dve"), (8, "qsum1", "dve"), (10, "ksum1", "dve")]
    attention(t, "l2a", prepare, preps, STACK32, "sel32", n_tiles=2, scale=1.0)


def l3_attention(t):
    def prepare(t, a):
        sb, at, pj, x, banks, reads = a["sb"], a["at"], a["pj"], a["x"], a["banks"], a["reads"]
        final, split = a["final"], a["split"]
        centred_w = [sb("q_centred_w", [128, 128]), sb("k_centred_w", [128, 128])]
        cen = [sb("q_cen", [128, S]), sb("k_cen", [128, S])]
        sq = [sb("q_sq", [128, S]), sb("k_sq", [128, S])]
        std = [sb("q_std", [128, S]), sb("k_std", [128, S])]
        rstd, unit = sb("rstd", [128, S]), sb("unit", [128, S])
        squared = [a["sem"]("q_squared"), a["sem"]("k_squared")]
        rstd_ready, unit_ready = a["sem"]("rstd_ready"), a["sem"]("unit_ready")
        pe_uses, act_uses, dve_uses = {}, {}, {}
        for s, n in enumerate("qk"):
            def centre_w(pe, b, j, to, n=n):
                return pe.matmul(to[:, 0:128], at("w" + n), at("head_centre"), start=True, stop=True)

            def project(pe, b, j, to, n=n, s=s):
                wait_turn(pe, a["x_ready"], lambda b: b + 1, b, j)
                banks.wait_read(pe, n + "w", 0, 0)
                return pe.matmul(to, centred_w[s][:, :], x[:, :], start=True, stop=True)

            def variance(pe, b, j, to, s=s):
                wait_turn(pe, squared[s], lambda b: b + 1, b, j)
                return pe.matmul(to, at("head_mean"), sq[s][:, :], start=True, stop=True)

            def copy_w(act, b, j, n=n, s=s):
                banks.wait_filled(act, n + "w", b, j)
                act.activation(centred_w[s][:, :], pj[:, banks.bank(n + "w", b), 0:128], ACT.Copy).then_inc(reads["act"], 1)

            def centred(act, b, j, n=n, s=s):
                banks.wait_filled(act, n, b, j)
                wait_turn(act, unit_ready, lambda b: 2 * b - 1 + s, b, j)
                act.activation(cen[s][:, :], pj[:, banks.bank(n, b), :], ACT.Copy).then_inc(reads["act"], 1)
                banks.wait_read(act, n, b, j)
                act.activation(sq[s][:, :], cen[s][:, :], ACT.Square).then_inc(squared[s], 1)

            def root(act, b, j, n=n, s=s):
                banks.wait_filled(act, n + "var", b, j)
                wait_turn(act, rstd_ready, lambda b: 2 * b - 1 + s, b, j)
                act.activation(std[s][:, :], pj[:, banks.bank(n + "var", b), :], ACT.Sqrt, bias=t.eps[:, 0:1])\
                   .then_inc(reads["act"], 1)

            def normalise(dve, b, j, n=n, s=s):
                banks.wait_read(dve, n + "var", b, j)
                wait_turn(dve, unit_ready, lambda b: 2 * b + s, b, j)
                dve.reciprocal(rstd[:, :], std[s][:, :]).then_inc(rstd_ready, 1)
                wait_turn(dve, rstd_ready, lambda b: 2 * b + s + 1, b, j)
                wait_turn(dve, final[1 - s], lambda b: b + s, b, j)
                dve.tensor_tensor(unit[:, :], cen[s][:, :], rstd[:, :], ALU.mult).then_inc(unit_ready, 1)
                wait_turn(dve, unit_ready, lambda b: 2 * b + s + 1, b, j)
                wait_turn(dve, split[s], lambda b: 4 * b, b, j)
                dve.tensor_scalar(a["qk"][s][:, 0, :], unit[:, :], at(n + "_gamma"), at(n + "_beta"), ALU.mult, ALU.add)\
                   .then_inc(final[s], 1)
            pe_uses.update({n + "w": centre_w, n: project, n + "var": variance})
            act_uses.update({n + "w": copy_w, n: centred, n + "var": root})
            dve_uses[n + "var"] = normalise
        return {"input": copy_input(t, a), "pe": pe_uses, "act": act_uses, "dve": dve_uses}
    attention(t, "l3a", prepare, [(1, "q", "act"), (2, "k", "act"), (5, "qvar", "act"), (6, "kvar", "act")],
              STACK16, "sel16", causal=True, once=("qw", "kw"))


class Chain:

    def __init__(self, eng, sem, idle=None):
        self.eng, self.sem, self.idle, self.per, self.turn, self.k = eng, sem, idle, None, 0, 0

    def start(self, turn):
        if not (isinstance(turn, int) and turn == 0) and self.per is None:
            self.per = self.k
        self.turn, self.k = turn, 0

    def value(self):
        return self.k if self.per is None else self.turn * self.per + self.k

    def then(self, ins):
        self.k += 1
        ins.then_inc(self.sem, 1)
        self.eng.wait_ge(self.sem, self.value())

    def then_alone(self, ins):
        self.then(ins)
        self.eng.sem_inc(self.idle, 1)


def route(t, ctx, name, n_exp, top):
    nc = t.nc
    E, drop = n_exp, top < 0
    rounds = (-top + 7) // 8 if drop else 1
    pads = 8 * rounds - abs(top)
    weights = t.sb(ctx, name + "_weights", [128, NT])
    parts = t.sb(ctx, name + "_parts", [128, NT], F16)
    with ExitStack() as own:
        sb = lambda n, shape, dt=F32: t.sb(own, f"{name}r_{n}", shape, dt)
        sem = lambda n: t.sem(f"{name}r_{n}")
        wr, br = sb("wr", [128, E]), sb("br", [128, E])
        x = sb("x", [128, S])
        lg, ex, e2, mask = (sb(n, [128, 4, E]) for n in ("lg", "ex", "e2", "mask"))
        prob = sb("prob", [128, 4, E])
        key = sb("key", [128, 4, E + pads])
        top8 = sb("top8", [128, 8])
        mx, sm, rs = (sb(n, [128, 4]) for n in ("mx", "sm", "rs"))
        comb = sb("comb", [128, 4, 128])
        p1 = sb("p1", [128, S], F16)
        ps_l = t.ps(own, name + "r_psl", [128, 4, E])
        ps_t = t.ps(own, name + "r_pst", [128, S])
        loaded, zeroed, x_ready, scored, shifted, exped, shifted2, exped2, comb_ready, turned, parted, chain = [
            sem(n) for n in ("loaded", "zeroed", "x_ready", "scored", "shifted", "exped", "shifted2", "exped2",
                             "comb_ready", "turned", "parted", "chain")]
        block = own.enter_context(nc.Block())
        n_loads = 2 if drop else 1

        def wide(tile):
            return tile.rearrange("p (c a) -> p c a", a=1).to_broadcast([128, 4, E])

        @block.sync
        def _(sp):
            sp.dma_start(wr[:, :], t.dram[name + "_router"]).then_inc(loaded, 16)
            if drop:
                sp.dma_start(br[:, :], t.dram[name + "_router_b"]).then_inc(loaded, 16)
            sp.wait_ge(loaded, 16 * n_loads)

        @block.gpsimd
        def _(pool):
            pool.memset(comb[:, :, :], 0.0).then_inc(zeroed, 1)

            def body(b):
                wait(pool, scored, b)
                pool.tensor_copy(x[:, :], t.xn[:, cols(b)]).then_inc(x_ready, 1)
            turns(pool, NB, body)

        @block.tensor
        def _(pe):
            pe.wait_ge(loaded, 16 * n_loads)

            def body(b):
                pe.wait_ge(x_ready, b + 1)
                wait(pe, shifted, b)
                for c in range(4):
                    last = pe.matmul(ps_l[:, c, :], x[:, 128 * c:128 * c + 128], wr[:, :], start=True, stop=True)
                last.then_inc(scored, 1)
                pe.wait_ge(comb_ready, b + 1)
                wait(pe, parted, b)
                for c in range(4):
                    last = pe.transpose(ps_t[:, 128 * c:128 * c + 128], comb[:, c, :], t.ident)
                last.then_inc(turned, 1)
            turns(pe, NB, body)

        @block.scalar
        def _(act):
            def body(b):
                act.wait_ge(shifted, b + 1)
                wait(act, comb_ready, b)
                act.activation(ex[:, :, :], lg[:, :, :], ACT.Exp).then_inc(exped, 1)
                if drop:
                    act.wait_ge(shifted2, b + 1)
                    act.activation(e2[:, :, :], prob[:, :, :], ACT.Exp).then_inc(exped2, 1)
            turns(act, NB, body)

        @block.vector
        def _(dve):
            dve.wait_ge(loaded, 16 * n_loads)
            dve.wait_ge(zeroed, 1)
            ch = Chain(dve, chain, t.sem(name + "r_idle"))

            def body(b):
                ch.start(b)
                then, then_alone = ch.then, ch.then_alone
                dve.wait_ge(scored, b + 1)
                if drop:
                    then(dve.tensor_tensor(lg[:, :, :], ps_l[:, :, :],
                                           br[:, :].rearrange("p (a e) -> p a e", a=1).to_broadcast([128, 4, E]), ALU.add))
                else:
                    then(dve.tensor_copy(lg[:, :, :], ps_l[:, :, :]))
                then(dve.tensor_reduce(mx[:, :], lg[:, :, :], AX.X, ALU.max))
                if not drop:
                    then(dve.tensor_copy(key[:, :, 0:E], lg[:, :, :]))
                then(dve.tensor_tensor(lg[:, :, :], lg[:, :, :], wide(mx[:, :]), ALU.subtract))
                dve.sem_inc(shifted, 1)
                if drop:
                    dve.wait_ge(exped, b + 1)
                    then(dve.tensor_reduce(sm[:, :], ex[:, :, :], AX.X, ALU.add))
                    then(dve.reciprocal(rs[:, :], sm[:, :]))
                    then(dve.tensor_tensor(prob[:, :, :], ex[:, :, :], wide(rs[:, :]), ALU.mult))
                    then(dve.tensor_scalar(key[:, :, 0:E], prob[:, :, :], -1.0, None, ALU.mult))
                    then(dve.tensor_tensor(prob[:, :, :], prob[:, :, :], wide(rs[:, :]), ALU.subtract))
                    dve.sem_inc(shifted2, 1)
                then_alone(dve.memset(key[:, :, E:E + pads], BIG))
                for c in range(4):
                    for _ in range(rounds):
                        then_alone(dve.max(top8[:, :], key[:, c, :]))
                        then_alone(dve.match_replace(key[:, c, :], top8[:, :], key[:, c, :], -BIG))
                then(dve.tensor_scalar(mask[:, :, :], key[:, :, 0:E], -0.5 * BIG, None, ALU.is_ge if drop else ALU.is_lt))
                dve.wait_ge(exped2 if drop else exped, b + 1)
                then(dve.tensor_tensor(mask[:, :, :], mask[:, :, :], (e2 if drop else ex)[:, :, :], ALU.mult))
                then(dve.tensor_reduce(sm[:, :], mask[:, :, :], AX.X, ALU.add))
                then(dve.reciprocal(rs[:, :], sm[:, :]))
                wait(dve, turned, b)
                then(dve.tensor_tensor(comb[:, :, 0:E], mask[:, :, :], wide(rs[:, :]), ALU.mult))
                then(dve.tensor_copy(comb[:, :, 64:64 + E], comb[:, :, 0:E]))
                dve.sem_inc(comb_ready, 1)
                dve.wait_ge(turned, b + 1)
                then(dve.tensor_copy(weights[:, cols(b)], ps_t[:, :]))
                then(dve.tensor_scalar(p1[:, :], ps_t[:, :], SCALE, None, ALU.mult))
                then(dve.scalar_tensor_tensor(parts[64:128, cols(b)], ps_t[64:128, :], SCALE, p1[64:128, :],
                                              ALU.mult, ALU.subtract))
                dve.sem_inc(parted, 1)
                then(dve.tensor_copy(parts[0:64, cols(b)], p1[0:64, :]))
            turns(dve, NB, body)
    return weights, parts


def experts(t, name, n_exp, hidden, func, top, acc_tiles, biased=False, gated=False, shared=False):
    nc, h, xn = t.nc, t.h, t.xn
    nch = hidden // 128
    passes = NB // acc_tiles
    upe = acc_tiles * nch
    upp = 2 * upe
    with ExitStack() as ctx:
        weights, parts = route(t, ctx, name, n_exp, top)
        sb = lambda n, shape, dt=F32: t.sb(ctx, f"{name}_{n}", shape, dt)
        sem = lambda n: t.sem(f"{name}_{n}")
        w1 = sb("w1", [128, 2, hidden])
        w2 = sb("w2", [128, 2, hidden])
        w3 = sb("w3", [128, 2, hidden]) if gated else None
        b1 = sb("b1", [128, n_exp * nch]) if biased else None
        b2 = sb("b2", [n_exp, D]) if biased else None
        onehot = sb("onehot", [128, 64], F16)
        acted = sb("acted", [128, 4, S])
        gate = sb("gate", [128, 2, S]) if gated else None
        prod = sb("prod", [128, 4, S])
        ps_acc = t.ps(ctx, name + "_acc", [128, acc_tiles, S])
        ps_h = t.ps(ctx, name + "_ps_h", [128, 2, S])
        ps_g = t.ps(ctx, name + "_ps_g", [128, 2, S]) if gated else None
        ps_b = t.ps(ctx, name + "_ps_b", [128, 2, S])
        loaded, cast, idle = sem("loaded"), sem("cast"), sem("idle")
        w_in = [sem("w_in0"), sem("w_in1")]
        hid, acted_ready, gate_ready, prod_ready = sem("hid"), sem("acted"), sem("gate"), sem("prod")
        spread, mixed, drained = sem("spread"), sem("mixed"), sem("drained")
        n_dma = 3 if gated else 2
        per_pass = n_exp * upe + (upe if shared else 0)
        spread_per_pass = n_exp * acc_tiles
        loads = [n_exp // 2 + (1 if shared else 0), n_exp // 2]
        block = ctx.enter_context(nc.Block())

        @block.sync
        def _(sp):
            if biased:
                sp.dma_start(b1[:, :], t.dram[name + "_b1"].rearrange("p e c -> p (e c)")).then_inc(loaded, 16)
                sp.dma_start(b2[:, :], t.dram[name + "_b2"]).then_inc(loaded, 16)

            def load(e, slot, used):
                wait(sp, mixed, used)
                e = bass.ds(e, 1)
                sp.dma_start(w1[:, slot, :], t.dram[name + "_w1"][e, :, :].rearrange("a p n -> p (a n)"))\
                  .then_inc(w_in[slot], 16)
                sp.dma_start(w2[:, slot, :], t.dram[name + "_w2"][e, :, :, :].rearrange("a p c n -> p (a c n)"))\
                  .then_inc(w_in[slot], 16)
                if gated:
                    sp.dma_start(w3[:, slot, :], t.dram[name + "_w3"][e, :, :].rearrange("a p n -> p (a n)"))\
                      .then_inc(w_in[slot], 16)

            for p in range(passes):
                def pair(j):
                    for s in range(2):
                        first = isinstance(j, int) and j == 0
                        if first:
                            used = per_pass * p - ((1 - s) * upe if not shared else s * 0)
                            if shared and s == 1:
                                used = per_pass * p - upe
                        else:
                            used = per_pass * p + upp * j - (1 - s) * upe
                        load(2 * j + s, s, used)
                turns(sp, n_exp // 2, pair)
                if shared:
                    sp.wait_ge(mixed, per_pass * p + n_exp * upe - upe)
                    sp.dma_start(w1[:, 0, :], t.dram[name + "_sw1"]).then_inc(w_in[0], 16)
                    sp.dma_start(w2[:, 0, :], t.dram[name + "_sw2"].rearrange("p c n -> p (c n)"))\
                      .then_inc(w_in[0], 16)

        w_per_pass = [16 * n_dma * (n_exp // 2) + (32 if shared else 0), 16 * n_dma * (n_exp // 2)]

        def units():
            return [(c, k) for c in range(acc_tiles) for k in range(nch)]

        @block.tensor
        def _(pe):
            pe.wait_ge(cast, 2)
            if biased:
                pe.wait_ge(loaded, 32)

            def mix(n, u, slot, first):
                c, k = units()[u % upe]
                pe.wait_ge(prod_ready, n + 1)
                pe.matmul(ps_acc[:, c, :], w2[:, slot, 128 * k:128 * k + 128], prod[:, u % 4, :],
                          start=(first and k == 0 and not biased), stop=False, skip_group_check=True)\
                  .then_inc(mixed, 1)

            def expert(p, n0, e, slot, spreads, in_loads, late, is_shared=False, before=None):
                pe.wait_ge(w_in[slot], in_loads)
                for u, (c, k) in enumerate(units()):
                    tile = acc_tiles * p + c
                    if k == 0 and not is_shared:
                        m = spreads + c
                        if not (isinstance(m, int) and m < 2):
                            pe.wait_ge(prod_ready, before(c - 2))
                        oh = onehot[:, bass.ds(e, 1)].to_broadcast([128, 128])
                        pe.matmul(ps_b[:, c % 2, :], oh, parts[:, S * tile:S * tile + S], start=True, stop=True)\
                          .then_inc(spread, 1)
                    n = n0 + u
                    if not (isinstance(n, int) and n < 2):
                        pe.wait_ge(acted_ready, n - 1)
                        if gated:
                            pe.wait_ge(prod_ready, n - 1)
                    x = xn[:, S * tile:S * tile + S]
                    last = pe.matmul(ps_h[:, u % 2, :], w1[:, slot, 128 * k:128 * k + 128], x, start=True, stop=True)
                    if gated and not is_shared:
                        last = pe.matmul(ps_g[:, u % 2, :], w3[:, slot, 128 * k:128 * k + 128], x, start=True, stop=True)
                    last.then_inc(hid, 1)
                    if u < 2:
                        if late is not None:
                            mix(n - 2, upe - 2 + u, late[0], late[1])
                    else:
                        mix(n - 2, u - 2, slot, isinstance(e, int) and e == 0 and not is_shared)

            for p in range(passes):
                wait(pe, drained, acc_tiles * p)
                if biased:
                    for c in range(acc_tiles):
                        tile = acc_tiles * p + c
                        pe.matmul(ps_acc[:, c, :], b2[:, :], weights[0:n_exp, S * tile:S * tile + S],
                                  start=True, stop=False, skip_group_check=True)

                def pair(j):
                    for s in range(2):
                        n0 = per_pass * p + upp * j + upe * s
                        first = isinstance(j, int) and j == 0
                        if first and s == 0:
                            late = None
                        else:
                            late = (1 - s, first and s == 1)
                        m = spread_per_pass * p + acc_tiles * (2 * j + s)

                        def before(c, n0=n0, first=first, s=s):
                            if c < 0 and first and s == 0 and shared:
                                return n0 - upe + nch * (c + 1)
                            return n0 + nch * (c + 1)
                        expert(p, n0, 2 * j + s, s, m, w_per_pass[s] * p + 16 * n_dma * (j + 1), late, before=before)
                turns(pe, n_exp // 2, pair)
                n_end = per_pass * p + n_exp * upe
                if shared:
                    expert(p, n_end, 0, 0, 0, w_per_pass[0] * (p + 1), (1, False), is_shared=True)
                    n_end += upe
                for i in (2, 1):
                    mix(n_end - i, upe - i, 0 if shared else 1, False)

        @block.scalar
        def _(act):
            if biased:
                act.wait_ge(loaded, 32)

            def expert(n0, e, f):
                for u, (c, k) in enumerate(units()):
                    n = n0 + u
                    act.wait_ge(hid, n + 1)
                    if not (isinstance(n, int) and n < 4):
                        act.wait_ge(prod_ready, n - 3)
                    if biased:
                        act.sem_inc(idle, 1)
                    kw = {"bias": b1[:, bass.ds(e * nch + k, 1)]} if biased else {}
                    act.activation(acted[:, u % 4, :], ps_h[:, u % 2, :], f, **kw).then_inc(acted_ready, 1)
            for p in range(passes):
                def pair(j):
                    for s in range(2):
                        expert(per_pass * p + upp * j + upe * s, 2 * j + s, func)
                turns(act, n_exp // 2, pair)
                if shared:
                    expert(per_pass * p + n_exp * upe, 0, ACT.Gelu)

        @block.vector
        def _(dve):
            for r in (0, 64):
                dve.tensor_scalar(onehot[r:r + 64, :], t.ident[r:r + 64, r:r + 64], 1.0 / SCALE, None, ALU.mult)\
                   .then_inc(cast, 1)

            def expert(n0, m0, g0):
                for u, (c, k) in enumerate(units()):
                    n = n0 + u
                    dve.wait_ge(acted_ready, n + 1)
                    src = acted[:, u % 4, :]
                    if gated:
                        dve.wait_ge(hid, n + 1)
                        if not (isinstance(n, int) and n < 2):
                            dve.wait_ge(prod_ready, n - 1)
                        dve.tensor_tensor(gate[:, u % 2, :], acted[:, u % 4, :], ps_g[:, u % 2, :], ALU.mult)\
                           .then_inc(gate_ready, 1)
                        dve.wait_ge(gate_ready, g0 + u + 1)
                        src = gate[:, u % 2, :]
                    if k == 0:
                        dve.wait_ge(spread, m0 + c + 1)
                    if not (isinstance(n, int) and n < 4):
                        dve.wait_ge(mixed, n - 3)
                    dve.tensor_tensor(prod[:, u % 4, :], src, ps_b[:, c % 2, :], ALU.mult).then_inc(prod_ready, 1)
            for p in range(passes):
                def pair(j):
                    for s in range(2):
                        expert(per_pass * p + upp * j + upe * s, spread_per_pass * p + acc_tiles * (2 * j + s),
                               n_exp * upe * p + upp * j + upe * s)
                turns(dve, n_exp // 2, pair)
                if shared:
                    for u in range(upe):
                        n = per_pass * p + n_exp * upe + u
                        dve.wait_ge(acted_ready, n + 1)
                        dve.wait_ge(mixed, n - 3)
                        dve.tensor_copy(prod[:, u % 4, :], acted[:, u % 4, :]).then_inc(prod_ready, 1)
                dve.wait_ge(mixed, per_pass * (p + 1))
                for c in range(acc_tiles):
                    tile = acc_tiles * p + c
                    dve.tensor_tensor(h[:, S * tile:S * tile + S], h[:, S * tile:S * tile + S], ps_acc[:, c, :], ALU.add)\
                       .then_inc(drained, 1)


def l1_experts(t):
    experts(t, "l1f", 64, 256, ACT.Gelu, -22, 4, biased=True)


def l2_experts(t):
    experts(t, "l2f", 8, 512, ACT.Silu, 1, 2, gated=True, shared=True)


def l3_experts(t):
    experts(t, "l3f", 8, 512, ACT.Relu, 2, 4, biased=True)


TOP = 16
RECTS = ((0, 1, 16), (1, 1, 8), (2, 2, 5), (4, 4, 3), (8, 8, 1))
CAND = sum(ra * rb for _, ra, rb in RECTS)
HEADS, KEYS = 8, 64
CCH = 4
CP = HEADS * CAND // CCH
MAJ, MIN = 16, 8


def product_key_ffn(t):
    nc, h, xn = t.nc, t.h, t.xn
    NG = 128 // 8
    with ExitStack() as ctx:
        sb = lambda n, shape, dt=F32: t.sb(ctx, "l0f_" + n, shape, dt)
        sem = lambda n: t.sem("l0f_" + n)
        w = sb("w", [128, t.where["l0f"]["_width"]])
        at = lambda n: t.at(w, "l0f", n)
        wq = sb("wq", [128, 4, 128])
        bq = sb("bq", [128, 4])
        keys, keys_sq, keys_norm = sb("keys", [128, 256]), sb("keys_sq", [128, 256]), sb("keys_norm", [128, 256])
        cen, sq, std, y1, y, sq2 = (sb(n, [128, 4, 128]) for n in ("cen", "sq", "std", "y1", "y", "sq2"))
        std_t, norm_t, rnorm_t = sb("std_t", [128, 8]), sb("norm_t", [128, 8, 2]), sb("rnorm_t", [128, 16])
        s, rep = sb("s", [128, 16, KEYS]), sb("rep", [128, 16, KEYS])
        v, vi = sb("v", [128, HEADS, 2, TOP]), sb("vi", [128, HEADS, 2, TOP], U32)
        cand, c2, c3 = (sb(n, [128, HEADS, CAND]) for n in ("cand", "c2", "c3"))
        ci, cm = sb("ci", [128, HEADS, CAND], U32), sb("cm", [128, 2, HEADS, CAND], U32)
        majmin = sb("majmin", [128, 2, HEADS * CAND], BF16)
        m1, m2 = sb("m1", [128, HEADS, 8]), sb("m2", [128, HEADS, 8])
        shifted, ex, wt = (sb(n, [128, HEADS, CAND]) for n in ("shifted", "ex", "wt"))
        zsum, rz = sb("zsum", [128, HEADS]), sb("rz", [128, HEADS])
        mm_t = sb("mm_t", [CP, 2, CCH, 128], F16)
        p1, p2 = (sb(n, [CP, CCH, 128], F16) for n in ("p1", "p2"))
        r1 = sb("r1", [CP, CCH, 128])
        hot_maj = sb("hot_maj", [CP, CCH * NG, MAJ, 8], F16)
        hot_min = sb("hot_min", [CP, CCH, MIN, 128], F16)
        hw = [sb(f"hw{p}", [CP, CCH, MIN, 128], F16) for p in range(2)]
        diag = sb("diag", [128, NG, MIN, 8])
        g, z = sb("g", [128, 128]), sb("z", [128, 128])
        ps_q = t.ps(ctx, "l0f_psq", [128, 4, 128])
        ps_s = t.ps(ctx, "l0f_pss", [128, 16, KEYS])
        ps_m = t.ps(ctx, "l0f_psm", [128, 4, 128])
        ps_w = t.ps(ctx, "l0f_psw", [CP, CCH, 128])
        ps_i = t.ps(ctx, "l0f_psi", [CP, 2, CCH, 128], BF16)
        ps_d = t.ps(ctx, "l0f_psd", [128, NG, MIN, 8])
        identb = sb("identb", [128, 128], BF16)
        names = ("loaded consts setup_mm setup_act ch_set q_mm cen sq var_mm std y1 y sq2 score_mm norm_act s_ready "
                 "vi_ready ci_ready cm_ready majmin shifted ex wt w_turned p1 r1 p2 mm_t hot_min hw0 group_mm "
                 "diag a_mm g_mm g_act z out_mm h_ready idle ch_top hots k_sq k_std").split()
        q = {n: sem(n) for n in names}
        block = ctx.enter_context(nc.Block())

        def tok(T):
            return bass.ds(T * 128, 128)

        def later(T, k=0):
            return not (isinstance(T, int) and T <= k)

        @block.sync
        def _(sp):
            sp.dma_start(w[:, :], t.dram["l0f"]).then_inc(q["loaded"], 16)
            sp.wait_ge(q["loaded"], 16)

        @block.gpsimd
        def _(pool):
            pool.tensor_copy(identb[:, :], t.ident).then_inc(q["consts"], 1)

            def front(T):
                pool.wait_ge(q["vi_ready"], T + 1)
                if later(T):
                    pool.wait_ge(q["cm_ready"], T)
                off = 0
                for a0, ra, rb in RECTS:
                    last = pool.tensor_tensor(
                        ci[:, :, off:off + ra * rb].rearrange("p h (a b) -> p h a b", b=rb),
                        vi[:, :, 0, a0:a0 + ra].rearrange("p h (a o) -> p h a o", o=1).to_broadcast([128, HEADS, ra, rb]),
                        vi[:, :, 1, 0:rb].rearrange("p h (o b) -> p h o b", o=1).to_broadcast([128, HEADS, ra, rb]), ALU.add)
                    off += ra * rb
                last.then_inc(q["ci_ready"], 1)

            def back(T):
                pool.wait_ge(q["p2"], T + 1)
                pool.wait_ge(q["hot_min"], T + 1)
                if later(T):
                    pool.wait_ge(q["group_mm"], T)
                for m in range(MIN):
                    last = pool.tensor_tensor(hw[1][:, :, m, :], hot_min[:, :, m, :], p2[:, :, :], ALU.mult)
                last.then_inc(q["hw0"], 1)
            front(0)
            back(0)
            front(1)
            with pool.Fori(2, NTT) as T:
                back(T - 1)
                front(T)
            back(NTT - 1)

        @block.tensor
        def _(pe):
            pe.wait_ge(q["loaded"], 16)
            for c in range(4):
                pe.matmul(ps_q[:, c, :], at("wq")[:, 128 * c:128 * c + 128], at("head_centre"), start=True, stop=True)
            pe.matmul(ps_m[:, 0, 0:4], at("head_centre"), at("bq"), start=True, stop=True).then_inc(q["setup_mm"], 1)
            pe.wait_ge(q["k_sq"], 1)
            pe.matmul(ps_s[:, 0:4, :], at("ones"), keys_sq[:, :], start=True, stop=True).then_inc(q["setup_mm"], 1)
            pe.wait_ge(q["ch_set"], 6)
            pe.wait_ge(q["consts"], 1)

            def project(T):
                if later(T):
                    pe.wait_ge(q["norm_act"], 2 * T)
                for c in range(4):
                    last = pe.matmul(ps_q[:, c, :], wq[:, c, :], xn[:, tok(T)], start=True, stop=True)
                last.then_inc(q["q_mm"], 1)

            def variance(T):
                pe.wait_ge(q["sq"], T + 1)
                pe.matmul(ps_q[:, :, :], at("head_mean"), sq[:, :, :], start=True, stop=True).then_inc(q["var_mm"], 1)

            def scores(T):
                pe.wait_ge(q["sq2"], T + 1)
                if later(T):
                    pe.wait_ge(q["s_ready"], T)
                for c in range(4):
                    pe.matmul(ps_q[:, 0, 16 + 2 * c:18 + 2 * c], sq[:, c, :], at("head_mean")[:, 0:128:64],
                              start=True, stop=True)
                    pe.matmul(ps_q[:, 0, 4 * c:4 * c + 4], sq2[:, c, :], at("quarter")[:, 0:128:32], start=True, stop=True)
                for c in range(4):
                    last = pe.matmul(ps_s[:, 4 * c:4 * c + 4, :], y[:, c, :], keys[:, :], start=True, stop=True)
                last.then_inc(q["score_mm"], 1)

            def turn(T):
                pe.wait_ge(q["wt"], T + 1)
                if later(T):
                    pe.wait_ge(q["r1"], T)
                    pe.wait_ge(q["mm_t"], T)
                wf = wt[:, :, :].rearrange("p h c -> p (h c)")
                for c in range(CCH):
                    pe.transpose(ps_w[:, c, :], wf[:, CP * c:CP * c + CP], t.ident)
                pe.wait_ge(q["majmin"], 2 * T + 2)
                for k in range(2):
                    for c in range(CCH):
                        last = pe.transpose(ps_i[:, k, c, :], majmin[:, k, CP * c:CP * c + CP], identb[:, :])
                last.then_inc(q["w_turned"], 1)

            def groups(T):
                pe.wait_ge(q["hots"], T + 1)
                pe.wait_ge(q["hw0"], T + 1)
                if later(T):
                    pe.wait_ge(q["diag"], T)
                for k in range(NG):
                    n = 0
                    for c in range(CCH):
                        for p in range(2):
                            last = pe.matmul(ps_d[:, k, :, :], hot_maj[:, NG * c + k, :, :].rearrange("p m t -> p (m t)"),
                                             hw[p][:, c, :, 8 * k:8 * k + 8], start=(n == 0), stop=(n == 2 * CCH - 1))
                            n += 1
                last.then_inc(q["group_mm"], 1)
                if later(T):
                    pe.wait_ge(q["h_ready"], T)
                pe.matmul(ps_m[:, 2, :], at("down"), xn[:, tok(T)], start=True, stop=True).then_inc(q["g_mm"], 1)

            def output(T):
                pe.wait_ge(q["diag"], T + 1)
                pe.wait_ge(q["g_act"], T + 1)
                for m in range(MIN):
                    last = pe.matmul(ps_m[:, 1, :], at("place")[:, 128 * m:128 * m + 128], diag[:, :, m, :],
                                     start=(m == 0), stop=(m == MIN - 1))
                last.then_inc(q["a_mm"], 1)
                pe.wait_ge(q["z"], T + 1)
                pe.matmul(ps_m[:, 3, :], at("up"), z[:, :], start=True, stop=True).then_inc(q["out_mm"], 1)

            def tile(T):
                if later(T):
                    turn(T - 1)
                if not isinstance(T, int) or T + 1 < NTT:
                    variance(T + 1)
                if later(T):
                    groups(T - 1)
                if not isinstance(T, int) or T + 1 < NTT:
                    scores(T + 1)
                if not isinstance(T, int) or T + 2 < NTT:
                    project(T + 2)
                if later(T):
                    output(T - 1)
            project(0)
            variance(0)
            scores(0)
            project(1)
            tile(0)
            tile(1)
            with pe.Fori(2, NTT - 2) as T:
                tile(T)
            tile(NTT - 2)
            tile(NTT - 1)
            turn(NTT - 1)
            groups(NTT - 1)
            output(NTT - 1)

        @block.scalar
        def _(act):
            act.wait_ge(q["loaded"], 16)
            act.activation(keys_sq[:, :], at("keys"), ACT.Square).then_inc(q["k_sq"], 1)
            act.wait_ge(q["setup_mm"], 2)
            act.activation(keys_norm[:, :], ps_s[:, 0:4, :].rearrange("p a b -> p (a b)"), ACT.Sqrt).then_inc(q["k_std"], 1)

            def squares(T):
                act.wait_ge(q["cen"], T + 1)
                if later(T):
                    act.wait_ge(q["score_mm"], T)
                act.activation(sq[:, :, :], cen[:, :, :], ACT.Square).then_inc(q["sq"], 1)
                if later(T):
                    act.wait_ge(q["y"], T)
                act.activation(y1[:, :, :], cen[:, :, :], ACT.Copy, scale=at("ln_g")).then_inc(q["y1"], 1)

            def root(T):
                act.wait_ge(q["var_mm"], T + 1)
                act.activation(std[:, :, :], ps_q[:, :, :], ACT.Sqrt, bias=t.eps[:, 0:1]).then_inc(q["std"], 1)

            def norms(T):
                act.wait_ge(q["y"], T + 1)
                act.activation(sq2[:, :, :], y[:, :, :], ACT.Square).then_inc(q["sq2"], 1)
                act.wait_ge(q["score_mm"], T + 1)
                if later(T):
                    act.wait_ge(q["s_ready"], T)
                act.activation(norm_t[:, :, :].rearrange("p h k -> p (h k)"), ps_q[:, 0, 0:16], ACT.Sqrt)\
                   .then_inc(q["norm_act"], 1)
                act.activation(std_t[:, :], ps_q[:, 0, 16:24], ACT.Sqrt, bias=t.eps[:, 0:1]).then_inc(q["norm_act"], 1)

            def chosen(T):
                act.wait_ge(q["shifted"], T + 1)
                if later(T):
                    act.wait_ge(q["wt"], T)
                act.activation(ex[:, :, :], shifted[:, :, :], ACT.Exp).then_inc(q["ex"], 1)
                act.wait_ge(q["cm_ready"], T + 1)
                if later(T):
                    act.wait_ge(q["w_turned"], T)
                for k in range(2):
                    act.activation(majmin[:, k, :], cm[:, k, :, :].rearrange("p h c -> p (h c)"), ACT.Copy)\
                       .then_inc(q["majmin"], 1)

            def first_part(T):
                act.wait_ge(q["w_turned"], T + 1)
                if later(T):
                    act.wait_ge(q["hots"], T)
                act.activation(p1[:, :, :], ps_w[:, :, :], ACT.Copy).then_inc(q["p1"], 1)
                act.activation(mm_t[:, :, :, :], ps_i[:, :, :, :], ACT.Copy).then_inc(q["mm_t"], 1)

            def second_part(T):
                act.wait_ge(q["r1"], T + 1)
                if later(T):
                    act.wait_ge(q["hw0"], T)
                act.activation(p2[:, :, :], r1[:, :, :], ACT.Copy).then_inc(q["p2"], 1)

            def inner(T):
                act.wait_ge(q["g_mm"], T + 1)
                if later(T):
                    act.wait_ge(q["z"], T)
                act.activation(g[:, :], ps_m[:, 2, :], ACT.Gelu).then_inc(q["g_act"], 1)

            def tile(T):
                ahead = not isinstance(T, int) or T + 1 < NTT
                if ahead:
                    squares(T + 1)
                if later(T):
                    first_part(T - 1)
                if ahead:
                    root(T + 1)
                if later(T):
                    second_part(T - 1)
                if ahead:
                    norms(T + 1)
                if later(T):
                    inner(T - 1)
                chosen(T)
            squares(0)
            root(0)
            norms(0)
            tile(0)
            tile(1)
            with act.Fori(2, NTT - 1) as T:
                tile(T)
            tile(NTT - 1)
            first_part(NTT - 1)
            second_part(NTT - 1)
            inner(NTT - 1)

        @block.vector
        def _(dve):
            dve.wait_ge(q["loaded"], 16)
            dve.wait_ge(q["setup_mm"], 2)
            k = [0]

            def once(ins):
                k[0] += 1
                ins.then_inc(q["ch_set"], 1)
                dve.wait_ge(q["ch_set"], k[0])
            once(dve.tensor_copy(wq[:, :, :], ps_q[:, :, :]))
            once(dve.tensor_copy(bq[:, :], ps_m[:, 0, 0:4]))
            dve.wait_ge(q["k_std"], 1)
            once(dve.tensor_scalar(keys_norm[:, :], keys_norm[:, :], 1e-12, None, ALU.max))
            once(dve.reciprocal(keys_sq[:, :], keys_norm[:, :]))
            once(dve.tensor_tensor(keys[:, :], at("keys"), keys_sq[:, :], ALU.mult))
            once(dve.tensor_copy(z[:, 0:8], wq[:, 0, 0:8]))
            dve.wait_ge(q["consts"], 1)
            top = Chain(dve, q["ch_top"], q["idle"])

            def centre(T):
                dve.wait_ge(q["q_mm"], T + 1)
                if later(T):
                    dve.wait_ge(q["y1"], T)
                dve.tensor_tensor(cen[:, :, :], ps_q[:, :, :],
                                  bq[:, :].rearrange("p (c o) -> p c o", o=1).to_broadcast([128, 4, 128]), ALU.add)\
                   .then_inc(q["cen"], 1)

            def scaled(T):
                dve.wait_ge(q["std"], T + 1)
                dve.wait_ge(q["y1"], T + 1)
                if later(T):
                    dve.wait_ge(q["score_mm"], T)
                dve.scalar_tensor_tensor(y[:, :, :], std[:, :, :], at("ln_b"), y1[:, :, :], ALU.mult, ALU.add)\
                   .then_inc(q["y"], 1)

            def middle(T, with_front=True, backs=True):
                top.start(T)
                then, alone = top.then, top.then_alone
                if with_front:
                    centre(T + 1)
                dve.wait_ge(q["norm_act"], 2 * T + 2)
                then(dve.scalar_tensor_tensor(norm_t[:, :, :],
                                              std_t[:, :].rearrange("p (h o) -> p h o", o=1).to_broadcast([128, 8, 2]),
                                              1e-12, norm_t[:, :, :], ALU.mult, ALU.max))
                then(dve.reciprocal(rnorm_t[:, :], norm_t[:, :, :].rearrange("p h k -> p (h k)")))
                dve.wait_ge(q["score_mm"], T + 1)
                then(dve.tensor_tensor(s[:, :, :], ps_s[:, :, :],
                                       rnorm_t[:, :].rearrange("p (r o) -> p r o", o=1).to_broadcast([128, 16, KEYS]),
                                       ALU.mult))
                dve.sem_inc(q["s_ready"], 1)
                halves = [(r // 2, r % 2, r) for r in range(16)]
                for hd, k, r in halves:
                    last = dve.max(v[:, hd, k, 0:8], s[:, r, :])
                alone(last)
                for hd, k, r in halves:
                    last = dve.match_replace(rep[:, r, :], v[:, hd, k, 0:8], s[:, r, :], -BIG)
                alone(last)
                if backs:
                    one_hots(T - 1)
                if with_front:
                    scaled(T + 1)
                for hd, k, r in halves:
                    last = dve.max(v[:, hd, k, 8:16], rep[:, r, :])
                alone(last)
                if later(T):
                    dve.wait_ge(q["ci_ready"], T)
                    dve.sem_inc(q["idle"], 1)
                for hd, k, r in halves:
                    dve.max_index(vi[:, hd, k, 0:8], v[:, hd, k, 0:8], s[:, r, :])
                    last = dve.max_index(vi[:, hd, k, 8:16], v[:, hd, k, 8:16], rep[:, r, :])
                last.then_inc(q["vi_ready"], 1)
                off = 0
                for a0, ra, rb in RECTS:
                    last = dve.tensor_tensor(
                        cand[:, :, off:off + ra * rb].rearrange("p h (a b) -> p h a b", b=rb),
                        v[:, :, 0, a0:a0 + ra].rearrange("p h (a o) -> p h a o", o=1).to_broadcast([128, HEADS, ra, rb]),
                        v[:, :, 1, 0:rb].rearrange("p h (o b) -> p h o b", o=1).to_broadcast([128, HEADS, ra, rb]), ALU.add)
                    off += ra * rb
                alone(last)
                for hd in range(HEADS):
                    last = dve.max(m1[:, hd, :], cand[:, hd, :])
                alone(last)
                for hd in range(HEADS):
                    last = dve.match_replace(c2[:, hd, :], m1[:, hd, :], cand[:, hd, :], -BIG)
                alone(last)
                for hd in range(HEADS):
                    last = dve.max(m2[:, hd, :], c2[:, hd, :])
                alone(last)
                for hd in range(HEADS):
                    last = dve.match_replace(c3[:, hd, :], m2[:, hd, :], c2[:, hd, :], -BIG)
                then(last)
                then(dve.tensor_tensor(shifted[:, :, :], cand[:, :, :],
                                       m1[:, :, 0:1].to_broadcast([128, HEADS, CAND]), ALU.subtract))
                dve.sem_inc(q["shifted"], 1)
                dve.wait_ge(q["ci_ready"], T + 1)
                if later(T):
                    dve.wait_ge(q["majmin"], 2 * T)
                dve.tensor_scalar(cm[:, 0, :, :], ci[:, :, :], 3, None, ALU.logical_shift_right)
                dve.tensor_scalar(cm[:, 1, :, :], ci[:, :, :], 7, None, ALU.bitwise_and).then_inc(q["cm_ready"], 1)
                if backs:
                    diagonals(T - 1)
                dve.wait_ge(q["ex"], T + 1)
                then(dve.scalar_tensor_tensor(c2[:, :, :], c3[:, :, :], -0.5 * BIG, ex[:, :, :], ALU.is_lt, ALU.mult))
                then(dve.tensor_reduce(zsum[:, :], c2[:, :, :], AX.X, ALU.add))
                then(dve.reciprocal(rz[:, :], zsum[:, :]))
                if later(T):
                    dve.wait_ge(q["w_turned"], T)
                dve.scalar_tensor_tensor(wt[:, :, :], c2[:, :, :], SCALE,
                                         rz[:, :].rearrange("p (h o) -> p h o", o=1).to_broadcast([128, HEADS, CAND]),
                                         ALU.mult, ALU.mult)\
                   .then_inc(q["wt"], 1)
                if backs:
                    output(T - 1)

            def one_hots(T):
                dve.wait_ge(q["p1"], T + 1)
                if later(T):
                    dve.wait_ge(q["p2"], T)
                dve.tensor_tensor(r1[:, :, :], ps_w[:, :, :], p1[:, :, :], ALU.subtract).then_inc(q["r1"], 1)
                dve.wait_ge(q["mm_t"], T + 1)
                if later(T):
                    dve.wait_ge(q["group_mm"], T)
                    dve.wait_ge(q["hw0"], T)

                for m in range(MIN):
                    last = dve.tensor_scalar(hot_min[:, :, m, :], mm_t[:, 1, :, :], float(m), None, ALU.is_equal)
                last.then_inc(q["hot_min"], 1)
                for m in range(MAJ):
                    dve.tensor_scalar(hot_maj[:, :, m, :], mm_t[:, 0, :, :].rearrange("p c (g t) -> p (c g) t", t=8),
                                      float(m), None, ALU.is_equal)
                dve.wait_ge(q["hot_min"], T + 1)
                dve.tensor_tensor(
                    hw[0][:, :, :, :], hot_min[:, :, :, :],
                    p1[:, :, :].rearrange("p c (o t) -> p c o t", o=1).to_broadcast([CP, CCH, MIN, 128]), ALU.mult)\
                   .then_inc(q["hots"], 1)

            def diagonals(T):
                dve.wait_ge(q["group_mm"], T + 1)
                if later(T):
                    dve.wait_ge(q["a_mm"], T)
                dve.tensor_tensor(diag[:, :, :, :].rearrange("p g m t -> p (g m) t"),
                                  ps_d[:, :, :, :].rearrange("p g m t -> p (g m) t"),
                                  at("own").rearrange("p (o t) -> p o t", o=1).to_broadcast([128, NG * MIN, 8]), ALU.mult)\
                   .then_inc(q["diag"], 1)

            def output(T):
                dve.wait_ge(q["a_mm"], T + 1)
                dve.wait_ge(q["g_act"], T + 1)
                if later(T):
                    dve.wait_ge(q["out_mm"], T)
                dve.tensor_tensor(z[:, :], g[:, :], ps_m[:, 1, :], ALU.mult).then_inc(q["z"], 1)
                dve.wait_ge(q["out_mm"], T + 1)
                dve.tensor_tensor(h[:, tok(T)], h[:, tok(T)], ps_m[:, 3, :], ALU.add).then_inc(q["h_ready"], 1)
            centre(0)
            scaled(0)
            middle(0, backs=False)
            middle(1)
            with dve.Fori(2, NTT - 1) as T:
                middle(T)
            middle(NTT - 1, with_front=False)
            one_hots(NTT - 1)
            diagonals(NTT - 1)
            output(NTT - 1)


STAGES = ("tok", "l0_attn", "l0_ffn", "l1_attn", "l1_ffn", "l2_attn", "l2_ffn", "l3_attn", "l3_ffn")


def build_tower(nc, dram, where, out, stages=STAGES, h_in=None):
    with ExitStack() as ctx:
        t = Tower(nc, ctx, dram, where)
        load_base(t)
        if h_in is not None:
            loaded = t.sem("h_loaded")
            with nc.Block() as block:
                @block.sync
                def _(sp):
                    sp.dma_start(t.h[:, :], h_in).then_inc(loaded, 16)
                    sp.wait_ge(loaded, 16)
        steps = {"tok": embed, "l0_attn": memory_mixer, "l0_ffn": product_key_ffn,
                 "l1_attn": l1_attention, "l1_ffn": l1_experts, "l2_attn": l2_attention,
                 "l2_ffn": l2_experts, "l3_attn": l3_attention, "l3_ffn": l3_experts}
        for name in stages:
            if name != "tok":
                layernorm(t)
            steps[name](t)
            t.end_stage()
        write_out(t, out)


class Pack:

    def __init__(self):
        self.parts, self.where, self.width = [], {}, 0

    def add(self, name, a):
        import numpy as np
        a = np.asarray(a)
        a = a.reshape(a.shape[0], -1)
        assert a.shape[0] == 128, (name, a.shape)
        self.where[name] = (self.width, self.width + a.shape[1])
        self.parts.append(a)
        self.width += a.shape[1]

    def array(self):
        import numpy as np
        self.where["_width"] = self.width
        return np.ascontiguousarray(np.concatenate(self.parts, axis=1))


def heads32(a, fill=None):
    import numpy as np
    out = np.zeros((*a.shape[:-1], 2, 4, 32), a.dtype)
    out[..., :16] = a.reshape(*a.shape[:-1], 2, 4, 16)
    for row, value in (fill or {}).items():
        out[..., row] = value
    return out


def lay_out(x):
    import numpy as np
    f = np.float32
    eye = np.eye(128, dtype=f)
    arrays, where = {}, {}

    base = Pack()
    base.add("ident", eye)
    base.add("mean", np.full((128, 128), 1.0 / D, f))
    base.add("mean_every", np.tile(np.arange(128 + NB - 1) % NB == NB - 1, (128, 1)).astype(f) / f(D))
    base.add("eps", np.full((128, 1), LN_EPS, f))
    arrays["base"] = base.array()
    where["base"] = base.where

    p = Pack()
    p.add("proj", x["L0_tok_proj_w"].reshape(D, 3, D).transpose(2, 1, 0))
    p.add("proj_b", x["L0_tok_proj_b"].reshape(D, 1))
    arrays["tok"], where["tok"] = p.array(), p.where
    arrays["x"] = np.ascontiguousarray(x["x"])
    for n in (2, 3, 4):
        arrays[f"emb{n}"] = np.ascontiguousarray(x[f"L0_tok_emb_{n}"])

    p = Pack()
    p.add("q1", x["L0_attn_w_q1"].T)
    p.add("q2", x["L0_attn_w_q2"].T)
    p.add("m1", x["L0_attn_mem_w1"].T)
    p.add("m2", x["L0_attn_mem_w2"].T.reshape(2, 128, 128).transpose(1, 0, 2))
    p.add("out", x["L0_attn_w_out"].T)
    p.add("ones", np.ones((128, 128), f))
    p.add("conv_w", x["L0_attn_conv_q_w"].reshape(128, 4))
    p.add("conv_b", x["L0_attn_conv_q_b"].reshape(128, 1))
    arrays["l0a"], where["l0a"] = p.array(), p.where

    rows = np.arange(128)
    same = (rows[:, None] // 32) == (rows[None, :] // 32)
    r32 = rows % 32
    den = (same & (r32[:, None] == 16)).astype(f)

    def selections(rows_per_head, stacks, blocks):
        out = []
        for s in range(2):
            for st, (m, *used) in enumerate(stacks):
                for p in used[s]:
                    for hd in range(128 // rows_per_head):
                        a = np.zeros((128, m), f)
                        for i, part in enumerate(blocks[s][st]):
                            if part == p:
                                r = np.arange(rows_per_head)
                                a[rows_per_head * hd + r, rows_per_head * i + r] = 1.0
                        out.append(a)
        return np.concatenate(out, axis=1)

    for n, a in (("sel16", selections(16, STACK16, ((Q16,), (K16,)))), ("sel32", selections(32, STACK32, (Q32, K32)))):
        arrays[n], where[n] = a, {"_width": a.shape[1]}

    def attention_pack(wv, bv, wo, bo, max0):
        p = Pack()
        p.add("v", wv)
        p.add("o", heads32(np.ascontiguousarray(wo.T)).reshape(128, 2, 128).transpose(2, 1, 0))
        p.add("den", den)
        p.add("bv", np.broadcast_to(bv[None, :], (128, 128)))
        p.add("bo", bo.reshape(128, 1))
        minus = np.zeros((128, 4), f)
        for part in range(3):
            for hd in range(4):
                minus[max0 + 4 * part + hd, hd] = -1.0
        p.add("minus", minus)
        return p

    p = attention_pack(x["L1_attn_Wv"], x["L1_attn_bv"], x["L1_attn_Wo"], x["L1_attn_bo"], 96)
    p.add("wq", x["L1_attn_Wq"])
    p.add("wk", x["L1_attn_Wv"])
    p.add("bq", x["L1_attn_bq"].reshape(128, 1))
    p.add("bk", x["L1_attn_bv"].reshape(128, 1))
    rot = np.zeros((128, 128), f)
    for r in range(128):
        if r % 16 < 8:
            rot[r + 8, r] = -1.0
        else:
            rot[r - 8, r] = 1.0
    p.add("rot", rot)
    theta = (1.0 / 10000.0 ** (np.arange(0, 16, 2, dtype=f) / f(16))).astype(f)
    angle = (np.arange(S, dtype=f)[:, None] * theta[None, :]).astype(f)
    angle = np.concatenate([angle, angle], axis=1).T
    for n, fn in (("cos", np.cos), ("sin", np.sin)):
        p.add(n, np.tile(fn(angle.astype(np.float64)).astype(f), (8, 1)))
    arrays["l1a"], where["l1a"] = p.array(), p.where

    def with_points(a, ap, fill=None):
        out = np.zeros((*a.shape[:-1], 2, 4, 32), f)
        out[..., :16] = a.reshape(*a.shape[:-1], 2, 4, 16)
        out[..., 16:28] = ap.reshape(*a.shape[:-1], 2, 4, 12)
        for row, value in (fill or {}).items():
            out[..., row] = value
        return out

    p = attention_pack(x["L2_attn_wv"], x["L2_attn_bv"], x["L2_attn_wo"], x["L2_attn_bo"], 64)
    p.add("wq", with_points(x["L2_attn_wq"], x["L2_attn_wqp"]))
    p.add("wk", with_points(x["L2_attn_wk"], x["L2_attn_wkp"]))
    p.add("bq", with_points(x["L2_attn_bq"], x["L2_attn_bqp"], {29: 1.0}).reshape(2, 128).T)
    p.add("bk", with_points(x["L2_attn_bk"], x["L2_attn_bkp"], {28: 1.0}).reshape(2, 128).T)
    p.add("ln_g", x["L2_attn_ln_g"].reshape(128, 1))
    p.add("ln_b", x["L2_attn_ln_b"].reshape(128, 1))
    p.add("ps", np.repeat(x["L2_attn_pscale"], 32).reshape(2, 128).T)
    points = (r32[:, None] >= 16) & (r32[:, None] < 28) & same
    p.add("sum_q", (points & (r32[None, :] == 28)).astype(f))
    p.add("sum_k", (points & (r32[None, :] == 29)).astype(f))
    p.add("two_on_points", np.where((r32 >= 16) & (r32 < 28), 2.0, 0.0).astype(f).reshape(128, 1))
    p.add("rest", np.where(r32 < 16, 0.25, np.where(r32 == 29, 1.0, 0.0)).astype(f).reshape(128, 1))
    arrays["l2a"], where["l2a"] = p.array(), p.where

    p = attention_pack(np.ascontiguousarray(x["L3_attn_Wv"].T), np.zeros(128, f),
                       np.ascontiguousarray(x["L3_attn_Wo"].T), x["L3_attn_bo"], 96)
    p.add("wq", x["L3_attn_Wq"])
    p.add("wk", x["L3_attn_Wk"])
    head = (rows[:, None] // 16) == (rows[None, :] // 16)
    p.add("head_mean", head.astype(f) / f(16))
    p.add("head_centre", eye - head.astype(f) / f(16))
    for n in "qk":
        for what in ("gamma", "beta"):
            p.add(f"{n}_{what}", np.tile(x[f"L3_attn_{n}_{what}"], 8).reshape(128, 1))
    arrays["l3a"], where["l3a"] = p.array(), p.where
    ij = rows[:, None] - rows[None, :]
    arrays["causal"] = np.concatenate([np.where(ij < 0, -BIG, 0.0), np.where(ij > 0, -BIG, 0.0)],
                                      axis=1).astype(f)

    p = Pack()
    p.add("wq", x["L0_ffn_Wq"].reshape(4, 128, 128).transpose(1, 0, 2))
    p.add("bq", x["L0_ffn_bq"].reshape(4, 128).T)
    half = (rows[:, None] // 64) == (rows[None, :] // 64)
    quarter = (rows[:, None] // 32) == (rows[None, :] // 32)
    p.add("head_mean", half.astype(f) / f(64))
    p.add("head_centre", eye - half.astype(f) / f(64))
    p.add("quarter", quarter.astype(f))
    p.add("ln_g", np.tile(x["L0_ffn_ln_g"], 2).reshape(128, 1))
    p.add("ln_b", np.tile(x["L0_ffn_ln_b"], 2).reshape(128, 1))
    keys = np.zeros((2, 2, 32, 4, 64), f)
    for hh in range(2):
        keys[hh, 0, :, 2 * hh, :] = x["L0_ffn_keys0"].T
        keys[hh, 1, :, 2 * hh + 1, :] = x["L0_ffn_keys1"].T
    p.add("keys", keys.reshape(128, 256))
    p.add("down", x["L0_ffn_expert_down"][0:128].T)
    p.add("up", x["L0_ffn_expert_up"][0:128])
    p.add("ones", np.ones((128, 128), f))
    p.add("own", (r32[:, None] % 8 == np.arange(8)[None, :]).astype(f) / f(SCALE))
    p.add("place", np.concatenate([(rows[:, None] // 8 * 8 + m == rows[None, :]).astype(f) for m in range(8)], axis=1))
    arrays["l0f"], where["l0f"] = p.array(), p.where

    def experts(name, w1, w2, b1=None, b2=None, w3=None):
        n_exp, _, hidden = w1.shape
        nch = hidden // 128
        arrays[name + "_w1"] = np.ascontiguousarray(w1)
        arrays[name + "_w2"] = np.ascontiguousarray(w2.reshape(n_exp, nch, 128, D).transpose(0, 2, 1, 3))
        if w3 is not None:
            arrays[name + "_w3"] = np.ascontiguousarray(w3)
        if b1 is not None:
            arrays[name + "_b1"] = np.ascontiguousarray(b1.reshape(n_exp, nch, 128).transpose(2, 0, 1))
            arrays[name + "_b2"] = np.ascontiguousarray(b2)

    experts("l1f", x["L1_ffn_w1"][::-1], x["L1_ffn_w2"][::-1], x["L1_ffn_b1"][::-1], x["L1_ffn_b2"][::-1])
    arrays["l1f_router"] = np.ascontiguousarray(x["L1_ffn_router_w"][:, ::-1])
    arrays["l1f_router_b"] = np.ascontiguousarray(np.broadcast_to(x["L1_ffn_router_b"][::-1][None, :], (128, 64)))
    experts("l2f", x["L2_ffn_w1"].transpose(0, 2, 1), x["L2_ffn_w2"].transpose(0, 2, 1),
            w3=x["L2_ffn_w3"].transpose(0, 2, 1))
    arrays["l2f_router"] = np.ascontiguousarray(x["L2_ffn_gate_w"].T)
    arrays["l2f_sw1"] = np.ascontiguousarray(x["L2_ffn_sw1"].T)
    arrays["l2f_sw2"] = np.ascontiguousarray(x["L2_ffn_sw2"].T.reshape(4, 128, D).transpose(1, 0, 2))
    experts("l3f", x["L3_ffn_w1"], x["L3_ffn_w2"], x["L3_ffn_b1"], x["L3_ffn_b2"])
    arrays["l3f_router"] = np.ascontiguousarray(x["L3_ffn_gate_w"].T)
    return arrays, where


def kernel(**inputs):
    import numpy as np
    import concourse.bacc as bacc
    from concourse.bass_utils import run_bass_kernel_spmd

    x = {k: np.asarray(v) for k, v in inputs.items()}
    arrays, where = lay_out(x)
    nc = bacc.Bacc("TRN2", target_bir_lowering=False, num_devices=1)
    dram = {n: nc.dram_tensor(f"in_{n}", a.shape, mybir.dt.from_np(a.dtype), kind="ExternalInput").ap()
            for n, a in arrays.items()}
    out = nc.dram_tensor("out_0", (NB, S, D), F32, kind="ExternalOutput").ap()
    build_tower(nc, dram, where, out)
    r = run_bass_kernel_spmd(nc, [{f"in_{n}": a for n, a in arrays.items()}], core_ids=[0])
    return r.results[0]["out_0"]
```

```python
from contextlib import ExitStack

import concourse.bass as bass
from concourse import mybir

F32 = mybir.dt.float32
BF16 = mybir.dt.bfloat16
F16 = mybir.dt.float16
I32 = mybir.dt.int32
U32 = mybir.dt.uint32
ALU = mybir.AluOpType
ACT = mybir.ActivationFunctionType
AX = mybir.AxisListType

D = 128
NB, S = 8, 512
NT = NB * S
NTT = NT // 128
VOCAB = 25000
LN_EPS = 1e-5
BIG = 1e30
SCALE = 4096.0


def wait(eng, sem, value):
    if isinstance(value, int) and value <= 0:
        return
    eng.wait_ge(sem, value)


def turns(eng, count, body, peel=1):
    for i in range(min(peel, count)):
        body(i)
    if count > peel:
        with eng.Fori(peel, count) as i:
            body(i)


def skewed(eng, count, first, second):
    first(0)
    first(1)
    second(0)
    with eng.Fori(2, count) as i:
        first(i)
        second(i - 1)
    second(count - 1)


def cols(i, n=S):
    return bass.ds(i * n, n)


class Tower:

    def __init__(self, nc, ctx, dram, where):
        self.nc, self.ctx, self.dram, self.where = nc, ctx, dram, where
        self.h = self.sb(ctx, "h", [128, NT])
        self.xn = self.sb(ctx, "xn", [128, NT])
        self.base = self.sb(ctx, "base", [128, where["base"]["_width"]])
        self.ident = self.at(self.base, "base", "ident")
        self.mean = self.at(self.base, "base", "mean")
        self.eps = self.at(self.base, "base", "eps")
        self.stage_sems = []
        self.mean_every = self.at(self.base, "base", "mean_every")
        self.ln_count = 0
        self.ln_sems = {n: ctx.enter_context(nc.semaphore("ln_" + n)) for n in
                        ("mean", "centred", "square", "var", "std", "rstd", "spread", "norm")}

    def sb(self, ctx, name, shape, dt=F32):
        return ctx.enter_context(self.nc.sbuf_tensor(name, shape, dt))

    def ps(self, ctx, name, shape, dt=F32):
        return ctx.enter_context(self.nc.psum_tensor(name, shape, dt))

    def sem(self, name):
        self.stage_sems.append(self.nc.alloc_semaphore(name))
        return self.stage_sems[-1]

    def end_stage(self):
        with self.nc.Block() as block:
            @block.gpsimd
            def _(pool):
                self.nc.clear_and_free_semaphores(self.stage_sems)
        self.stage_sems = []

    def at(self, tile, pack, name):
        lo, hi = self.where[pack][name]
        return tile[:, lo:hi]


def load_base(t):
    nc = t.nc
    loaded = t.sem("base_loaded")
    with nc.Block() as block:
        @block.sync
        def _(sp):
            sp.dma_start(t.base[:, :], t.dram["base"]).then_inc(loaded, 16)
            sp.wait_ge(loaded, 16)


def layernorm(t):
    nc, h, xn = t.nc, t.h, t.xn
    q = t.ln_sems
    k = t.ln_count
    t.ln_count += 1
    with ExitStack() as ctx:
        n = f"ln{k}_"
        square = t.sb(ctx, n + "square", [128, 2, S])
        std, rstd = t.sb(ctx, n + "std", [128, S]), t.sb(ctx, n + "rstd", [128, S])
        ps_mean = t.ps(ctx, n + "ps_mean", [128, 3, S])
        ps_var = t.ps(ctx, n + "ps_var", [128, S])
        ps_b = t.ps(ctx, n + "ps_b", [128, 4, S])
        block = ctx.enter_context(nc.Block())

        @block.tensor
        def _(pe):
            def mean(i):
                if i >= 3:
                    pe.wait_ge(q["centred"], NB * k + i - 2)
                pe.matmul(ps_mean[:, i % 3, :], t.mean, h[:, cols(i)], start=True, stop=True).then_inc(q["mean"], 1)

            def var(i):
                pe.wait_ge(q["square"], NB * k + i + 1)
                pe.matmul(ps_var[:, :], t.mean_every[:, NB - 1 - i:NB - 1 - i + 128], square[:, i % 2, :],
                          start=(i == 0), stop=(i == NB - 1)).then_inc(q["var"], 1)
            mean(0)
            mean(1)
            for i in range(2, NB):
                mean(i)
                var(i - 2)
            var(NB - 2)
            var(NB - 1)
            pe.wait_ge(q["rstd"], k + 1)
            for i in range(NB):
                if i >= 4:
                    pe.wait_ge(q["norm"], NB * k + i - 3)
                pe.matmul(ps_b[:, i % 4, :], t.ident[:, i:i + 1].to_broadcast([128, 128]), rstd[:, :],
                          start=True, stop=True).then_inc(q["spread"], 1)

        @block.vector
        def _(dve):
            for i in range(NB):
                dve.wait_ge(q["mean"], NB * k + i + 1)
                dve.tensor_tensor(xn[:, cols(i)], h[:, cols(i)], ps_mean[:, i % 3, :], ALU.subtract)\
                   .then_inc(q["centred"], 1)
            dve.wait_ge(q["std"], k + 1)
            dve.reciprocal(rstd[:, :], std[:, :]).then_inc(q["rstd"], 1)
            for i in range(NB):
                dve.wait_ge(q["spread"], NB * k + i + 1)
                if i == 0:
                    dve.wait_ge(q["square"], NB * k + NB)
                dve.tensor_tensor(xn[:, cols(i)], xn[:, cols(i)], ps_b[:, i % 4, :], ALU.mult).then_inc(q["norm"], 1)

        @block.scalar
        def _(act):
            for i in range(NB):
                act.wait_ge(q["centred"], NB * k + i + 1)
                if i >= 2:
                    act.wait_ge(q["var"], NB * k + i - 1)
                act.activation(square[:, i % 2, :], xn[:, cols(i)], ACT.Square).then_inc(q["square"], 1)
            act.wait_ge(q["var"], NB * k + NB)
            act.activation(std[:, :], ps_var[:, :], ACT.Sqrt, bias=t.eps[:, 0:1]).then_inc(q["std"], 1)


def write_out(t, out):
    nc, h = t.nc, t.h
    with ExitStack() as ctx:
        hb = t.sb(ctx, "wo_hb", [128, 2, S])
        rows = t.sb(ctx, "wo_rows", [128, 2, S])
        ps_t = t.ps(ctx, "wo_ps", [128, 2, S])
        copied, turned, evacuated = t.sem("wo_copied"), t.sem("wo_turned"), t.sem("wo_evacuated")
        stored = [t.sem("wo_stored0"), t.sem("wo_stored1")]
        block = ctx.enter_context(nc.Block())

        @block.gpsimd
        def _(pool):
            def body(j):
                for s in range(2):
                    wait(pool, turned, 2 * j + s - 1)
                    pool.tensor_copy(hb[:, s, :], h[:, bass.ds(j * 2 * S + s * S, S)]).then_inc(copied, 1)
            turns(pool, NB // 2, body)

        @block.tensor
        def _(pe):
            def body(j):
                for s in range(2):
                    pe.wait_ge(copied, 2 * j + s + 1)
                    wait(pe, evacuated, 2 * j + s - 1)
                    for c in range(4):
                        last = pe.transpose(ps_t[:, s, 128 * c:128 * c + 128], hb[:, s, 128 * c:128 * c + 128],
                                            t.ident)
                    last.then_inc(turned, 1)
            turns(pe, NB // 2, body)

        @block.vector
        def _(dve):
            def body(j):
                for s in range(2):
                    dve.wait_ge(turned, 2 * j + s + 1)
                    wait(dve, stored[s], 16 * j)
                    dve.tensor_copy(rows[:, s, :], ps_t[:, s, :]).then_inc(evacuated, 1)
            turns(dve, NB // 2, body)

        @block.sync
        def _(sp):
            def body(j):
                for s in range(2):
                    sp.wait_ge(evacuated, 2 * j + s + 1)
                    sp.dma_start(out[bass.ds(j * 2 + s, 1), :, :].rearrange("a (c p) d -> p (a c) d", p=128),
                                 rows[:, s, :].rearrange("p (c d) -> p c d", c=4)).then_inc(stored[s], 16)
            turns(sp, NB // 2, body)
            for s in range(2):
                sp.wait_ge(stored[s], 16 * (NB // 2))


def embed(t):
    nc, h = t.nc, t.h
    with ExitStack() as ctx:
        sb = lambda n, shape, dt=F32: t.sb(ctx, "tok_" + n, shape, dt)
        sem = lambda n: t.sem("tok_" + n)
        w = sb("w", [128, t.where["tok"]["_width"]])
        proj, proj_b = t.at(w, "tok", "proj"), t.at(w, "tok", "proj_b")
        xi, xf = sb("xi", [NB, S], I32), sb("xf", [NB, S])
        v, r, fix = sb("v", [NB, S]), sb("r", [NB, S]), sb("fix", [NB, S])
        quot = sb("quot", [NB, S], I32)
        ids = sb("ids", [NB, 3, S])
        idx = sb("idx", [128, 3, 4, NB], U32)
        rows = sb("rows", [128, 2, 3, 4, 128])
        emb = sb("emb", [128, 3, S])
        ps_i = t.ps(ctx, "tok_ps_i", [128, S])
        ps_t = t.ps(ctx, "tok_ps_t", [128, 3, S])
        ps_p = t.ps(ctx, "tok_ps_p", [128, 2, S])
        loaded, zeroed, x_in, chain = sem("loaded"), sem("zeroed"), sem("x_in"), sem("chain")
        ids_ready, ids_turned, idx_ready = sem("ids_ready"), sem("ids_turned"), sem("idx_ready")
        gathered = [sem("gathered0"), sem("gathered1")]
        turned, emb_ready, projected, h_ready = sem("turned"), sem("emb_ready"), sem("projected"), sem("h_ready")
        block = ctx.enter_context(nc.Block())

        @block.sync
        def _(sp):
            sp.dma_start(xi[:, :], t.dram["x"]).then_inc(x_in, 16)
            sp.dma_start(w[:, :], t.dram["tok"]).then_inc(loaded, 16)
            sp.wait_ge(loaded, 16)

        @block.vector
        def _(dve):
            steps = [0]

            def then(ins):
                steps[0] += 1
                ins.then_inc(chain, 1)
                dve.wait_ge(chain, steps[0])

            def modulo(n):
                then(dve.tensor_scalar(quot[:, 0:n], v[:, 0:n], 1.0 / VOCAB, None, ALU.mult))
                then(dve.scalar_tensor_tensor(r[:, 0:n], quot[:, 0:n], -float(VOCAB), v[:, 0:n], ALU.mult, ALU.add))
                then(dve.tensor_scalar(fix[:, 0:n], r[:, 0:n], 0.0, float(VOCAB), ALU.is_lt, ALU.mult))
                then(dve.tensor_tensor(r[:, 0:n], r[:, 0:n], fix[:, 0:n], ALU.add))
                then(dve.tensor_scalar(fix[:, 0:n], r[:, 0:n], float(VOCAB), -float(VOCAB), ALU.is_ge, ALU.mult))
                then(dve.tensor_tensor(r[:, 0:n], r[:, 0:n], fix[:, 0:n], ALU.add))

            dve.memset(ids[:, :, :], 0.0).then_inc(zeroed, 1)
            dve.wait_ge(x_in, 16)
            then(dve.tensor_copy(xf[:, :], xi[:, :]))
            then(dve.tensor_copy(v[:, :], xf[:, :]))
            modulo(S)
            dve.wait_ge(zeroed, 1)
            for n in range(2, 5):
                m, c = S - n + 1, n // 2
                then(dve.scalar_tensor_tensor(v[:, 0:m], r[:, 0:m], 64.0, xf[:, n - 1:n - 1 + m], ALU.mult, ALU.add))
                modulo(m)
                then(dve.tensor_copy(ids[:, n - 2, c:c + m], r[:, 0:m]))
            dve.sem_inc(ids_ready, 1)
            dve.wait_ge(ids_turned, 1)
            dve.tensor_copy(idx[:, :, :, :].rearrange("p a c b -> p (a c b)"), ps_i[:, 0:96]).then_inc(idx_ready, 1)

            def body(b):
                dve.wait_ge(turned, b + 1)
                wait(dve, projected, b)
                dve.tensor_copy(emb[:, 0, 1:S], ps_t[:, 0, 1:S]).then_inc(emb_ready, 1)
                dve.tensor_copy(emb[:, 1, 1:S - 1], ps_t[:, 1, 1:S - 1]).then_inc(emb_ready, 1)
                dve.tensor_copy(emb[:, 2, 2:S - 1], ps_t[:, 2, 2:S - 1]).then_inc(emb_ready, 1)
            dve.memset(emb[:, :, 0:2], 0.0).then_inc(zeroed, 1)
            dve.memset(emb[:, :, S - 1:S], 0.0).then_inc(zeroed, 1)
            dve.wait_ge(zeroed, 3)
            turns(dve, NB, body)

        @block.gpsimd
        def _(pool):
            pool.wait_ge(idx_ready, 1)
            for b in range(NB):
                wait(pool, turned, b - 1)
                for n in range(3):
                    for c in range(4):
                        pool.indirect_dma_start(
                            rows[:, b % 2, n, c, :], None, t.dram[f"emb{n + 2}"],
                            bass.IndirectOffsetOnAxis(ap=idx[:, n, c, b:b + 1], axis=0),
                            ).then_inc(gathered[b % 2], 16)

        @block.scalar
        def _(act):
            act.wait_ge(loaded, 16)

            def body(b):
                act.wait_ge(projected, b + 1)
                act.activation(h[:, cols(b)], ps_p[:, b % 2, :], ACT.Identity, bias=proj_b).then_inc(h_ready, 1)
            turns(act, NB, body)

        @block.tensor
        def _(pe):
            pe.wait_ge(ids_ready, 1)
            for n in range(3):
                for c in range(4):
                    at = 32 * n + 8 * c
                    last = pe.transpose(ps_i[:, at:at + 8], ids[:, n, 128 * c:128 * c + 128], t.ident[0:NB, 0:NB])
            last.then_inc(ids_turned, 1)
            pe.wait_ge(loaded, 16)

            def body(j):
                for s in range(2):
                    b = 2 * j + s
                    pe.wait_ge(gathered[s], 16 * 12 * (j + 1))
                    wait(pe, emb_ready, 3 * b)
                    for n in range(3):
                        for c in range(4):
                            last = pe.transpose(ps_t[:, n, 128 * c:128 * c + 128], rows[:, s, n, c, :], t.ident)
                    last.then_inc(turned, 1)
                    pe.wait_ge(emb_ready, 3 * b + 3)
                    wait(pe, h_ready, b - 1)
                    for n in range(3):
                        last = pe.matmul(ps_p[:, s, :], proj[:, 128 * n:128 * n + 128], emb[:, n, :],
                                         start=(n == 0), stop=(n == 2))
                    last.then_inc(projected, 1)
            turns(pe, NB // 2, body)


def memory_mixer(t):
    nc, h, xn = t.nc, t.h, t.xn
    with ExitStack() as ctx:
        sb = lambda n, shape, dt=F32: t.sb(ctx, "l0a_" + n, shape, dt)
        sem = lambda n: t.sem("l0a_" + n)
        w = sb("w", [128, t.where["l0a"]["_width"]])
        at = lambda n: t.at(w, "l0a", n)
        s1, qp = sb("s1", [128, 2, S]), sb("qp", [128, 2, S + 3])
        conv = sb("conv", [128, 2, S])
        s2, sq = sb("s2", [128, NT]), sb("sq", [128, 2, S])
        norm, rnorm, qn = sb("norm", [128, S]), sb("rnorm", [128, S]), sb("qn", [128, 2, S])
        u, r = sb("u", [128, 2, 2, S]), sb("r", [128, 2, S])
        ps_1, ps_2 = t.ps(ctx, "l0a_ps1", [128, 2, S]), t.ps(ctx, "l0a_ps2", [128, 2, S])
        ps_n = t.ps(ctx, "l0a_psn", [128, S])
        ps_u, ps_o = t.ps(ctx, "l0a_psu", [128, 2, S]), t.ps(ctx, "l0a_pso", [128, S])
        ps_b, ps_r = ps_1, ps_2
        loaded, zeroed = sem("loaded"), sem("zeroed")
        p1, s1_ready, p2, qp_ready, tapped = sem("p1"), sem("s1_ready"), sem("p2"), sem("qp_ready"), sem("tapped")
        s2_ready, sq_ready, summed, norm_ready = sem("s2_ready"), sem("sq_ready"), sem("summed"), sem("norm_ready")
        guarded, inverted, spread, qn_ready = sem("guarded"), sem("inverted"), sem("spread"), sem("qn_ready")
        up, u_ready, down, r_ready, outp, h_ready = [sem(n) for n in
                                                    ("up", "u_ready", "down", "r_ready", "outp", "h_ready")]
        block = ctx.enter_context(nc.Block())

        @block.sync
        def _(sp):
            sp.dma_start(w[:, :], t.dram["l0a"]).then_inc(loaded, 16)
            sp.wait_ge(loaded, 16)

        def pipeline(*stages):
            for turn in range(NB + len(stages) - 1):
                for k, stage in enumerate(stages):
                    if 0 <= turn - k < NB:
                        stage(turn - k)

        @block.tensor
        def _(pe):
            pe.wait_ge(loaded, 16)

            def first(b):
                wait(pe, s1_ready, b - 1)
                pe.matmul(ps_1[:, b % 2, :], at("q1"), xn[:, cols(b)], start=True, stop=True).then_inc(p1, 1)

            def second(b):
                pe.wait_ge(s1_ready, b + 1)
                wait(pe, qp_ready, b - 1)
                pe.matmul(ps_2[:, b % 2, :], at("q2"), s1[:, b % 2, :], start=True, stop=True).then_inc(p2, 1)

            def nothing(b):
                pass

            def sums(b):
                pe.wait_ge(sq_ready, b + 1)
                pe.matmul(ps_n[:, :], at("every")[:, NB - 1 - b:NB - 1 - b + 128], sq[:, b % 2, :],
                          start=(b == 0), stop=(b == NB - 1)).then_inc(summed, 1)
            pipeline(first, second, nothing, sums)

            def spread_norm(b):
                pe.wait_ge(inverted, 1)
                wait(pe, qn_ready, b - 1)
                pe.matmul(ps_b[:, b % 2, :], t.ident[:, b:b + 1].to_broadcast([128, 128]), rnorm[:, :],
                          start=True, stop=True).then_inc(spread, 1)

            def hidden(b):
                pe.wait_ge(qn_ready, b + 1)
                wait(pe, u_ready, b)
                for c in range(2):
                    last = pe.matmul(ps_u[:, c, :], at("m1")[:, 128 * c:128 * c + 128], qn[:, b % 2, :],
                                     start=True, stop=True)
                last.then_inc(up, 1)

            def retrieved(b):
                pe.wait_ge(u_ready, b + 1)
                wait(pe, r_ready, b - 1)
                for c in range(2):
                    last = pe.matmul(ps_r[:, b % 2, :], at("m2")[:, 128 * c:128 * c + 128], u[:, b % 2, c, :],
                                     start=(c == 0), stop=(c == 1))
                last.then_inc(down, 1)

            def output(b):
                pe.wait_ge(r_ready, b + 1)
                wait(pe, h_ready, b)
                pe.matmul(ps_o[:, :], at("out"), r[:, b % 2, :], start=True, stop=True).then_inc(outp, 1)
            pipeline(spread_norm, hidden, retrieved, output)

        @block.scalar
        def _(act):
            act.wait_ge(zeroed, 1)

            def first(b):
                act.wait_ge(p1, b + 1)
                wait(act, p2, b - 1)
                act.activation(s1[:, b % 2, :], ps_1[:, b % 2, :], ACT.Silu).then_inc(s1_ready, 1)

            def second(b):
                act.wait_ge(p2, b + 1)
                wait(act, tapped, 4 * (b - 1))
                act.activation(qp[:, b % 2, 3:S + 3], ps_2[:, b % 2, :], ACT.Copy).then_inc(qp_ready, 1)

            def third(b):
                act.wait_ge(tapped, 4 * b + 4)
                act.activation(s2[:, cols(b)], conv[:, b % 2, :], ACT.Silu).then_inc(s2_ready, 1)
                wait(act, summed, b - 1)
                act.wait_ge(s2_ready, b + 1)
                act.activation(sq[:, b % 2, :], s2[:, cols(b)], ACT.Square).then_inc(sq_ready, 1)
            pipeline(first, second, third)
            act.wait_ge(summed, NB)
            act.activation(norm[:, :], ps_n[:, :], ACT.Sqrt).then_inc(norm_ready, 1)

            def hidden(b):
                act.wait_ge(up, b + 1)
                wait(act, down, b - 1)
                act.activation(u[:, b % 2, :, :], ps_u[:, :, :], ACT.Silu).then_inc(u_ready, 1)

            def retrieved(b):
                act.wait_ge(down, b + 1)
                wait(act, outp, b - 1)
                act.activation(r[:, b % 2, :], ps_r[:, b % 2, :], ACT.Copy).then_inc(r_ready, 1)
            pipeline(hidden, retrieved)

        @block.vector
        def _(dve):
            dve.memset(qp[:, :, 0:3], 0.0).then_inc(zeroed, 1)
            dve.wait_ge(zeroed, 1)
            dve.wait_ge(loaded, 16)
            for b in range(NB):
                dve.wait_ge(qp_ready, b + 1)
                wait(dve, s2_ready, b - 1)
                taps, to = qp[:, b % 2, :], conv[:, b % 2, :]
                dve.tensor_scalar(to, taps[:, 0:S], at("conv_w")[:, 0:1], at("conv_b"), ALU.mult, ALU.add)\
                   .then_inc(tapped, 1)
                for i in range(1, 4):
                    dve.wait_ge(tapped, 4 * b + i)
                    dve.scalar_tensor_tensor(to, taps[:, i:S + i], at("conv_w")[:, i:i + 1], to, ALU.mult, ALU.add)\
                       .then_inc(tapped, 1)
            dve.wait_ge(norm_ready, 1)
            dve.tensor_scalar(norm[:, :], norm[:, :], 1e-12, None, ALU.max).then_inc(guarded, 1)
            dve.wait_ge(guarded, 1)
            dve.reciprocal(rnorm[:, :], norm[:, :]).then_inc(inverted, 1)

            def normalise(b):
                dve.wait_ge(spread, b + 1)
                if b == 0:
                    dve.wait_ge(s2_ready, NB)
                wait(dve, up, b - 1)
                dve.tensor_tensor(qn[:, b % 2, :], s2[:, cols(b)], ps_b[:, b % 2, :], ALU.mult).then_inc(qn_ready, 1)

            def add(b):
                dve.wait_ge(outp, b + 1)
                dve.tensor_tensor(h[:, cols(b)], h[:, cols(b)], ps_o[:, :], ALU.add).then_inc(h_ready, 1)

            def nothing(b):
                pass
            pipeline(normalise, nothing, nothing, add)


TURNS = 2
FIRST = 4


def per_turn(f, b, j):
    if isinstance(j, int):
        return f(b)
    return j * (f(b + 2) - f(b)) + f(b)


def wait_turn(eng, sem, f, b, j):
    if f(b) <= 0:
        assert isinstance(j, int), "a loop's wait has to be above zero in its first turn"
        return
    eng.wait_ge(sem, per_turn(f, b, j))


class Banks:

    def __init__(self, items, sems):
        self.number, self.count, self.sems, self.before = {}, {}, sems, []
        counts = {"act": 0, "dve": 0}
        for n in range(-2, 18):
            for slot, kind, b, reader in items(n):
                counts[reader] += 1
                self.number[kind, b] = len(self.before)
                self.count[kind, b] = (reader, counts[reader])
                self.before.append((reader, counts[reader]))

    def bank(self, kind, b):
        return self.number[kind, b] % 2

    def wait_free(self, pe, kind, b, j):
        if self.number[kind, b] >= 2:
            reader, _ = self.before[self.number[kind, b] - 2]
            def value(b):
                r, count = self.before[self.number[kind, b] - 2]
                assert r == reader
                return count
            wait_turn(pe, self.sems[reader], value, b, j)

    def wait_filled(self, eng, kind, b, j):
        wait_turn(eng, self.sems["filled"], lambda b: self.number[kind, b] + 1, b, j)

    def wait_read(self, eng, kind, b, j):
        reader, _ = self.count[kind, b]
        wait_turn(eng, self.sems[reader], lambda b: self.count[kind, b][1], b, j)


def attention(t, name, prepare, preps, stacks, sel, n_tiles=1, causal=False, scale=0.25, plus_input=False,
              once=()):
    nc = t.nc
    GROUPS, LAST = 2 * NB, 20
    NST = len(stacks)
    MAX0 = stacks[-1][0]
    heads_per_tile = 8 // n_tiles
    with ExitStack() as ctx:
        sb = lambda n, shape, dt=F32: t.sb(ctx, f"{name}_{n}", shape, dt)
        sem = lambda n: t.sem(f"{name}_{n}")
        w = sb("w", [128, t.where[name]["_width"]])
        at = lambda n: t.at(w, name, n)
        sel_w = t.where[sel]["_width"]
        select = [sb("select_q", [128, sel_w // 2], BF16), sb("select_k", [128, sel_w // 2], BF16)]
        x = sb("x", [128, S])
        qk = [sb("q", [128, n_tiles, S]), sb("k", [128, n_tiles, S])]
        rest = sb("rest", [128, S])
        parts = [sb("q_parts", [128, 2, 3, n_tiles, S], BF16), sb("k_parts", [128, 2, 3, n_tiles, S], BF16)]
        stack = [sb("q_stack", [128, NST, 4, 4, S], BF16), sb("k_stack", [128, NST, 4, 4, S], BF16)]
        maxima = sb("maxima", [128, 4, 4])
        max_rest = sb("max_rest", [128, 2, 4, 4])
        max_parts = sb("max_parts", [128, 4, 128], BF16)
        v = sb("v", [128, 2, 4, 8, 32])
        probs = sb("probs", [128, 8, S])
        o = sb("o", [128, 2, S])
        o_norm = sb("o_norm", [128, 2, S])
        den_sb, rden = sb("den_sb", [128, 2, S]), sb("rden", [128, S])
        identb = sb("identb", [128, 128], BF16)
        mask, maskb = (sb("mask", [128, 2, 128]), sb("maskb", [128, 2, 128], BF16)) if causal else (None, None)
        ps_1 = t.ps(ctx, name + "_ps_1", [128, 2, S])
        ps_2 = t.ps(ctx, name + "_ps_2", [128, 2, S])
        ps_o = t.ps(ctx, name + "_ps_o", [128, S])
        ps_m = t.ps(ctx, name + "_ps_m", [128, 1024], BF16)
        pj = t.ps(ctx, name + "_pj", [128, 2, S])
        idle = sem("idle")
        loaded, sel_in, sel_cast, zeroed, filled_in = sem("loaded"), sem("sel_in"), sem("sel_cast"), sem("zeroed"), sem("filled_in")
        x_ready, v_ready = sem("x_ready"), sem("v_ready")
        final = [sem("q_final"), sem("k_final")]
        split = [sem("q_split"), sem("k_split")]
        scored1, maxed, max_split, turned, shift_ready = [sem(n) for n in
                                                          ("scored1", "maxed", "max_split", "turned", "shift_ready")]
        scored2, exped, mixed, o_ready = sem("scored2"), sem("exped"), sem("mixed"), sem("o_ready")
        o_normed, h_ready, inverted = sem("o_normed"), sem("h_ready"), sem("inverted")
        reads = {"filled": sem("filled"), "act": sem("read_act"), "dve": sem("read_dve")}
        n_loads = 32 if causal else 16

        sels = [("sel", hd, s, st) for hd in range(4) for s in range(2) for st in range(NST)]

        def items(n):
            out = []
            if n % 2 == 0:
                if n == -2:
                    out += [(0, use, 0, "act") for use in once]
                out += [(place, use, n // 2 + 1, reader) for place, use, reader in preps if n // 2 + 1 < NB]
            else:
                if n // 2 + 1 < NB:
                    out += [(0, "v", n // 2 + 1, "dve")]
                if n // 2 - 1 >= 0:
                    out += [(p, use, n // 2 - 1, reader) for p, use, reader in
                            ((3, "den0", "act"), (7, "den1", "act"), (14, "out", "dve"))]
            if 0 <= n + 1 < GROUPS:
                first = 2 if causal else 4
                out += [(first + i * (LAST - first) // len(sels), (*u, (n + 1) % 2), (n + 1) // 2, ("act", "dve")[u[2]])
                        for i, u in enumerate(sels)]
            return sorted(out, key=lambda item: item[0])

        banks = Banks(items, reads)
        a = {"at": at, "sb": sb, "sem": sem, "x": x, "qk": qk, "pj": pj, "x_ready": x_ready, "final": final,
             "split": split, "banks": banks, "reads": reads,
             "loaded": (loaded, n_loads)}
        pre = prepare(t, a)
        wv, wo, den, bv, bo = at("v"), at("o"), at("den"), at("bv"), at("bo")
        block = ctx.enter_context(nc.Block())

        def steps(eng, step):
            for n in range(-2, FIRST):
                step(n, 0)
            with eng.Fori(0, TURNS) as j:
                for n in range(FIRST, FIRST + 4):
                    step(n, j)
            for n in range(FIRST + 4 * TURNS, GROUPS + 2):
                step(n, 0)

        def span(tile, as_keys):
            if not causal:
                return 0, S
            return (128 * tile, S) if as_keys else (0, 128 * tile + 128)

        def cols_turn(b, j):
            return cols(b) if isinstance(j, int) else bass.ds(j * (2 * S) + b * S, S)

        @block.sync
        def _(sp):
            sp.dma_start(w[:, :], t.dram[name]).then_inc(loaded, 16)
            if causal:
                sp.dma_start(mask[:, :, :], t.dram["causal"].rearrange("p (a c) -> p a c", a=2)).then_inc(loaded, 16)
            for s in range(2):
                wait(sp, sel_cast, s)
                sp.dma_start(probs[:, :, :].rearrange("p a s -> p (a s)")[:, 0:sel_w // 2],
                             t.dram[sel][:, s * (sel_w // 2):(s + 1) * (sel_w // 2)]).then_inc(sel_in, 16)
            sp.wait_ge(loaded, n_loads)
            sp.wait_ge(sel_in, 32)

        @block.gpsimd
        def _(pool):
            pool.memset(max_parts[:, :, :], 0.0).then_inc(zeroed, 1)
            pool.memset(v[:, :, :, :, 16:32], 0.0).then_inc(zeroed, 1)
            pool.wait_ge(zeroed, 2)
            pool.memset(v[:, :, :, :, 16:17], 1.0).then_inc(zeroed, 1)

            def body(jj):
                for parity in range(2):
                    b = 2 * jj + parity
                    wait(pool, v_ready, b)
                    pre["input"](pool, b)
                    for i in range(n_tiles):
                        for s in range(2):
                            m = n_tiles * b + i
                            pool.wait_ge(final[s], m + 1)
                            wait(pool, scored1, 32 * b - 32)
                            pool.sem_inc(idle, 1)
                            p, tile = parts[s][:, parity, :, i, :], qk[s][:, i, :]
                            pool.tensor_copy(p[:, 0, :], tile).then_inc(split[s], 1)
                            pool.wait_ge(split[s], 4 * m + 1)
                            pool.tensor_tensor(rest[:, :], tile, p[:, 0, :], ALU.subtract).then_inc(split[s], 1)
                            pool.wait_ge(split[s], 4 * m + 2)
                            pool.sem_inc(idle, 1)
                            pool.tensor_copy(p[:, 1, :], rest[:, :]).then_inc(split[s], 1)
                            pool.wait_ge(split[s], 4 * m + 3)
                            pool.tensor_tensor(p[:, 2, :], rest[:, :], p[:, 1, :], ALU.subtract).then_inc(split[s], 1)
                            pool.wait_ge(split[s], 4 * m + 4)
            turns(pool, NB // 2, body, peel=2)

        @block.scalar
        def _(act):
            act.wait_ge(loaded, n_loads)

            def cast_selections():
                for s in range(2):
                    act.wait_ge(sel_in, 16 * s + 16)
                    act.activation(select[s][:, :], probs[:, :, :].rearrange("p a s -> p (a s)")[:, 0:sel_w // 2], ACT.Copy)\
                       .then_inc(sel_cast, 1)
                act.wait_ge(sel_cast, 2)

            def step(n, j):
                if n == -1:
                    cast_selections()
                m, bm, gm = n - 1, (n - 1) // 2, (n - 1) % 2
                todo = items(n)
                for place in range(LAST + 1):
                    u = place - 3
                    if 0 <= m < GROUPS and 0 <= u < 16:
                        lo, hi = span(u // 4, True)
                        wait_turn(act, scored2, lambda b: 16 * (2 * b + gm) + u + 1, bm, j)
                        wait_turn(act, mixed, lambda b: 4 * (2 * b + gm) + u // 4 - 1, bm, j)
                        act.activation(probs[:, u % 8, lo:hi], ps_2[:, u % 2, lo:hi], ACT.Exp, scale=scale)\
                           .then_inc(exped, 1)
                    for _, use, b, reader in [item for item in todo if item[0] == place]:
                        if use[0] == "sel":
                            _, hd, s, st, g = use
                            if reader == "act":
                                banks.wait_filled(act, use, b, j)
                                M = stacks[st][0]
                                act.activation(stack[s][0:M, st, (2 * b + g) % 4, hd, :], pj[0:M, banks.bank(use, b), :],
                                               ACT.Copy).then_inc(reads["act"], 1)
                        elif use in ("den0", "den1"):
                            i = int(use[3])
                            banks.wait_filled(act, use, b, j)
                            wait_turn(act, inverted, lambda b: 4 * (2 * b - 1 + i), b, j)
                            act.activation(den_sb[:, i, :], pj[:, banks.bank(use, b), :], ACT.Copy).then_inc(reads["act"], 1)
                        elif use in pre["act"]:
                            pre["act"][use](act, b, j)
                    if place == 18 and 0 <= n < GROUPS:
                        wait_turn(act, turned, lambda b: 2 * b + n % 2 + 1, n // 2, j)
                        act.activation(stack[0][MAX0:MAX0 + 32, NST - 1, n % 4, :, :],
                                       ps_m[MAX0:MAX0 + 32, 0:S].rearrange("p (o s) -> p o s", o=1).to_broadcast([32, 4, S]),
                                       ACT.Copy).then_inc(shift_ready, 1)
            steps(act, step)

        @block.vector
        def _(dve):
            dve.wait_ge(loaded, n_loads)
            if "setup" in pre:
                pre["setup"](dve)

            def fill():
                for i in range(4):
                    dve.tensor_copy(stack[1][MAX0:MAX0 + 32, NST - 1, i, :, :],
                                    at("minus")[MAX0:MAX0 + 32, :].rearrange("p (h o) -> p h o", o=1).to_broadcast([32, 4, S]))\
                       .then_inc(filled_in, 1)
                dve.tensor_copy(identb[:, :], t.ident).then_inc(filled_in, 1)
                if causal:
                    dve.tensor_copy(maskb[:, :, :], mask[:, :, :]).then_inc(filled_in, 1)
                dve.wait_ge(filled_in, 6 if causal else 5)
                dve.wait_ge(zeroed, 3)

            def normalise(dve, i, quarter, b, j):
                cut = slice(128 * quarter, 128 * quarter + 128)
                count = lambda b: 4 * (2 * b + i) + quarter
                if quarter == 0:
                    banks.wait_read(dve, f"den{i}", b, j)
                    wait_turn(dve, o_normed, lambda b: 2 * b + i, b, j)
                dve.reciprocal(rden[:, cut], den_sb[:, i, cut]).then_inc(inverted, 1)
                if quarter == 3:
                    wait_turn(dve, inverted, lambda b: count(b) + 1, b, j)
                    wait_turn(dve, o_ready, lambda b: 2 * b + i + 1, b, j)
                    wait_turn(dve, h_ready, lambda b: (2 if plus_input else 1) * b, b, j)
                    dve.tensor_tensor(o_norm[:, i, :], o[:, i, :], rden[:, :], ALU.mult).then_inc(o_normed, 1)

            def step(n, j):
                if n == -1:
                    fill()
                bn, g = n // 2, n % 2
                todo = items(n)
                for place in range(LAST + 1):
                    u = place
                    if 0 <= n < GROUPS and u < 16:
                        hd, c = u // 4, u % 4
                        lo, hi = span(c, False)
                        wait_turn(dve, scored1, lambda b: 16 * (2 * b + g) + u + 1, bn, j)
                        dve.tensor_reduce(maxima[:, c, hd:hd + 1], ps_1[:, u % 2, lo:hi], AX.X, ALU.max).then_inc(maxed, 1)
                    if place == 2 and 0 <= n - 2 < GROUPS:
                        wait_turn(dve, mixed, lambda b: 4 * (2 * b + g) + 4, bn - 1, j)
                        dve.tensor_copy(o[:, g, :], ps_o[:, :]).then_inc(o_ready, 1)
                    for _, use, b, reader in [item for item in todo if item[0] == place]:
                        if use[0] == "sel":
                            _, hd, s, st, sg = use
                            if reader == "dve":
                                banks.wait_filled(dve, use, b, j)
                                M = stacks[st][0]
                                dve.tensor_copy(stack[s][0:M, st, (2 * b + sg) % 4, hd, :], pj[0:M, banks.bank(use, b), :])\
                                   .then_inc(reads["dve"], 1)
                        elif use == "v":
                            banks.wait_filled(dve, use, b, j)
                            dve.tensor_tensor(v[:, b % 2, :, :, 0:16],
                                              pj[:, banks.bank(use, b), :].rearrange("p (c h d) -> p c h d", c=4, d=16),
                                              bv.rearrange("p (a h d) -> p a h d", a=1, d=16).to_broadcast([128, 4, 8, 16]),
                                              ALU.add).then_inc(reads["dve"], 1)
                            banks.wait_read(dve, use, b, j)
                            dve.sem_inc(v_ready, 1)
                        elif use == "out":
                            hb = t.h[:, cols_turn(b, j)]
                            banks.wait_filled(dve, use, b, j)
                            dve.scalar_tensor_tensor(hb, pj[:, banks.bank(use, b), :], bo, hb, ALU.add, ALU.add)\
                               .then_inc(reads["dve"], 1)
                            banks.wait_read(dve, use, b, j)
                            dve.sem_inc(h_ready, 1)
                            if plus_input:
                                dve.tensor_tensor(hb, hb, t.xn[:, cols_turn(b, j)], ALU.add).then_inc(h_ready, 1)
                        elif use in pre["dve"]:
                            pre["dve"][use](dve, b, j)
                    if n % 2 == 1 and n // 2 - 1 >= 0 and 5 <= place < 13:
                        normalise(dve, (place - 5) // 4, (place - 5) % 4, n // 2 - 1, j)
                    if n % 2 == 0 and n // 2 + 1 < NB and place in pre.get("dve_at", {}):
                        pre["dve_at"][place](dve, n // 2 + 1, j)
                    if place == 16 and 0 <= n < GROUPS:
                        wait_turn(dve, maxed, lambda b: 16 * (2 * b + g) + 16, bn, j)
                        wait_turn(dve, turned, lambda b: 2 * b + g, bn, j)
                        into = lambda i: max_parts[:, :, MAX0 + 4 * i:MAX0 + 4 * i + 4]
                        done = lambda i: wait_turn(dve, max_split, lambda b: 5 * (2 * b + g) + i, bn, j)
                        dve.tensor_copy(into(0), maxima[:, :, :]).then_inc(max_split, 1)
                        done(1)
                        dve.tensor_tensor(max_rest[:, 0, :, :], maxima[:, :, :], into(0), ALU.subtract).then_inc(max_split, 1)
                        done(2)
                        dve.tensor_copy(into(1), max_rest[:, 0, :, :]).then_inc(max_split, 1)
                        done(3)
                        dve.tensor_tensor(max_rest[:, 1, :, :], max_rest[:, 0, :, :], into(1), ALU.subtract)\
                           .then_inc(max_split, 1)
                        done(4)
                        dve.tensor_copy(into(2), max_rest[:, 1, :, :]).then_inc(max_split, 1)
            steps(dve, step)

        @block.tensor
        def _(pe):
            pe.wait_ge(loaded, n_loads)

            def step(n, j):
                if n == -1:
                    pe.wait_ge(sel_cast, 2)
                    pe.wait_ge(filled_in, 6 if causal else 5)
                bn, g = n // 2, n % 2
                m, bm, gm = n - 1, (n - 1) // 2, (n - 1) % 2
                todo = items(n)
                for place in range(LAST + 1):
                    u = place
                    if 0 <= n < GROUPS and u < 16:
                        hd, c = u // 4, u % 4
                        lo, hi = span(c, False)
                        if c == 0:
                            for s in range(2):
                                banks.wait_read(pe, ("sel", hd, s, NST - 1, g), bn, j)
                        wait_turn(pe, maxed, lambda b: 16 * (2 * b + g) + u - 1, bn, j)
                        M, d = stacks[0][0], 128 * c
                        last = pe.matmul(ps_1[:, u % 2, lo:hi], stack[0][0:M, 0, n % 4, hd, d:d + 128],
                                         stack[1][0:M, 0, n % 4, hd, lo:hi], start=True, stop=not causal)
                        if causal:
                            last = pe.matmul(ps_1[:, u % 2, d:d + 128], identb[:, :], maskb[:, 0, :], start=False, stop=True)
                        last.then_inc(scored1, 1)
                    u = place - 3
                    if 0 <= m < GROUPS and 0 <= u < 16:
                        c, hd = u // 4, u % 4
                        lo, hi = span(c, True)
                        if u == 0:
                            wait_turn(pe, shift_ready, lambda b: 2 * b + gm + 1, bm, j)
                        wait_turn(pe, exped, lambda b: 16 * (2 * b + gm) + u - 1, bm, j)
                        d = 128 * c
                        for st in range(NST):
                            M = MAX0 + 32 if st == NST - 1 else stacks[st][0]
                            last = pe.matmul(ps_2[:, u % 2, lo:hi], stack[1][0:M, st, m % 4, hd, d:d + 128],
                                             stack[0][0:M, st, m % 4, hd, lo:hi], start=(st == 0),
                                             stop=(st == NST - 1 and not causal))
                        if causal:
                            last = pe.matmul(ps_2[:, u % 2, d:d + 128], identb[:, :], maskb[:, 1, :], start=False, stop=True)
                        last.then_inc(scored2, 1)
                    if 0 <= m < GROUPS and place >= 8 and place % 4 == 0:
                        c = (place - 8) // 4
                        lo, hi = span(c, True)
                        if c == 0:
                            wait_turn(pe, v_ready, lambda b: b + 1, bm, j)
                            wait_turn(pe, o_ready, lambda b: 2 * b + gm, bm, j)
                        wait_turn(pe, exped, lambda b: 16 * (2 * b + gm) + 4 * c + 4, bm, j)
                        for hd in range(4):
                            last = pe.matmul(ps_o[32 * hd:32 * hd + 32, lo:hi], v[:, bm % 2, c, 4 * gm + hd, :],
                                             probs[:, (4 * c + hd) % 8, lo:hi], start=(c == 0), stop=(c == 3))
                        last.then_inc(mixed, 1)
                    for _, use, b, reader in [item for item in todo if item[0] == place]:
                        banks.wait_free(pe, use, b, j)
                        to = pj[:, banks.bank(use, b), :]
                        if use[0] == "sel":
                            _, hd, s, st, sg = use
                            M, used = stacks[st][0], stacks[st][1 + s]
                            head = 4 * sg + hd
                            tile, head = head // heads_per_tile, head % heads_per_tile
                            wait_turn(pe, split[s], lambda b: 4 * (n_tiles * b + tile + 1), b, j)
                            lo = sum(len(stacks[i][1 + s]) * heads_per_tile * stacks[i][0] for i in range(st))
                            for i, p in enumerate(used):
                                at_ = lo + (i * heads_per_tile + head) * M
                                last = pe.matmul(to[0:M, :], select[s][:, at_:at_ + M], parts[s][:, b % 2, p, tile, :],
                                                 start=(i == 0), stop=(i == len(used) - 1))
                        elif use == "v":
                            for c in range(4):
                                last = pe.matmul(to[:, 128 * c:128 * c + 128], x[:, 128 * c:128 * c + 128], wv,
                                                 start=True, stop=True)
                        elif use in ("den0", "den1"):
                            i = int(use[3])
                            wait_turn(pe, o_ready, lambda b: 2 * b + i + 1, b, j)
                            last = pe.matmul(to, den, o[:, i, :], start=True, stop=True)
                        elif use == "out":
                            wait_turn(pe, o_normed, lambda b: 2 * b + 2, b, j)
                            for i in range(2):
                                last = pe.matmul(to, wo[:, 128 * i:128 * i + 128], o_norm[:, i, :],
                                                 start=(i == 0), stop=(i == 1))
                        else:
                            last = pre["pe"][use](pe, b, j, to)
                        last.then_inc(reads["filled"], 1)
                    if place == 17 and 0 <= n < GROUPS:
                        wait_turn(pe, max_split, lambda b: 5 * (2 * b + g) + 5, bn, j)
                        wait_turn(pe, shift_ready, lambda b: 2 * b + g, bn, j)
                        for c in range(4):
                            last = pe.transpose(ps_m[:, 128 * c:128 * c + 128], max_parts[:, c, :], identb[:, :])
                        last.then_inc(turned, 1)
            steps(pe, step)


STACK16 = [(96, (0, 1, 2), (0, 1, 2))]
Q16, K16 = (0, 0, 0, 1, 1, 2), (0, 1, 2, 0, 1, 0)
STACK32 = [(128, (0, 1), (0, 1)), (64, (0, 2), (0, 2))]
Q32, K32 = ((0, 0, 1, 1), (0, 2)), ((0, 1, 0, 1), (2, 0))


def copy_input(t, a):
    def copy(pool, b):
        pool.tensor_copy(a["x"][:, :], t.xn[:, cols(b)]).then_inc(a["x_ready"], 1)
    return copy


def l1_attention(t):
    def prepare(t, a):
        sb, at, pj, x, banks, reads = a["sb"], a["at"], a["pj"], a["x"], a["banks"], a["reads"]
        q, k = a["qk"]
        lin, qcos, qsin = sb("lin", [128, S]), sb("qcos", [128, S]), sb("qsin", [128, S])
        cos_ready = a["sem"]("cos_ready")

        def project(wn):
            def f(pe, b, j, to):
                wait_turn(pe, a["x_ready"], lambda b: b + 1, b, j)
                return pe.matmul(to, at(wn), x[:, :], start=True, stop=True)
            return f

        def rotate(pe, b, j, to):
            banks.wait_read(pe, "q", b, j)
            return pe.matmul(to, at("rot"), lin[:, :], start=True, stop=True)

        def act_q(act, b, j):
            banks.wait_filled(act, "q", b, j)
            wait_turn(act, a["final"][0], lambda b: b, b, j)
            act.activation(lin[:, :], pj[:, banks.bank("q", b), :], ACT.Identity, bias=at("bq")).then_inc(reads["act"], 1)

        def act_k(act, b, j):
            banks.wait_filled(act, "k", b, j)
            wait_turn(act, a["split"][1], lambda b: 4 * b, b, j)
            act.activation(k[:, 0, :], pj[:, banks.bank("k", b), :], ACT.Identity, bias=at("bk")).then_inc(reads["act"], 1)
            banks.wait_read(act, "k", b, j)
            act.sem_inc(a["final"][1], 1)

        def dve_rot(dve, b, j):
            banks.wait_read(dve, "q", b, j)
            dve.tensor_tensor(qcos[:, :], lin[:, :], at("cos"), ALU.mult).then_inc(cos_ready, 1)
            banks.wait_filled(dve, "rot", b, j)
            dve.tensor_tensor(qsin[:, :], pj[:, banks.bank("rot", b), :], at("sin"), ALU.mult).then_inc(reads["dve"], 1)
            banks.wait_read(dve, "rot", b, j)
            wait_turn(dve, cos_ready, lambda b: b + 1, b, j)
            wait_turn(dve, a["split"][0], lambda b: 4 * b, b, j)
            dve.tensor_tensor(q[:, 0, :], qcos[:, :], qsin[:, :], ALU.add).then_inc(a["final"][0], 1)

        return {"input": copy_input(t, a), "pe": {"q": project("wq"), "k": project("wk"), "rot": rotate},
                "act": {"q": act_q, "k": act_k}, "dve": {"rot": dve_rot}}
    attention(t, "l1a", prepare, [(1, "q", "act"), (2, "k", "act"), (4, "rot", "dve")], STACK16, "sel16",
              plus_input=True)


def l2_attention(t):
    def prepare(t, a):
        sb, at, pj, x, banks, reads = a["sb"], a["at"], a["pj"], a["x"], a["banks"], a["reads"]
        final, split = a["final"], a["split"]
        lin = [sb("q_lin", [128, 2, S]), sb("k_lin", [128, 2, S])]
        sq = [sb("q_sq", [128, 2, S]), sb("k_sq", [128, 2, S])]
        q_scaled = sb("q_scaled", [128, S])
        q_scale, minus_ps = sb("q_scale", [128, 2]), sb("minus_ps", [128, 2])
        normed, copied, idle = sb("normed", [128, S]), a["sem"]("copied"), a["sem"]("idle_input")
        squared, scaled, constants = a["sem"]("squared"), a["sem"]("scaled"), a["sem"]("constants")

        def input_scaled(pool, b):
            if isinstance(b, int) and b == 0:
                pool.wait_ge(*a["loaded"])
            pool.tensor_copy(normed[:, :], t.xn[:, cols(b)]).then_inc(copied, 1)
            pool.wait_ge(copied, b + 1)
            pool.sem_inc(idle, 1)
            pool.tensor_scalar(x[:, :], normed[:, :], at("ln_g"), at("ln_b"), ALU.mult, ALU.add)\
                .then_inc(a["x_ready"], 1)

        def setup(dve):
            for g in range(2):
                dve.scalar_tensor_tensor(q_scale[:, g:g + 1], at("ps")[:, g:g + 1], at("two_on_points"), at("rest"),
                                         ALU.mult, ALU.add).then_inc(constants, 1)
            dve.tensor_scalar(minus_ps[:, :], at("ps"), -1.0, None, ALU.mult).then_inc(constants, 1)
            dve.wait_ge(constants, 3)

        pe_uses, act_uses, dve_uses = {}, {}, {}
        for g in range(2):
            for s, n in enumerate("qk"):
                def project(pe, b, j, to, n=n, g=g):
                    wait_turn(pe, a["x_ready"], lambda b: b + 1, b, j)
                    return pe.matmul(to, at("w" + n)[:, 128 * g:128 * g + 128], x[:, :], start=True, stop=True)

                def linear(act, b, j, n=n, s=s, g=g):
                    use = f"{n}{g}"
                    banks.wait_filled(act, use, b, j)
                    wait_turn(act, final[s], lambda b: 2 * b, b, j)
                    act.activation(lin[s][:, g, :], pj[:, banks.bank(use, b), :], ACT.Identity,
                                   bias=at("b" + n)[:, g:g + 1]).then_inc(reads["act"], 1)
                    banks.wait_read(act, use, b, j)
                    act.activation(sq[s][:, g, :], lin[s][:, g, :], ACT.Square).then_inc(squared, 1)

                def norms(pe, b, j, to, n=n, s=s, g=g):
                    wait_turn(pe, squared, lambda b: 4 * b + 2 * g + s + 1, b, j)
                    return pe.matmul(to, at("sum_" + n), sq[s][:, g, :], start=True, stop=True)

                def combine(dve, b, j, n=n, s=s, g=g):
                    use = f"{n}sum{g}"
                    other = lin[1][:, g, :]
                    banks.wait_read(dve, f"{n}{g}", b, j)
                    if s == 0:
                        wait_turn(dve, final[0], lambda b: 2 * b + g, b, j)
                        other = q_scaled[:, :]
                        dve.tensor_scalar(q_scaled[:, :], lin[0][:, g, :], q_scale[:, g:g + 1], None, ALU.mult)\
                           .then_inc(scaled, 1)
                        wait_turn(dve, scaled, lambda b: 2 * b + g + 1, b, j)
                    banks.wait_filled(dve, use, b, j)
                    wait_turn(dve, split[s], lambda b: 4 * (2 * b - 1 + g), b, j)
                    dve.scalar_tensor_tensor(a["qk"][s][:, g, :], pj[:, banks.bank(use, b), :], minus_ps[:, g:g + 1],
                                             other, ALU.mult, ALU.add).then_inc(reads["dve"], 1)
                    banks.wait_read(dve, use, b, j)
                    dve.sem_inc(final[s], 1)
                pe_uses[f"{n}{g}"], pe_uses[f"{n}sum{g}"] = project, norms
                act_uses[f"{n}{g}"], dve_uses[f"{n}sum{g}"] = linear, combine
        return {"input": input_scaled, "pe": pe_uses, "act": act_uses, "dve": dve_uses, "setup": setup}
    preps = [(0, "q0", "act"), (1, "k0", "act"), (2, "q1", "act"), (3, "k1", "act"),
             (4, "qsum0", "dve"), (6, "ksum0", "dve"), (8, "qsum1", "dve"), (10, "ksum1", "dve")]
    attention(t, "l2a", prepare, preps, STACK32, "sel32", n_tiles=2, scale=1.0)


def l3_attention(t):
    def prepare(t, a):
        sb, at, pj, x, banks, reads = a["sb"], a["at"], a["pj"], a["x"], a["banks"], a["reads"]
        final, split = a["final"], a["split"]
        centred_w = [sb("q_centred_w", [128, 128]), sb("k_centred_w", [128, 128])]
        cen = [sb("q_cen", [128, S]), sb("k_cen", [128, S])]
        sq = [sb("q_sq", [128, S]), sb("k_sq", [128, S])]
        std = [sb("q_std", [128, S]), sb("k_std", [128, S])]
        rstd, unit = sb("rstd", [128, S]), sb("unit", [128, S])
        squared = [a["sem"]("q_squared"), a["sem"]("k_squared")]
        rstd_ready, unit_ready = a["sem"]("rstd_ready"), a["sem"]("unit_ready")
        pe_uses, act_uses, dve_at = {}, {}, {}
        for s, n in enumerate("qk"):
            def centre_w(pe, b, j, to, n=n):
                return pe.matmul(to[:, 0:128], at("w" + n), at("head_centre"), start=True, stop=True)

            def project(pe, b, j, to, n=n, s=s):
                wait_turn(pe, a["x_ready"], lambda b: b + 1, b, j)
                banks.wait_read(pe, n + "w", 0, 0)
                return pe.matmul(to, centred_w[s][:, :], x[:, :], start=True, stop=True)

            def variance(pe, b, j, to, s=s):
                wait_turn(pe, squared[s], lambda b: b + 1, b, j)
                return pe.matmul(to, at("head_mean"), sq[s][:, :], start=True, stop=True)

            def copy_w(act, b, j, n=n, s=s):
                banks.wait_filled(act, n + "w", b, j)
                act.activation(centred_w[s][:, :], pj[:, banks.bank(n + "w", b), 0:128], ACT.Copy).then_inc(reads["act"], 1)

            def centred(act, b, j, n=n, s=s):
                banks.wait_filled(act, n, b, j)
                wait_turn(act, unit_ready, lambda b: 2 * b - 1 + s, b, j)
                act.activation(cen[s][:, :], pj[:, banks.bank(n, b), :], ACT.Copy).then_inc(reads["act"], 1)
                banks.wait_read(act, n, b, j)
                act.activation(sq[s][:, :], cen[s][:, :], ACT.Square).then_inc(squared[s], 1)

            def root(act, b, j, n=n, s=s):
                banks.wait_filled(act, n + "var", b, j)
                wait_turn(act, rstd_ready, lambda b: 4 * (2 * b - 1 + s), b, j)
                act.activation(std[s][:, :], pj[:, banks.bank(n + "var", b), :], ACT.Sqrt, bias=t.eps[:, 0:1])\
                   .then_inc(reads["act"], 1)

            def normalise(dve, b, j, n=n, s=s, quarter=0):
                cut = slice(128 * quarter, 128 * quarter + 128)
                if quarter == 0:
                    banks.wait_read(dve, n + "var", b, j)
                    wait_turn(dve, unit_ready, lambda b: 2 * b + s, b, j)
                dve.reciprocal(rstd[:, cut], std[s][:, cut]).then_inc(rstd_ready, 1)
                if quarter < 3:
                    return
                wait_turn(dve, rstd_ready, lambda b: 4 * (2 * b + s + 1), b, j)
                wait_turn(dve, final[1 - s], lambda b: b + s, b, j)
                dve.tensor_tensor(unit[:, :], cen[s][:, :], rstd[:, :], ALU.mult).then_inc(unit_ready, 1)
                wait_turn(dve, unit_ready, lambda b: 2 * b + s + 1, b, j)
                wait_turn(dve, split[s], lambda b: 4 * b, b, j)
                dve.tensor_scalar(a["qk"][s][:, 0, :], unit[:, :], at(n + "_gamma"), at(n + "_beta"), ALU.mult, ALU.add)\
                   .then_inc(final[s], 1)
            pe_uses.update({n + "w": centre_w, n: project, n + "var": variance})
            act_uses.update({n + "w": copy_w, n: centred, n + "var": root})
            for quarter in range(4):
                dve_at[7 + 4 * s + quarter] = lambda dve, b, j, f=normalise, quarter=quarter: f(dve, b, j, quarter=quarter)
        return {"input": copy_input(t, a), "pe": pe_uses, "act": act_uses, "dve": {}, "dve_at": dve_at}
    attention(t, "l3a", prepare, [(1, "q", "act"), (1, "k", "act"), (6, "qvar", "act"), (6, "kvar", "act")],
              STACK16, "sel16", causal=True, once=("qw", "kw"))


class Chain:

    def __init__(self, eng, sem, idle=None):
        self.eng, self.sem, self.idle, self.per, self.turn, self.k = eng, sem, idle, None, 0, 0

    def start(self, turn):
        if not (isinstance(turn, int) and turn == 0) and self.per is None:
            self.per = self.k
        self.turn, self.k = turn, 0

    def value(self):
        return self.k if self.per is None else self.turn * self.per + self.k

    def then(self, ins):
        self.k += 1
        ins.then_inc(self.sem, 1)
        self.eng.wait_ge(self.sem, self.value())

    def then_alone(self, ins):
        self.then(ins)
        self.eng.sem_inc(self.idle, 1)


def route(t, ctx, name, n_exp, top):
    nc = t.nc
    E, drop = n_exp, top < 0
    R, C = 2 * S, 2 * S // 128
    rounds = (-top + 7) // 8 if drop else 1
    pads = 8 * rounds - abs(top)
    weights = t.sb(ctx, name + "_weights", [128, NT])
    parts = t.sb(ctx, name + "_parts", [128, NT], F16)
    with ExitStack() as own:
        sb = lambda n, shape, dt=F32: t.sb(own, f"{name}r_{n}", shape, dt)
        sem = lambda n: t.sem(f"{name}r_{n}")
        wr, br = sb("wr", [128, E]), sb("br", [128, E])
        x = sb("x", [128, R])
        lg, ex, e2, mask = (sb(n, [128, C, E]) for n in ("lg", "ex", "e2", "mask"))
        prob = sb("prob", [128, C, E])
        key = sb("key", [128, C, E + pads])
        top8 = sb("top8", [128, C, 8])
        mx, sm, rs = (sb(n, [128, C]) for n in ("mx", "sm", "rs"))
        comb = sb("comb", [128, C, 128])
        p1 = sb("p1", [128, R], F16)
        ps_l = t.ps(own, name + "r_psl", [128, C, 64])
        ps_t = t.ps(own, name + "r_pst", [128, R])
        loaded, zeroed, x_ready, scored, shifted, exped, shifted2, exped2, comb_ready, turned, parted, chain = [
            sem(n) for n in ("loaded", "zeroed", "x_ready", "scored", "shifted", "exped", "shifted2", "exped2",
                             "comb_ready", "turned", "parted", "chain")]
        block = own.enter_context(nc.Block())
        n_loads = 2 if drop else 1

        def wide(tile):
            return tile.rearrange("p (c a) -> p c a", a=1).to_broadcast([128, C, E])

        @block.sync
        def _(sp):
            sp.dma_start(wr[:, :], t.dram[name + "_router"]).then_inc(loaded, 16)
            if drop:
                sp.dma_start(br[:, :], t.dram[name + "_router_b"]).then_inc(loaded, 16)
            sp.wait_ge(loaded, 16 * n_loads)

        @block.gpsimd
        def _(pool):
            pool.memset(comb[:, :, :], 0.0).then_inc(zeroed, 1)

            def body(b):
                wait(pool, scored, b)
                pool.tensor_copy(x[:, :], t.xn[:, cols(b, R)]).then_inc(x_ready, 1)
            turns(pool, NT // R, body)

        @block.tensor
        def _(pe):
            pe.wait_ge(loaded, 16 * n_loads)

            def body(b):
                pe.wait_ge(x_ready, b + 1)
                wait(pe, shifted, b)
                for c in range(C):
                    last = pe.matmul(ps_l[:, c, 0:E], x[:, 128 * c:128 * c + 128], wr[:, :], start=True, stop=True)
                last.then_inc(scored, 1)
                pe.wait_ge(comb_ready, b + 1)
                wait(pe, parted, b)
                for c in range(C):
                    last = pe.transpose(ps_t[:, 128 * c:128 * c + 128], comb[:, c, :], t.ident)
                last.then_inc(turned, 1)
            turns(pe, NT // R, body)

        @block.scalar
        def _(act):
            def body(b):
                act.wait_ge(shifted, b + 1)
                wait(act, comb_ready, b)
                act.activation(ex[:, :, :], lg[:, :, :], ACT.Exp).then_inc(exped, 1)
                if drop:
                    act.wait_ge(shifted2, b + 1)
                    act.activation(e2[:, :, :], prob[:, :, :], ACT.Exp).then_inc(exped2, 1)
            turns(act, NT // R, body)

        @block.vector
        def _(dve):
            dve.wait_ge(loaded, 16 * n_loads)
            dve.wait_ge(zeroed, 1)
            ch = Chain(dve, chain, t.sem(name + "r_idle"))

            def body(b):
                ch.start(b)
                then, then_alone = ch.then, ch.then_alone
                dve.wait_ge(scored, b + 1)
                if drop:
                    then(dve.tensor_tensor(lg[:, :, :], ps_l[:, :, 0:E],
                                           br[:, :].rearrange("p (a e) -> p a e", a=1).to_broadcast([128, C, E]), ALU.add))
                else:
                    then(dve.tensor_copy(lg[:, :, :], ps_l[:, :, 0:E]))
                then(dve.tensor_reduce(mx[:, :], lg[:, :, :], AX.X, ALU.max))
                if not drop:
                    then(dve.tensor_copy(key[:, :, 0:E], lg[:, :, :]))
                then(dve.tensor_tensor(lg[:, :, :], lg[:, :, :], wide(mx[:, :]), ALU.subtract))
                dve.sem_inc(shifted, 1)
                if drop:
                    dve.wait_ge(exped, b + 1)
                    then(dve.tensor_reduce(sm[:, :], ex[:, :, :], AX.X, ALU.add))
                    then(dve.reciprocal(rs[:, :], sm[:, :]))
                    then(dve.tensor_tensor(prob[:, :, :], ex[:, :, :], wide(rs[:, :]), ALU.mult))
                    then(dve.tensor_scalar(key[:, :, 0:E], prob[:, :, :], -1.0, None, ALU.mult))
                    then(dve.tensor_tensor(prob[:, :, :], prob[:, :, :], wide(rs[:, :]), ALU.subtract))
                    dve.sem_inc(shifted2, 1)
                then_alone(dve.memset(key[:, :, E:E + pads], BIG))
                for _ in range(rounds):
                    for c in range(C):
                        last = dve.max(top8[:, c, :], key[:, c, :])
                    then_alone(last)
                    for c in range(C):
                        last = dve.match_replace(key[:, c, :], top8[:, c, :], key[:, c, :], -BIG)
                    then_alone(last)
                then(dve.tensor_scalar(mask[:, :, :], key[:, :, 0:E], -0.5 * BIG, None, ALU.is_ge if drop else ALU.is_lt))
                dve.wait_ge(exped2 if drop else exped, b + 1)
                then(dve.tensor_tensor(mask[:, :, :], mask[:, :, :], (e2 if drop else ex)[:, :, :], ALU.mult))
                then(dve.tensor_reduce(sm[:, :], mask[:, :, :], AX.X, ALU.add))
                then(dve.reciprocal(rs[:, :], sm[:, :]))
                wait(dve, turned, b)
                then(dve.tensor_tensor(comb[:, :, 0:E], mask[:, :, :], wide(rs[:, :]), ALU.mult))
                then(dve.tensor_copy(comb[:, :, 64:64 + E], comb[:, :, 0:E]))
                dve.sem_inc(comb_ready, 1)
                dve.wait_ge(turned, b + 1)
                then(dve.tensor_copy(weights[:, cols(b, R)], ps_t[:, :]))
                then(dve.tensor_scalar(p1[:, :], ps_t[:, :], SCALE, None, ALU.mult))
                then(dve.scalar_tensor_tensor(parts[64:128, cols(b, R)], ps_t[64:128, :], SCALE, p1[64:128, :],
                                              ALU.mult, ALU.subtract))
                dve.sem_inc(parted, 1)
                then(dve.tensor_copy(parts[0:64, cols(b, R)], p1[0:64, :]))
            turns(dve, NT // R, body)
    return weights, parts


W_SCALE = 64.0
LAG = 3


def experts(t, name, n_exp, hidden, func, top, acc_tiles, prod_scale, biased=False, gated=False, shared=False):
    nc, h, xn = t.nc, t.h, t.xn
    nch = hidden // 128
    passes = NB // acc_tiles
    upe = acc_tiles * nch
    upp = 2 * upe
    with ExitStack() as ctx:
        weights, parts = route(t, ctx, name, n_exp, top)
        sb = lambda n, shape, dt=F32: t.sb(ctx, f"{name}_{n}", shape, dt)
        sem = lambda n: t.sem(f"{name}_{n}")
        n_mat = 3 if gated else 2
        w_raw = sb("w_raw", [128, 2, n_mat, hidden])
        w_hi, w_lo = sb("w_hi", [128, 2, n_mat, hidden], F16), sb("w_lo", [128, 2, n_mat, hidden], F16)
        x_hi, x_lo = sb("x_hi", [128, NT], F16), sb("x_lo", [128, NT], F16)
        acc_scale = prod_scale * W_SCALE
        b1 = sb("b1", [128, n_exp * nch]) if biased else None
        b2, b2s = (sb("b2", [n_exp, D]), sb("b2s", [n_exp, D])) if biased else (None, None)
        onehot = sb("onehot", [128, 64], F16)
        acted = sb("acted", [128, 4, S])
        gate = sb("gate", [128, 2, S]) if gated else None
        prod = sb("prod", [128, 2, S])
        p_hi, p_lo = sb("p_hi", [128, 4, S], F16), sb("p_lo", [128, 4, S], F16)
        ps_acc = t.ps(ctx, name + "_acc", [128, acc_tiles, S])
        ps_h = t.ps(ctx, name + "_ps_h", [128, 2, S])
        ps_g = t.ps(ctx, name + "_ps_g", [128, 2, S]) if gated else None
        ps_b = t.ps(ctx, name + "_ps_b", [128, 2, S])
        loaded, cast, idle = sem("loaded"), sem("cast"), sem("idle")
        w_in = [sem("w_in0"), sem("w_in1")]
        x_high, x_split, w_high, w_split = sem("x_high"), sem("x_split"), sem("w_high"), sem("w_split")
        multiplied, p_high = sem("multiplied"), sem("p_high")
        hid, acted_ready, gate_read, prod_ready = sem("hid"), sem("acted"), sem("gate"), sem("prod")
        spread, mixed, drained = sem("spread"), sem("mixed"), sem("drained")
        per_pass = n_exp * upe + (upe if shared else 0)
        spread_per_pass = n_exp * acc_tiles
        per_pass_exp = n_exp + (1 if shared else 0)
        block = ctx.enter_context(nc.Block())

        def slot_of(p, s):
            return (s + p * per_pass_exp) % 2

        def loads(p, s, j):
            slot = slot_of(p, s)
            before = sum(16 * n_mat * (n_exp // 2) + (32 if shared and slot_of(i, 0) == slot else 0) for i in range(p))
            if j is None:
                return before + 16 * n_mat * (n_exp // 2) + 32
            return before + 16 * n_mat * (j + 1)

        @block.sync
        def _(sp):
            if biased:
                sp.dma_start(b1[:, :], t.dram[name + "_b1"].rearrange("p e c -> p (e c)")).then_inc(loaded, 16)
                sp.dma_start(b2[:, :], t.dram[name + "_b2"]).then_inc(loaded, 16)

            def load(order, slot, sources):
                wait(sp, w_split, order - 1)
                for i, source in enumerate(sources):
                    sp.dma_start(w_raw[:, slot, i, :], source).then_inc(w_in[slot], 16)

            for p in range(passes):
                def pair(j):
                    for s in range(2):
                        e = bass.ds(2 * j + s, 1)
                        sources = [t.dram[name + "_w1"][e, :, :].rearrange("a p n -> p (a n)"),
                                   t.dram[name + "_w2"][e, :, :, :].rearrange("a p c n -> p (a c n)")]
                        if gated:
                            sources.append(t.dram[name + "_w3"][e, :, :].rearrange("a p n -> p (a n)"))
                        load(per_pass_exp * p + 2 * j + s, slot_of(p, s), sources)
                turns(sp, n_exp // 2, pair)
                if shared:
                    load(per_pass_exp * p + n_exp, slot_of(p, 0), [t.dram[name + "_sw1"],
                                                       t.dram[name + "_sw2"].rearrange("p c n -> p (c n)")])


        def units():
            return [(c, k) for c in range(acc_tiles) for k in range(nch)]

        @block.tensor
        def _(pe):
            pe.wait_ge(cast, 3 if biased else 2)

            def product(to, slot, i, k, hi, lo, start, stop):
                cut = slice(128 * k, 128 * k + 128)
                pe.matmul(to, w_hi[:, slot, i, cut], hi, start=start, stop=False, skip_group_check=True)
                pe.matmul(to, w_hi[:, slot, i, cut], lo, start=False, stop=False, skip_group_check=True)
                return pe.matmul(to, w_lo[:, slot, i, cut], hi, start=False, stop=stop, skip_group_check=True)

            def mix(n, u, slot, first):
                c, k = units()[u % upe]
                pe.wait_ge(prod_ready, n + 1)
                product(ps_acc[:, c, :], slot, 1, k, p_hi[:, u % 4, :], p_lo[:, u % 4, :],
                        first and k == 0 and not biased, False).then_inc(mixed, 1)

            def open_sums(p):
                wait(pe, drained, acc_tiles * p)
                if biased:
                    for c in range(acc_tiles):
                        tile = acc_tiles * p + c
                        pe.matmul(ps_acc[:, c, :], b2s[:, :], weights[0:n_exp, S * tile:S * tile + S],
                                  start=True, stop=False, skip_group_check=True)

            def expert(p, n0, e, slot, spreads, order, late, is_shared=False, before=None):
                pe.wait_ge(w_split, order + 1)
                for u, (c, k) in enumerate(units()):
                    tile = acc_tiles * p + c
                    if k == 0 and not is_shared:
                        m = spreads + c
                        if not (isinstance(m, int) and m < 2):
                            pe.wait_ge(multiplied, before(c - 2))
                        oh = onehot[:, bass.ds(e, 1)].to_broadcast([128, 128])
                        pe.matmul(ps_b[:, c % 2, :], oh, parts[:, S * tile:S * tile + S], start=True, stop=True)\
                          .then_inc(spread, 1)
                    n = n0 + u
                    if not (isinstance(n, int) and n < 2):
                        pe.wait_ge(acted_ready, n - 1)
                        if gated and not is_shared:
                            pe.wait_ge(gate_read, n - (upe * p if shared else 0) - 1)
                    if isinstance(e, int) and e == 0 and not is_shared and k == 0:
                        pe.wait_ge(x_split, tile + 1)
                    hi, lo = x_hi[:, S * tile:S * tile + S], x_lo[:, S * tile:S * tile + S]
                    last = product(ps_h[:, u % 2, :], slot, 0, k, hi, lo, True, True)
                    if gated and not is_shared:
                        last = product(ps_g[:, u % 2, :], slot, 2, k, hi, lo, True, True)
                    last.then_inc(hid, 1)
                    if u < LAG:
                        if late is not None:
                            mix(n - LAG, upe - LAG + u, late[0], late[1])
                    else:
                        if late is None and u == LAG:
                            open_sums(p)
                        mix(n - LAG, u - LAG, slot, isinstance(e, int) and e == 0 and not is_shared)

            for p in range(passes):
                def pair(j):
                    for s in range(2):
                        n0 = per_pass * p + upp * j + upe * s
                        first = isinstance(j, int) and j == 0
                        if first and s == 0:
                            late = None
                        else:
                            late = (slot_of(p, 1 - s), first and s == 1)
                        m = spread_per_pass * p + acc_tiles * (2 * j + s)

                        def before(c, n0=n0, first=first, s=s):
                            if c < 0 and first and s == 0 and shared:
                                return n0 - upe + nch * (c + 1)
                            return n0 + nch * (c + 1)
                        expert(p, n0, 2 * j + s, slot_of(p, s), m, per_pass_exp * p + 2 * j + s, late, before=before)
                turns(pe, n_exp // 2, pair)
                n_end = per_pass * p + n_exp * upe
                if shared:
                    expert(p, n_end, 0, slot_of(p, 0), 0, per_pass_exp * p + n_exp, (slot_of(p, 1), False), is_shared=True)
                    n_end += upe
                for i in range(LAG, 0, -1):
                    mix(n_end - i, upe - i, slot_of(p, 0 if shared else 1), False)

        def next_weights(p, j, s):
            last = isinstance(j, int) and j == n_exp // 2 - 1 and s == 1
            if j is None or (last and not shared):
                if p == passes - 1:
                    return None
                return per_pass_exp * (p + 1), slot_of(p + 1, 0), loads(p + 1, 0, 0), n_mat
            if last:
                return per_pass_exp * p + n_exp, slot_of(p, 0), loads(p, 0, None), 2
            j_next, s_next = (j, 1) if s == 0 else (j + 1, 0)
            return per_pass_exp * p + 2 * j_next + s_next, slot_of(p, s_next), loads(p, s_next, j_next), n_mat

        def pairs(eng, pair):
            pair(0)
            if n_exp // 2 > 2:
                with eng.Fori(1, n_exp // 2 - 1) as j:
                    pair(j)
            pair(n_exp // 2 - 1)

        @block.scalar
        def _(act):
            if biased:
                act.wait_ge(loaded, 32)

            def split_w(order, slot, in_loads, mats):
                act.wait_ge(w_in[slot], in_loads)
                act.activation(w_hi[:, slot, 0:mats, :], w_raw[:, slot, 0:mats, :], ACT.Copy, scale=W_SCALE)\
                   .then_inc(w_high, 1)

            def high(n, u):
                act.wait_ge(multiplied, n + 1)
                if not (isinstance(n, int) and n < 4):
                    act.wait_ge(mixed, n - 3)
                act.activation(p_hi[:, u % 4, :], prod[:, u % 2, :], ACT.Copy).then_inc(p_high, 1)

            def expert(n0, e, f, next_w, first):
                for u, (c, k) in enumerate(units()):
                    n = n0 + u
                    act.wait_ge(hid, n + 1)
                    if not (isinstance(n, int) and n < 4):
                        act.wait_ge(multiplied, n - 3)
                    if biased:
                        act.sem_inc(idle, 1)
                    kw = {"bias": b1[:, bass.ds(e * nch + k, 1)]} if biased else {}
                    act.activation(acted[:, u % 4, :], ps_h[:, u % 2, :], f, scale=1.0 / W_SCALE, **kw)\
                       .then_inc(acted_ready, 1)
                    if not (first and u == 0):
                        high(n - 1, u - 1)
                    if u == upe // 2 and next_w is not None:
                        wait(act, mixed, n0)
                        split_w(*next_w)
            for i in range(NB):
                act.activation(x_hi[:, S * i:S * i + S], xn[:, S * i:S * i + S], ACT.Copy).then_inc(x_high, 1)
                if i == acc_tiles - 1:
                    split_w(0, 0, 16 * n_mat, n_mat)
            for p in range(passes):
                def pair(j):
                    for s in range(2):
                        expert(per_pass * p + upp * j + upe * s, 2 * j + s, func, next_weights(p, j, s),
                               isinstance(j, int) and j == 0 and s == 0)
                pairs(act, pair)
                if shared:
                    expert(per_pass * p + n_exp * upe, 0, ACT.Gelu, next_weights(p, None, 0), False)
                high(per_pass * (p + 1) - 1, upe - 1)

        @block.vector
        def _(dve):
            for r in (0, 64):
                dve.tensor_scalar(onehot[r:r + 64, :], t.ident[r:r + 64, r:r + 64],
                                  prod_scale / SCALE / (W_SCALE if gated else 1.0), None, ALU.mult).then_inc(cast, 1)
            if biased:
                dve.wait_ge(loaded, 32)
                dve.tensor_scalar(b2s[:, :], b2[:, :], acc_scale, None, ALU.mult).then_inc(cast, 1)

            def split_w(order, slot, in_loads, mats):
                dve.wait_ge(w_high, order + 1)
                dve.scalar_tensor_tensor(w_lo[:, slot, 0:mats, :], w_raw[:, slot, 0:mats, :], W_SCALE,
                                         w_hi[:, slot, 0:mats, :], ALU.mult, ALU.subtract).then_inc(w_split, 1)

            def low(n, u):
                dve.wait_ge(p_high, n + 1)
                if not (isinstance(n, int) and n < 4):
                    dve.wait_ge(mixed, n - 3)
                dve.tensor_tensor(p_lo[:, u % 4, :], prod[:, u % 2, :], p_hi[:, u % 4, :], ALU.subtract)\
                   .then_inc(prod_ready, 1)

            def expert(n0, m0, g0, next_w, first=False, is_shared=False):
                for u, (c, k) in enumerate(units()):
                    n = n0 + u
                    dve.wait_ge(acted_ready, n + 1)
                    src = acted[:, u % 4, :]
                    if gated and not is_shared:
                        dve.wait_ge(hid, n + 1)
                        if not (isinstance(n, int) and n < 2):
                            dve.wait_ge(multiplied, n - 1)
                        dve.tensor_tensor(gate[:, u % 2, :], acted[:, u % 4, :], ps_g[:, u % 2, :], ALU.mult)\
                           .then_inc(gate_read, 1)
                        dve.wait_ge(gate_read, g0 + u + 1)
                        src = gate[:, u % 2, :]
                    if not (isinstance(n, int) and n < 2):
                        dve.wait_ge(prod_ready, n - 1)
                    if is_shared:
                        dve.tensor_scalar(prod[:, u % 2, :], src, prod_scale, None, ALU.mult).then_inc(multiplied, 1)
                    else:
                        if k == 0:
                            dve.wait_ge(spread, m0 + c + 1)
                        dve.tensor_tensor(prod[:, u % 2, :], src, ps_b[:, c % 2, :], ALU.mult).then_inc(multiplied, 1)
                    if not (first and u == 0):
                        low(n - 1, u - 1)
                    if u == upe // 2 and next_w is not None:
                        split_w(*next_w)
            for i in range(NB):
                dve.wait_ge(x_high, i + 1)
                dve.tensor_tensor(x_lo[:, S * i:S * i + S], xn[:, S * i:S * i + S], x_hi[:, S * i:S * i + S], ALU.subtract)\
                   .then_inc(x_split, 1)
                if i == acc_tiles - 1:
                    split_w(0, 0, 16 * n_mat, n_mat)
            for p in range(passes):
                def pair(j):
                    for s in range(2):
                        expert(per_pass * p + upp * j + upe * s, spread_per_pass * p + acc_tiles * (2 * j + s),
                               n_exp * upe * p + upp * j + upe * s, next_weights(p, j, s),
                               isinstance(j, int) and j == 0 and s == 0)
                pairs(dve, pair)
                if shared:
                    expert(per_pass * p + n_exp * upe, 0, 0, next_weights(p, None, 0), is_shared=True)
                low(per_pass * (p + 1) - 1, upe - 1)
                dve.wait_ge(mixed, per_pass * (p + 1))
                for c in range(acc_tiles):
                    tile = acc_tiles * p + c
                    hb = h[:, S * tile:S * tile + S]
                    dve.scalar_tensor_tensor(hb, ps_acc[:, c, :], 1.0 / acc_scale, hb, ALU.mult, ALU.add)\
                       .then_inc(drained, 1)


def l1_experts(t):
    experts(t, "l1f", 64, 256, ACT.Gelu, -22, 4, 256.0, biased=True)


def l2_experts(t):
    experts(t, "l2f", 8, 512, ACT.Silu, 1, 2, 16.0, gated=True, shared=True)


def l3_experts(t):
    experts(t, "l3f", 8, 512, ACT.Relu, 2, 4, 16.0, biased=True)


TOP = 16
RECTS = ((0, 1, 16), (1, 1, 8), (2, 2, 5), (4, 4, 3), (8, 8, 1))
CAND = sum(ra * rb for _, ra, rb in RECTS)
HEADS, KEYS = 8, 64
CCH = 4
CP = HEADS * CAND // CCH
MAJ, MIN = 16, 8


def product_key_ffn(t):
    nc, h, xn = t.nc, t.h, t.xn
    NG = 128 // 8
    with ExitStack() as ctx:
        sb = lambda n, shape, dt=F32: t.sb(ctx, "l0f_" + n, shape, dt)
        sem = lambda n: t.sem("l0f_" + n)
        w = sb("w", [128, t.where["l0f"]["_width"]])
        at = lambda n: t.at(w, "l0f", n)
        wq = sb("wq", [128, 4, 128])
        bq = sb("bq", [128, 4])
        keys, keys_sq, keys_norm = sb("keys", [128, 256]), sb("keys_sq", [128, 256]), sb("keys_norm", [128, 256])
        cen, sq, std, y1, y, sq2 = (sb(n, [128, 4, 128]) for n in ("cen", "sq", "std", "y1", "y", "sq2"))
        std_t, norm_t, rnorm_t = sb("std_t", [128, 8]), sb("norm_t", [128, 8, 2]), sb("rnorm_t", [128, 16])
        s, rep = sb("s", [128, 16, KEYS]), sb("rep", [128, 16, KEYS])
        v, vi = sb("v", [128, HEADS, 2, TOP]), sb("vi", [128, HEADS, 2, TOP], U32)
        cand, c2, c3 = (sb(n, [128, HEADS, CAND]) for n in ("cand", "c2", "c3"))
        ci, cm = sb("ci", [128, HEADS, CAND], U32), sb("cm", [128, 2, HEADS, CAND], U32)
        majmin = sb("majmin", [128, 2, HEADS * CAND], BF16)
        m1, m2 = sb("m1", [128, HEADS, 8]), sb("m2", [128, HEADS, 8])
        shifted, ex, wt = (sb(n, [128, HEADS, CAND]) for n in ("shifted", "ex", "wt"))
        zsum, rz = sb("zsum", [128, HEADS]), sb("rz", [128, HEADS])
        mm_t = sb("mm_t", [CP, 2, CCH, 128], F16)
        p1, p2 = (sb(n, [CP, CCH, 128], F16) for n in ("p1", "p2"))
        r1 = sb("r1", [CP, CCH, 128])
        hot_maj = sb("hot_maj", [CP, CCH * NG, MAJ, 8], F16)
        hot_min = sb("hot_min", [CP, CCH, MIN, 128], F16)
        hw = [sb(f"hw{p}", [CP, CCH, MIN, 128], F16) for p in range(2)]
        diag = sb("diag", [128, NG, MIN, 8])
        g, z = sb("g", [128, 128]), sb("z", [128, 128])
        ps_q = t.ps(ctx, "l0f_psq", [128, 4, 128])
        ps_s = t.ps(ctx, "l0f_pss", [128, 16, KEYS])
        ps_m = t.ps(ctx, "l0f_psm", [128, 4, 128])
        ps_w = t.ps(ctx, "l0f_psw", [CP, CCH, 128])
        ps_i = t.ps(ctx, "l0f_psi", [CP, 2, CCH, 128], BF16)
        ps_d = t.ps(ctx, "l0f_psd", [128, NG, MIN, 8])
        identb = sb("identb", [128, 128], BF16)
        names = ("loaded consts setup_mm ch_set q_mm cen sq var_mm std y1 y sq2 score_mm norm_act guarded rnorm s_ready "
                 "vi_ready ci_ready cm_ready majmin shifted ex wt w_turned p1 r1 p2 mm_t hot_min hw0 group_mm "
                 "diag a_mm g_mm g_act z out_mm h_ready idle ch_top hots k_sq k_std").split()
        q = {n: sem(n) for n in names}
        block = ctx.enter_context(nc.Block())

        def tok(T):
            return bass.ds(T * 128, 128)

        def later(T, k=0):
            return not (isinstance(T, int) and T <= k)

        @block.sync
        def _(sp):
            sp.dma_start(w[:, :], t.dram["l0f"]).then_inc(q["loaded"], 16)
            sp.wait_ge(q["loaded"], 16)

        @block.gpsimd
        def _(pool):
            pool.tensor_copy(identb[:, :], t.ident).then_inc(q["consts"], 1)

            def front(T):
                pool.wait_ge(q["vi_ready"], T + 1)
                if later(T):
                    pool.wait_ge(q["cm_ready"], T)
                off = 0
                for a0, ra, rb in RECTS:
                    last = pool.tensor_tensor(
                        ci[:, :, off:off + ra * rb].rearrange("p h (a b) -> p h a b", b=rb),
                        vi[:, :, 0, a0:a0 + ra].rearrange("p h (a o) -> p h a o", o=1).to_broadcast([128, HEADS, ra, rb]),
                        vi[:, :, 1, 0:rb].rearrange("p h (o b) -> p h o b", o=1).to_broadcast([128, HEADS, ra, rb]), ALU.add)
                    off += ra * rb
                last.then_inc(q["ci_ready"], 1)

            def back(T):
                pool.wait_ge(q["p2"], T + 1)
                pool.wait_ge(q["hot_min"], T + 1)
                if later(T):
                    pool.wait_ge(q["group_mm"], T)
                for m in range(MIN):
                    last = pool.tensor_tensor(hw[1][:, :, m, :], hot_min[:, :, m, :], p2[:, :, :], ALU.mult)
                last.then_inc(q["hw0"], 1)
            front(0)
            back(0)
            front(1)
            with pool.Fori(2, NTT) as T:
                back(T - 1)
                front(T)
            back(NTT - 1)

        @block.tensor
        def _(pe):
            pe.wait_ge(q["loaded"], 16)
            for c in range(4):
                pe.matmul(ps_q[:, c, :], at("wq")[:, 128 * c:128 * c + 128], at("head_centre"), start=True, stop=True)
            pe.matmul(ps_m[:, 0, 0:4], at("head_centre"), at("bq"), start=True, stop=True).then_inc(q["setup_mm"], 1)
            pe.wait_ge(q["k_sq"], 1)
            pe.matmul(ps_s[:, 0:4, :], at("ones"), keys_sq[:, :], start=True, stop=True).then_inc(q["setup_mm"], 1)
            pe.wait_ge(q["ch_set"], 6)
            pe.wait_ge(q["consts"], 1)

            def project(T):
                if later(T):
                    pe.wait_ge(q["norm_act"], 2 * T)
                for c in range(4):
                    last = pe.matmul(ps_q[:, c, :], wq[:, c, :], xn[:, tok(T)], start=True, stop=True)
                last.then_inc(q["q_mm"], 1)

            def variance(T):
                pe.wait_ge(q["sq"], T + 1)
                pe.matmul(ps_q[:, :, :], at("head_mean"), sq[:, :, :], start=True, stop=True).then_inc(q["var_mm"], 1)

            def scores(T):
                pe.wait_ge(q["sq2"], T + 1)
                if later(T):
                    pe.wait_ge(q["s_ready"], T)
                for c in range(4):
                    pe.matmul(ps_q[:, 0, 16 + 2 * c:18 + 2 * c], sq[:, c, :], at("head_mean")[:, 0:128:64],
                              start=True, stop=True)
                    pe.matmul(ps_q[:, 0, 4 * c:4 * c + 4], sq2[:, c, :], at("quarter")[:, 0:128:32], start=True, stop=True)
                for c in range(4):
                    last = pe.matmul(ps_s[:, 4 * c:4 * c + 4, :], y[:, c, :], keys[:, :], start=True, stop=True)
                last.then_inc(q["score_mm"], 1)

            def turn(T):
                pe.wait_ge(q["wt"], T + 1)
                if later(T):
                    pe.wait_ge(q["r1"], T)
                    pe.wait_ge(q["mm_t"], T)
                wf = wt[:, :, :].rearrange("p h c -> p (h c)")
                for c in range(CCH):
                    pe.transpose(ps_w[:, c, :], wf[:, CP * c:CP * c + CP], t.ident)
                pe.wait_ge(q["majmin"], 2 * T + 2)
                for k in range(2):
                    for c in range(CCH):
                        last = pe.transpose(ps_i[:, k, c, :], majmin[:, k, CP * c:CP * c + CP], identb[:, :])
                last.then_inc(q["w_turned"], 1)

            def groups(T):
                pe.wait_ge(q["hots"], T + 1)
                pe.wait_ge(q["hw0"], T + 1)
                if later(T):
                    pe.wait_ge(q["diag"], T)
                for k in range(NG):
                    n = 0
                    for c in range(CCH):
                        for p in range(2):
                            last = pe.matmul(ps_d[:, k, :, :], hot_maj[:, NG * c + k, :, :].rearrange("p m t -> p (m t)"),
                                             hw[p][:, c, :, 8 * k:8 * k + 8], start=(n == 0), stop=(n == 2 * CCH - 1))
                            n += 1
                last.then_inc(q["group_mm"], 1)
                if later(T):
                    pe.wait_ge(q["h_ready"], T)
                pe.matmul(ps_m[:, 2, :], at("down"), xn[:, tok(T)], start=True, stop=True).then_inc(q["g_mm"], 1)

            def place(T):
                pe.wait_ge(q["diag"], T + 1)
                pe.wait_ge(q["g_act"], T + 1)
                for m in range(MIN):
                    last = pe.matmul(ps_m[:, 1, :], at("place")[:, 128 * m:128 * m + 128], diag[:, :, m, :],
                                     start=(m == 0), stop=(m == MIN - 1))
                last.then_inc(q["a_mm"], 1)

            def output(T):
                pe.wait_ge(q["z"], T + 1)
                pe.matmul(ps_m[:, 3, :], at("up"), z[:, :], start=True, stop=True).then_inc(q["out_mm"], 1)

            def tile(T):
                if later(T):
                    turn(T - 1)
                if later(T, 1):
                    output(T - 2)
                if not isinstance(T, int) or T + 1 < NTT:
                    variance(T + 1)
                if not isinstance(T, int) or T + 1 < NTT:
                    scores(T + 1)
                if later(T):
                    groups(T - 1)
                if not isinstance(T, int) or T + 2 < NTT:
                    project(T + 2)
                if later(T):
                    place(T - 1)
            project(0)
            variance(0)
            scores(0)
            project(1)
            tile(0)
            tile(1)
            tile(2)
            with pe.Fori(3, NTT - 2) as T:
                tile(T)
            tile(NTT - 2)
            tile(NTT - 1)
            turn(NTT - 1)
            output(NTT - 2)
            groups(NTT - 1)
            place(NTT - 1)
            output(NTT - 1)

        @block.scalar
        def _(act):
            act.wait_ge(q["loaded"], 16)
            act.activation(keys_sq[:, :], at("keys"), ACT.Square).then_inc(q["k_sq"], 1)
            act.wait_ge(q["setup_mm"], 2)
            act.activation(keys_norm[:, :], ps_s[:, 0:4, :].rearrange("p a b -> p (a b)"), ACT.Sqrt).then_inc(q["k_std"], 1)

            def squares(T):
                act.wait_ge(q["q_mm"], T + 1)
                if later(T):
                    act.wait_ge(q["y1"], T)
                for c in range(4):
                    last = act.activation(cen[:, c, :], ps_q[:, c, :], ACT.Identity, bias=bq[:, c:c + 1])
                last.then_inc(q["cen"], 1)
                act.wait_ge(q["cen"], T + 1)
                if later(T):
                    act.wait_ge(q["score_mm"], T)
                act.activation(sq[:, :, :], cen[:, :, :], ACT.Square).then_inc(q["sq"], 1)
                if later(T):
                    act.wait_ge(q["y"], T)
                act.activation(y1[:, :, :], cen[:, :, :], ACT.Copy, scale=at("ln_g")).then_inc(q["y1"], 1)

            def root(T):
                act.wait_ge(q["var_mm"], T + 1)
                act.activation(std[:, :, :], ps_q[:, :, :], ACT.Sqrt, bias=t.eps[:, 0:1]).then_inc(q["std"], 1)

            def norms(T):
                act.wait_ge(q["y"], T + 1)
                act.activation(sq2[:, :, :], y[:, :, :], ACT.Square).then_inc(q["sq2"], 1)
                act.wait_ge(q["score_mm"], T + 1)
                if later(T):
                    act.wait_ge(q["rnorm"], T)
                act.activation(norm_t[:, :, :].rearrange("p h k -> p (h k)"), ps_q[:, 0, 0:16], ACT.Sqrt)\
                   .then_inc(q["norm_act"], 1)
                act.activation(std_t[:, :], ps_q[:, 0, 16:24], ACT.Sqrt, bias=t.eps[:, 0:1]).then_inc(q["norm_act"], 1)

            def scale(T):
                act.wait_ge(q["rnorm"], T + 1)
                if later(T):
                    act.wait_ge(q["vi_ready"], T)
                for r in range(16):
                    last = act.activation(s[:, r, :], ps_s[:, r, :], ACT.Copy, scale=rnorm_t[:, r:r + 1])
                last.then_inc(q["s_ready"], 1)

            def chosen(T):
                act.wait_ge(q["shifted"], T + 1)
                if later(T):
                    act.wait_ge(q["wt"], T)
                act.activation(ex[:, :, :], shifted[:, :, :], ACT.Exp).then_inc(q["ex"], 1)
                act.wait_ge(q["cm_ready"], T + 1)
                if later(T):
                    act.wait_ge(q["w_turned"], T)
                for k in range(2):
                    act.activation(majmin[:, k, :], cm[:, k, :, :].rearrange("p h c -> p (h c)"), ACT.Copy)\
                       .then_inc(q["majmin"], 1)

            def first_part(T):
                act.wait_ge(q["w_turned"], T + 1)
                if later(T):
                    act.wait_ge(q["hots"], T)
                act.activation(p1[:, :, :], ps_w[:, :, :], ACT.Copy).then_inc(q["p1"], 1)
                act.activation(mm_t[:, :, :, :], ps_i[:, :, :, :], ACT.Copy).then_inc(q["mm_t"], 1)

            def second_part(T):
                act.wait_ge(q["r1"], T + 1)
                if later(T):
                    act.wait_ge(q["hw0"], T)
                act.activation(p2[:, :, :], r1[:, :, :], ACT.Copy).then_inc(q["p2"], 1)

            def inner(T):
                act.wait_ge(q["g_mm"], T + 1)
                if later(T):
                    act.wait_ge(q["z"], T)
                act.activation(g[:, :], ps_m[:, 2, :], ACT.Gelu).then_inc(q["g_act"], 1)

            def tile(T):
                ahead = not isinstance(T, int) or T + 1 < NTT
                if ahead:
                    squares(T + 1)
                if later(T):
                    first_part(T - 1)
                if ahead:
                    root(T + 1)
                if later(T):
                    second_part(T - 1)
                if ahead:
                    norms(T + 1)
                if later(T):
                    inner(T - 1)
                chosen(T)
                if ahead:
                    scale(T + 1)
            act.wait_ge(q["ch_set"], 2)
            squares(0)
            root(0)
            norms(0)
            scale(0)
            tile(0)
            tile(1)
            with act.Fori(2, NTT - 1) as T:
                tile(T)
            tile(NTT - 1)
            first_part(NTT - 1)
            second_part(NTT - 1)
            inner(NTT - 1)

        @block.vector
        def _(dve):
            dve.wait_ge(q["loaded"], 16)
            dve.wait_ge(q["setup_mm"], 2)
            k = [0]

            def once(ins):
                k[0] += 1
                ins.then_inc(q["ch_set"], 1)
                dve.wait_ge(q["ch_set"], k[0])
            once(dve.tensor_copy(wq[:, :, :], ps_q[:, :, :]))
            once(dve.tensor_copy(bq[:, :], ps_m[:, 0, 0:4]))
            dve.wait_ge(q["k_std"], 1)
            once(dve.tensor_scalar(keys_norm[:, :], keys_norm[:, :], 1e-12, None, ALU.max))
            once(dve.reciprocal(keys_sq[:, :], keys_norm[:, :]))
            once(dve.tensor_tensor(keys[:, :], at("keys"), keys_sq[:, :], ALU.mult))
            once(dve.tensor_copy(z[:, 0:8], wq[:, 0, 0:8]))
            dve.wait_ge(q["consts"], 1)
            top = Chain(dve, q["ch_top"], q["idle"])

            def scaled(T):
                dve.wait_ge(q["std"], T + 1)
                dve.wait_ge(q["y1"], T + 1)
                if later(T):
                    dve.wait_ge(q["score_mm"], T)
                dve.scalar_tensor_tensor(y[:, :, :], std[:, :, :], at("ln_b"), y1[:, :, :], ALU.mult, ALU.add)\
                   .then_inc(q["y"], 1)

            def norms(T):
                dve.wait_ge(q["norm_act"], 2 * T + 2)
                dve.scalar_tensor_tensor(norm_t[:, :, :],
                                         std_t[:, :].rearrange("p (h o) -> p h o", o=1).to_broadcast([128, 8, 2]),
                                         1e-12, norm_t[:, :, :], ALU.mult, ALU.max).then_inc(q["guarded"], 1)
                dve.wait_ge(q["guarded"], T + 1)
                if later(T):
                    dve.wait_ge(q["s_ready"], T)
                dve.reciprocal(rnorm_t[:, :], norm_t[:, :, :].rearrange("p h k -> p (h k)")).then_inc(q["rnorm"], 1)

            def middle(T, with_front=True, backs=True):
                top.start(T)
                then, alone = top.then, top.then_alone
                dve.wait_ge(q["s_ready"], T + 1)
                dve.sem_inc(q["idle"], 1)
                halves = [(r // 2, r % 2, r) for r in range(16)]
                for hd, k, r in halves:
                    last = dve.max(v[:, hd, k, 0:8], s[:, r, :])
                alone(last)
                for hd, k, r in halves:
                    last = dve.match_replace(rep[:, r, :], v[:, hd, k, 0:8], s[:, r, :], -BIG)
                alone(last)
                if later(T, 1):
                    weigh(T - 2)
                if backs:
                    one_hots(T - 1)
                if later(T, 1):
                    add(T - 2)
                if with_front:
                    scaled(T + 1)
                for hd, k, r in halves:
                    last = dve.max(v[:, hd, k, 8:16], rep[:, r, :])
                alone(last)
                if later(T):
                    dve.wait_ge(q["ci_ready"], T)
                    dve.sem_inc(q["idle"], 1)
                for hd, k, r in halves:
                    dve.max_index(vi[:, hd, k, 0:8], v[:, hd, k, 0:8], s[:, r, :])
                    last = dve.max_index(vi[:, hd, k, 8:16], v[:, hd, k, 8:16], rep[:, r, :])
                last.then_inc(q["vi_ready"], 1)
                off = 0
                for a0, ra, rb in RECTS:
                    last = dve.tensor_tensor(
                        cand[:, :, off:off + ra * rb].rearrange("p h (a b) -> p h a b", b=rb),
                        v[:, :, 0, a0:a0 + ra].rearrange("p h (a o) -> p h a o", o=1).to_broadcast([128, HEADS, ra, rb]),
                        v[:, :, 1, 0:rb].rearrange("p h (o b) -> p h o b", o=1).to_broadcast([128, HEADS, ra, rb]), ALU.add)
                    off += ra * rb
                alone(last)
                for hd in range(HEADS):
                    last = dve.max(m1[:, hd, :], cand[:, hd, :])
                alone(last)
                for hd in range(HEADS):
                    last = dve.match_replace(c2[:, hd, :], m1[:, hd, :], cand[:, hd, :], -BIG)
                alone(last)
                for hd in range(HEADS):
                    last = dve.max(m2[:, hd, :], c2[:, hd, :])
                alone(last)
                for hd in range(HEADS):
                    last = dve.match_replace(c3[:, hd, :], m2[:, hd, :], c2[:, hd, :], -BIG)
                then(last)
                then(dve.tensor_tensor(shifted[:, :, :], cand[:, :, :],
                                       m1[:, :, 0:1].to_broadcast([128, HEADS, CAND]), ALU.subtract))
                dve.sem_inc(q["shifted"], 1)
                dve.wait_ge(q["ci_ready"], T + 1)
                if later(T):
                    dve.wait_ge(q["majmin"], 2 * T)
                dve.tensor_scalar(cm[:, 0, :, :], ci[:, :, :], 3, None, ALU.logical_shift_right)
                dve.tensor_scalar(cm[:, 1, :, :], ci[:, :, :], 7, None, ALU.bitwise_and).then_inc(q["cm_ready"], 1)
                if with_front:
                    norms(T + 1)
                dve.wait_ge(q["ex"], T + 1)
                then(dve.scalar_tensor_tensor(c2[:, :, :], c3[:, :, :], -0.5 * BIG, ex[:, :, :], ALU.is_lt, ALU.mult))
                then(dve.tensor_reduce(zsum[:, :], c2[:, :, :], AX.X, ALU.add))
                then(dve.reciprocal(rz[:, :], zsum[:, :]))
                if later(T):
                    dve.wait_ge(q["w_turned"], T)
                dve.scalar_tensor_tensor(wt[:, :, :], c2[:, :, :], SCALE,
                                         rz[:, :].rearrange("p (h o) -> p h o", o=1).to_broadcast([128, HEADS, CAND]),
                                         ALU.mult, ALU.mult)\
                   .then_inc(q["wt"], 1)
                if backs:
                    diagonals(T - 1)

            def one_hots(T):
                dve.wait_ge(q["p1"], T + 1)
                if later(T):
                    dve.wait_ge(q["p2"], T)
                dve.tensor_tensor(r1[:, :, :], ps_w[:, :, :], p1[:, :, :], ALU.subtract).then_inc(q["r1"], 1)
                dve.wait_ge(q["mm_t"], T + 1)
                if later(T):
                    dve.wait_ge(q["group_mm"], T)
                    dve.wait_ge(q["hw0"], T)

                for m in range(MIN):
                    last = dve.tensor_scalar(hot_min[:, :, m, :], mm_t[:, 1, :, :], float(m), None, ALU.is_equal)
                last.then_inc(q["hot_min"], 1)
                for m in range(MAJ):
                    dve.tensor_scalar(hot_maj[:, :, m, :], mm_t[:, 0, :, :].rearrange("p c (g t) -> p (c g) t", t=8),
                                      float(m), None, ALU.is_equal)
                dve.wait_ge(q["hot_min"], T + 1)
                dve.tensor_tensor(
                    hw[0][:, :, :, :], hot_min[:, :, :, :],
                    p1[:, :, :].rearrange("p c (o t) -> p c o t", o=1).to_broadcast([CP, CCH, MIN, 128]), ALU.mult)\
                   .then_inc(q["hots"], 1)

            def diagonals(T):
                dve.wait_ge(q["group_mm"], T + 1)
                if later(T):
                    dve.wait_ge(q["a_mm"], T)
                dve.tensor_tensor(diag[:, :, :, :].rearrange("p g m t -> p (g m) t"),
                                  ps_d[:, :, :, :].rearrange("p g m t -> p (g m) t"),
                                  at("own").rearrange("p (o t) -> p o t", o=1).to_broadcast([128, NG * MIN, 8]), ALU.mult)\
                   .then_inc(q["diag"], 1)

            def weigh(T):
                dve.wait_ge(q["a_mm"], T + 1)
                dve.wait_ge(q["g_act"], T + 1)
                if later(T):
                    dve.wait_ge(q["out_mm"], T)
                dve.tensor_tensor(z[:, :], g[:, :], ps_m[:, 1, :], ALU.mult).then_inc(q["z"], 1)

            def add(T):
                dve.wait_ge(q["out_mm"], T + 1)
                dve.tensor_tensor(h[:, tok(T)], h[:, tok(T)], ps_m[:, 3, :], ALU.add).then_inc(q["h_ready"], 1)
            scaled(0)
            norms(0)
            middle(0, backs=False)
            middle(1)
            middle(2)
            with dve.Fori(3, NTT - 1) as T:
                middle(T)
            middle(NTT - 1, with_front=False)
            weigh(NTT - 2)
            add(NTT - 2)
            one_hots(NTT - 1)
            diagonals(NTT - 1)
            weigh(NTT - 1)
            add(NTT - 1)


STAGES = ("tok", "l0_attn", "l0_ffn", "l1_attn", "l1_ffn", "l2_attn", "l2_ffn", "l3_attn", "l3_ffn")


def build_tower(nc, dram, where, out, stages=STAGES, h_in=None):
    with ExitStack() as ctx:
        t = Tower(nc, ctx, dram, where)
        load_base(t)
        if h_in is not None:
            loaded = t.sem("h_loaded")
            with nc.Block() as block:
                @block.sync
                def _(sp):
                    sp.dma_start(t.h[:, :], h_in).then_inc(loaded, 16)
                    sp.wait_ge(loaded, 16)
        steps = {"tok": embed, "l0_attn": memory_mixer, "l0_ffn": product_key_ffn,
                 "l1_attn": l1_attention, "l1_ffn": l1_experts, "l2_attn": l2_attention,
                 "l2_ffn": l2_experts, "l3_attn": l3_attention, "l3_ffn": l3_experts}
        for name in stages:
            if name != "tok":
                layernorm(t)
            steps[name](t)
            t.end_stage()
        write_out(t, out)


class Pack:

    def __init__(self):
        self.parts, self.where, self.width = [], {}, 0

    def add(self, name, a):
        import numpy as np
        a = np.asarray(a)
        a = a.reshape(a.shape[0], -1)
        assert a.shape[0] == 128, (name, a.shape)
        self.where[name] = (self.width, self.width + a.shape[1])
        self.parts.append(a)
        self.width += a.shape[1]

    def array(self):
        import numpy as np
        self.where["_width"] = self.width
        return np.ascontiguousarray(np.concatenate(self.parts, axis=1))


def heads32(a, fill=None):
    import numpy as np
    out = np.zeros((*a.shape[:-1], 2, 4, 32), a.dtype)
    out[..., :16] = a.reshape(*a.shape[:-1], 2, 4, 16)
    for row, value in (fill or {}).items():
        out[..., row] = value
    return out


def lay_out(x):
    import numpy as np
    f = np.float32
    eye = np.eye(128, dtype=f)
    arrays, where = {}, {}

    base = Pack()
    base.add("ident", eye)
    base.add("mean", np.full((128, 128), 1.0 / D, f))
    base.add("mean_every", np.tile(np.arange(128 + NB - 1) % NB == NB - 1, (128, 1)).astype(f) / f(D))
    base.add("eps", np.full((128, 1), LN_EPS, f))
    arrays["base"] = base.array()
    where["base"] = base.where

    p = Pack()
    p.add("proj", x["L0_tok_proj_w"].reshape(D, 3, D).transpose(2, 1, 0))
    p.add("proj_b", x["L0_tok_proj_b"].reshape(D, 1))
    arrays["tok"], where["tok"] = p.array(), p.where
    arrays["x"] = np.ascontiguousarray(x["x"])
    for n in (2, 3, 4):
        arrays[f"emb{n}"] = np.ascontiguousarray(x[f"L0_tok_emb_{n}"])

    p = Pack()
    p.add("q1", x["L0_attn_w_q1"].T)
    p.add("q2", x["L0_attn_w_q2"].T)
    p.add("m1", x["L0_attn_mem_w1"].T)
    p.add("m2", x["L0_attn_mem_w2"].T.reshape(2, 128, 128).transpose(1, 0, 2))
    p.add("out", x["L0_attn_w_out"].T)
    p.add("every", np.tile(np.arange(128 + NB - 1) % NB == NB - 1, (128, 1)).astype(f))
    p.add("conv_w", x["L0_attn_conv_q_w"].reshape(128, 4))
    p.add("conv_b", x["L0_attn_conv_q_b"].reshape(128, 1))
    arrays["l0a"], where["l0a"] = p.array(), p.where

    rows = np.arange(128)
    same = (rows[:, None] // 32) == (rows[None, :] // 32)
    r32 = rows % 32
    den = (same & (r32[:, None] == 16)).astype(f)

    def selections(rows_per_head, stacks, blocks):
        out = []
        for s in range(2):
            for st, (m, *used) in enumerate(stacks):
                for p in used[s]:
                    for hd in range(128 // rows_per_head):
                        a = np.zeros((128, m), f)
                        for i, part in enumerate(blocks[s][st]):
                            if part == p:
                                r = np.arange(rows_per_head)
                                a[rows_per_head * hd + r, rows_per_head * i + r] = 1.0
                        out.append(a)
        return np.concatenate(out, axis=1)

    for n, a in (("sel16", selections(16, STACK16, ((Q16,), (K16,)))), ("sel32", selections(32, STACK32, (Q32, K32)))):
        arrays[n], where[n] = a, {"_width": a.shape[1]}

    def attention_pack(wv, bv, wo, bo, max0):
        p = Pack()
        p.add("v", wv)
        p.add("o", heads32(np.ascontiguousarray(wo.T)).reshape(128, 2, 128).transpose(2, 1, 0))
        p.add("den", den)
        p.add("bv", np.broadcast_to(bv[None, :], (128, 128)))
        p.add("bo", bo.reshape(128, 1))
        minus = np.zeros((128, 4), f)
        for part in range(3):
            for hd in range(4):
                minus[max0 + 4 * part + hd, hd] = -1.0
        p.add("minus", minus)
        return p

    p = attention_pack(x["L1_attn_Wv"], x["L1_attn_bv"], x["L1_attn_Wo"], x["L1_attn_bo"], 96)
    p.add("wq", x["L1_attn_Wq"])
    p.add("wk", x["L1_attn_Wv"])
    p.add("bq", x["L1_attn_bq"].reshape(128, 1))
    p.add("bk", x["L1_attn_bv"].reshape(128, 1))
    rot = np.zeros((128, 128), f)
    for r in range(128):
        if r % 16 < 8:
            rot[r + 8, r] = -1.0
        else:
            rot[r - 8, r] = 1.0
    p.add("rot", rot)
    theta = (1.0 / 10000.0 ** (np.arange(0, 16, 2, dtype=f) / f(16))).astype(f)
    angle = (np.arange(S, dtype=f)[:, None] * theta[None, :]).astype(f)
    angle = np.concatenate([angle, angle], axis=1).T
    for n, fn in (("cos", np.cos), ("sin", np.sin)):
        p.add(n, np.tile(fn(angle.astype(np.float64)).astype(f), (8, 1)))
    arrays["l1a"], where["l1a"] = p.array(), p.where

    def with_points(a, ap, fill=None):
        out = np.zeros((*a.shape[:-1], 2, 4, 32), f)
        out[..., :16] = a.reshape(*a.shape[:-1], 2, 4, 16)
        out[..., 16:28] = ap.reshape(*a.shape[:-1], 2, 4, 12)
        for row, value in (fill or {}).items():
            out[..., row] = value
        return out

    p = attention_pack(x["L2_attn_wv"], x["L2_attn_bv"], x["L2_attn_wo"], x["L2_attn_bo"], 64)
    p.add("wq", with_points(x["L2_attn_wq"], x["L2_attn_wqp"]))
    p.add("wk", with_points(x["L2_attn_wk"], x["L2_attn_wkp"]))
    p.add("bq", with_points(x["L2_attn_bq"], x["L2_attn_bqp"], {29: 1.0}).reshape(2, 128).T)
    p.add("bk", with_points(x["L2_attn_bk"], x["L2_attn_bkp"], {28: 1.0}).reshape(2, 128).T)
    p.add("ln_g", x["L2_attn_ln_g"].reshape(128, 1))
    p.add("ln_b", x["L2_attn_ln_b"].reshape(128, 1))
    p.add("ps", np.repeat(x["L2_attn_pscale"], 32).reshape(2, 128).T)
    points = (r32[:, None] >= 16) & (r32[:, None] < 28) & same
    p.add("sum_q", (points & (r32[None, :] == 28)).astype(f))
    p.add("sum_k", (points & (r32[None, :] == 29)).astype(f))
    p.add("two_on_points", np.where((r32 >= 16) & (r32 < 28), 2.0, 0.0).astype(f).reshape(128, 1))
    p.add("rest", np.where(r32 < 16, 0.25, np.where(r32 == 29, 1.0, 0.0)).astype(f).reshape(128, 1))
    arrays["l2a"], where["l2a"] = p.array(), p.where

    p = attention_pack(np.ascontiguousarray(x["L3_attn_Wv"].T), np.zeros(128, f),
                       np.ascontiguousarray(x["L3_attn_Wo"].T), x["L3_attn_bo"], 96)
    p.add("wq", x["L3_attn_Wq"])
    p.add("wk", x["L3_attn_Wk"])
    head = (rows[:, None] // 16) == (rows[None, :] // 16)
    p.add("head_mean", head.astype(f) / f(16))
    p.add("head_centre", eye - head.astype(f) / f(16))
    for n in "qk":
        for what in ("gamma", "beta"):
            p.add(f"{n}_{what}", np.tile(x[f"L3_attn_{n}_{what}"], 8).reshape(128, 1))
    arrays["l3a"], where["l3a"] = p.array(), p.where
    ij = rows[:, None] - rows[None, :]
    arrays["causal"] = np.concatenate([np.where(ij < 0, -BIG, 0.0), np.where(ij > 0, -BIG, 0.0)],
                                      axis=1).astype(f)

    p = Pack()
    p.add("wq", x["L0_ffn_Wq"].reshape(4, 128, 128).transpose(1, 0, 2))
    p.add("bq", x["L0_ffn_bq"].reshape(4, 128).T)
    half = (rows[:, None] // 64) == (rows[None, :] // 64)
    quarter = (rows[:, None] // 32) == (rows[None, :] // 32)
    p.add("head_mean", half.astype(f) / f(64))
    p.add("head_centre", eye - half.astype(f) / f(64))
    p.add("quarter", quarter.astype(f))
    p.add("ln_g", np.tile(x["L0_ffn_ln_g"], 2).reshape(128, 1))
    p.add("ln_b", np.tile(x["L0_ffn_ln_b"], 2).reshape(128, 1))
    keys = np.zeros((2, 2, 32, 4, 64), f)
    for hh in range(2):
        keys[hh, 0, :, 2 * hh, :] = x["L0_ffn_keys0"].T
        keys[hh, 1, :, 2 * hh + 1, :] = x["L0_ffn_keys1"].T
    p.add("keys", keys.reshape(128, 256))
    p.add("down", x["L0_ffn_expert_down"][0:128].T)
    p.add("up", x["L0_ffn_expert_up"][0:128])
    p.add("ones", np.ones((128, 128), f))
    p.add("own", (r32[:, None] % 8 == np.arange(8)[None, :]).astype(f) / f(SCALE))
    p.add("place", np.concatenate([(rows[:, None] // 8 * 8 + m == rows[None, :]).astype(f) for m in range(8)], axis=1))
    arrays["l0f"], where["l0f"] = p.array(), p.where

    def experts(name, w1, w2, b1=None, b2=None, w3=None):
        n_exp, _, hidden = w1.shape
        nch = hidden // 128
        arrays[name + "_w1"] = np.ascontiguousarray(w1)
        arrays[name + "_w2"] = np.ascontiguousarray(w2.reshape(n_exp, nch, 128, D).transpose(0, 2, 1, 3))
        if w3 is not None:
            arrays[name + "_w3"] = np.ascontiguousarray(w3)
        if b1 is not None:
            arrays[name + "_b1"] = np.ascontiguousarray(b1.reshape(n_exp, nch, 128).transpose(2, 0, 1))
            arrays[name + "_b2"] = np.ascontiguousarray(b2)

    experts("l1f", x["L1_ffn_w1"][::-1], x["L1_ffn_w2"][::-1], x["L1_ffn_b1"][::-1], x["L1_ffn_b2"][::-1])
    arrays["l1f_router"] = np.ascontiguousarray(x["L1_ffn_router_w"][:, ::-1])
    arrays["l1f_router_b"] = np.ascontiguousarray(np.broadcast_to(x["L1_ffn_router_b"][::-1][None, :], (128, 64)))
    experts("l2f", x["L2_ffn_w1"].transpose(0, 2, 1), x["L2_ffn_w2"].transpose(0, 2, 1),
            w3=x["L2_ffn_w3"].transpose(0, 2, 1))
    arrays["l2f_router"] = np.ascontiguousarray(x["L2_ffn_gate_w"].T)
    arrays["l2f_sw1"] = np.ascontiguousarray(x["L2_ffn_sw1"].T)
    arrays["l2f_sw2"] = np.ascontiguousarray(x["L2_ffn_sw2"].T.reshape(4, 128, D).transpose(1, 0, 2))
    experts("l3f", x["L3_ffn_w1"], x["L3_ffn_w2"], x["L3_ffn_b1"], x["L3_ffn_b2"])
    arrays["l3f_router"] = np.ascontiguousarray(x["L3_ffn_gate_w"].T)
    return arrays, where


def kernel(**inputs):
    import numpy as np
    import concourse.bacc as bacc
    from concourse.bass_utils import run_bass_kernel_spmd

    x = {k: np.asarray(v) for k, v in inputs.items()}
    arrays, where = lay_out(x)
    nc = bacc.Bacc("TRN2", target_bir_lowering=False, num_devices=1)
    dram = {n: nc.dram_tensor(f"in_{n}", a.shape, mybir.dt.from_np(a.dtype), kind="ExternalInput").ap()
            for n, a in arrays.items()}
    out = nc.dram_tensor("out_0", (NB, S, D), F32, kind="ExternalOutput").ap()
    build_tower(nc, dram, where, out)
    r = run_bass_kernel_spmd(nc, [{f"in_{n}": a for n, a in arrays.items()}], core_ids=[0])
    return r.results[0]["out_0"]
```
